# Optimizing a Trainium2 kernel written in Bass

```python
import numpy as np
import jax
import jax.numpy as jnp

def _softmax(x, axis=-1):
    return jax.nn.softmax(x, axis=axis)

def _gelu(x):
    return jax.nn.gelu(x, approximate=True)

def _silu(x):
    return jax.nn.silu(x)

def _sigmoid(x):
    return jax.nn.sigmoid(x)

def _layernorm(x, axis=-1, eps=1e-05):
    m = jnp.mean(x, axis=axis, keepdims=True)
    v = jnp.var(x, axis=axis, keepdims=True)
    return (x - m) / jnp.sqrt(v + eps)

def _scatter_add(tgt, idx, src, axis=0):
    return tgt.at[idx].add(src)

def _segment_sum(src, seg, n):
    return jax.ops.segment_sum(src, seg, n)
kernel_name = 'mk_gnn_ffn_d1_gnn_r8_cf3b71'

def setup_inputs(seed: int=0):
    np.random.seed(seed)
    _w = jnp.asarray

    def _rec_inputs():
        import jax
        import jax.numpy as jnp
        _gk = jax.random.key(seed)
        x = -0.0002117 + 1 * jax.random.normal(jax.random.fold_in(_gk, 1), (12500, 256), jnp.float32)
        _s = jax.random.randint(jax.random.fold_in(_gk, 2), (100000,), 0, 12500, jnp.int32)
        _d = jax.random.randint(jax.random.fold_in(_gk, 3), (100000,), 0, 12500, jnp.int32)
        _loop = jnp.arange(12500, dtype=jnp.int32)
        src = jnp.concatenate([_s, _d, _loop])
        dst = jnp.concatenate([_d, _s, _loop])
        _o = jnp.argsort(dst, stable=True)
        src = src[_o]
        dst = dst[_o]
        return (x, src, dst)
    x, src, dst = _rec_inputs()

    def _L0_gnn_setup():
        import jax, jax.numpy as jnp
        import numpy as np
        N_NODES = 12500
        N_EDGES = 200000
        IN_CH = 256
        OUT_CH = 256
        BN_EPS = 1e-05

        def gcn_conv(x, W, b, src, dst, n_nodes):
            loop = jnp.arange(n_nodes)
            s = jnp.concatenate([src, loop])
            d = jnp.concatenate([dst, loop])
            ones = jnp.ones(s.shape[0], dtype=x.dtype)
            deg = jax.ops.segment_sum(ones, d, num_segments=n_nodes)
            dinv = jnp.where(deg > 0, jax.lax.rsqrt(deg), 0.0)
            norm = dinv[s] * dinv[d]
            xw = x @ W
            msg = xw[s] * norm[:, None]
            out = jax.ops.segment_sum(msg, d, num_segments=n_nodes)
            return out + b

        def batch_norm(x, gamma, beta):
            mean = jnp.mean(x, axis=0)
            var = jnp.mean(jnp.square(x - mean), axis=0)
            return (x - mean) * jax.lax.rsqrt(var + BN_EPS) * gamma + beta
        key = jax.random.key(seed)
        ks = jax.random.split(key, 8)
        x = jax.random.normal(ks[0], (N_NODES, IN_CH), dtype=jnp.float32)
        edge_index = jax.random.randint(ks[1], (2, N_EDGES), 0, N_NODES, dtype=jnp.int32)
        s1 = 1.0 / np.sqrt(IN_CH)
        s2 = 1.0 / np.sqrt(OUT_CH)
        W1 = jax.random.uniform(ks[2], (IN_CH, OUT_CH), jnp.float32, -s1, s1)
        b1 = jnp.zeros((OUT_CH,), jnp.float32)
        W2 = jax.random.uniform(ks[3], (OUT_CH, OUT_CH), jnp.float32, -s2, s2)
        b2 = jnp.zeros((OUT_CH,), jnp.float32)
        gamma1 = jnp.ones((OUT_CH,), jnp.float32)
        beta1 = jnp.zeros((OUT_CH,), jnp.float32)
        gamma2 = jnp.ones((OUT_CH,), jnp.float32)
        beta2 = jnp.zeros((OUT_CH,), jnp.float32)
        return {'x': x, 'edge_index': edge_index, 'W1': W1, 'b1': b1, 'W2': W2, 'b2': b2, 'gamma1': gamma1, 'beta1': beta1, 'gamma2': gamma2, 'beta2': beta2}
    _L0_gnn_all = _L0_gnn_setup()
    _L0_gnn_in = {k: v for k, v in _L0_gnn_all.items() if k in ('W1', 'b1', 'W2', 'b2', 'gamma1', 'beta1', 'gamma2', 'beta2')}
    del _L0_gnn_all

    def _L0_ffn_setup():
        import jax, jax.numpy as jnp
        import numpy as np
        E, D, H, TOP_K = (6, 256, 256, 2)
        ROUTER_H = D // 2
        key = jax.random.key(seed)
        ks = jax.random.split(key, 12)
        s = 1.0 / np.sqrt(D)
        sh = 1.0 / np.sqrt(H)
        sr = 1.0 / np.sqrt(ROUTER_H)
        return {'features': jax.random.normal(ks[0], (8, 512, D), dtype=jnp.float32), 'router_w1': jax.random.uniform(ks[1], (D, ROUTER_H), jnp.float32, -s, s), 'router_b1': jnp.zeros((ROUTER_H,), jnp.float32), 'router_w2': jax.random.uniform(ks[2], (ROUTER_H, E), jnp.float32, -sr, sr), 'router_b2': jnp.zeros((E,), jnp.float32), 'expert_w1': jax.random.uniform(ks[3], (E, D, H), jnp.float32, -s, s), 'expert_b1': jnp.zeros((E, H), jnp.float32), 'expert_w2': jax.random.uniform(ks[4], (E, H, H), jnp.float32, -sh, sh), 'expert_b2': jnp.zeros((E, H), jnp.float32), 'expert_w3': jax.random.uniform(ks[5], (E, H, D), jnp.float32, -sh, sh), 'expert_b3': jnp.zeros((E, D), jnp.float32)}
    _L0_ffn_all = _L0_ffn_setup()
    _L0_ffn_in = {k: v for k, v in _L0_ffn_all.items() if k in ('router_w1', 'router_b1', 'router_w2', 'router_b2', 'expert_w1', 'expert_b1', 'expert_w2', 'expert_b2', 'expert_w3', 'expert_b3')}
    del _L0_ffn_all
    return {'x': x, 'src': src, 'dst': dst, 'L0_gnn_W1': _L0_gnn_in['W1'], 'L0_gnn_b1': _L0_gnn_in['b1'], 'L0_gnn_W2': _L0_gnn_in['W2'], 'L0_gnn_b2': _L0_gnn_in['b2'], 'L0_gnn_gamma1': _L0_gnn_in['gamma1'], 'L0_gnn_beta1': _L0_gnn_in['beta1'], 'L0_gnn_gamma2': _L0_gnn_in['gamma2'], 'L0_gnn_beta2': _L0_gnn_in['beta2'], 'L0_ffn_router_w1': _L0_ffn_in['router_w1'], 'L0_ffn_router_b1': _L0_ffn_in['router_b1'], 'L0_ffn_router_w2': _L0_ffn_in['router_w2'], 'L0_ffn_router_b2': _L0_ffn_in['router_b2'], 'L0_ffn_expert_w1': _L0_ffn_in['expert_w1'], 'L0_ffn_expert_b1': _L0_ffn_in['expert_b1'], 'L0_ffn_expert_w2': _L0_ffn_in['expert_w2'], 'L0_ffn_expert_b2': _L0_ffn_in['expert_b2'], 'L0_ffn_expert_w3': _L0_ffn_in['expert_w3'], 'L0_ffn_expert_b3': _L0_ffn_in['expert_b3']}

def reference(x, src, dst, L0_gnn_W1, L0_gnn_b1, L0_gnn_W2, L0_gnn_b2, L0_gnn_gamma1, L0_gnn_beta1, L0_gnn_gamma2, L0_gnn_beta2, L0_ffn_router_w1, L0_ffn_router_b1, L0_ffn_router_w2, L0_ffn_router_b2, L0_ffn_expert_w1, L0_ffn_expert_b1, L0_ffn_expert_w2, L0_ffn_expert_b2, L0_ffn_expert_w3, L0_ffn_expert_b3):
    import jax
    import jax.numpy as jnp

    def _L0_gnn_ref(x, edge_index, W1, b1, W2, b2, gamma1, beta1, gamma2, beta2):
        import jax, jax.numpy as jnp
        import numpy as np
        N_NODES = 12500
        N_EDGES = 200000
        IN_CH = 256
        OUT_CH = 256
        BN_EPS = 1e-05

        def gcn_conv(x, W, b, src, dst, n_nodes):
            loop = jnp.arange(n_nodes)
            s = jnp.concatenate([src, loop])
            d = jnp.concatenate([dst, loop])
            ones = jnp.ones(s.shape[0], dtype=x.dtype)
            deg = jax.ops.segment_sum(ones, d, num_segments=n_nodes)
            dinv = jnp.where(deg > 0, jax.lax.rsqrt(deg), 0.0)
            norm = dinv[s] * dinv[d]
            xw = x @ W
            msg = xw[s] * norm[:, None]
            out = jax.ops.segment_sum(msg, d, num_segments=n_nodes)
            return out + b

        def batch_norm(x, gamma, beta):
            mean = jnp.mean(x, axis=0)
            var = jnp.mean(jnp.square(x - mean), axis=0)
            return (x - mean) * jax.lax.rsqrt(var + BN_EPS) * gamma + beta
        src, dst = (edge_index[0], edge_index[1])
        identity = x
        out = gcn_conv(x, W1, b1, src, dst, N_NODES)
        out = jax.nn.relu(batch_norm(out, gamma1, beta1))
        out = gcn_conv(out, W2, b2, src, dst, N_NODES)
        out = batch_norm(out, gamma2, beta2)
        out = jax.nn.relu(out + identity)
        return out

    def _L0_ffn_ref(features, router_w1, router_b1, router_w2, router_b2, expert_w1, expert_b1, expert_w2, expert_b2, expert_w3, expert_b3):
        import jax, jax.numpy as jnp
        import numpy as np
        E, D, H, TOP_K = (6, 256, 256, 2)
        ROUTER_H = D // 2
        rh = jax.nn.relu(features @ router_w1 + router_b1)
        expert_logits = jax.nn.softmax(rh @ router_w2 + router_b2, axis=-1)
        top_w, top_i = jax.lax.top_k(expert_logits, TOP_K)
        routing_weights = jax.nn.softmax(top_w, axis=-1)
        h1 = jax.nn.relu(jnp.einsum('bsd,edh->bseh', features, expert_w1) + expert_b1)
        h2 = jax.nn.relu(jnp.einsum('bseh,ehf->bsef', h1, expert_w2) + expert_b2)
        expert_out = jnp.einsum('bsef,efo->bseo', h2, expert_w3) + expert_b3
        sel = jnp.take_along_axis(expert_out, top_i[:, :, :, None], axis=2)
        combined = jnp.sum(sel * routing_weights[..., None], axis=2)
        return combined
    edge_index = jnp.stack([src, dst])
    x = x + _L0_gnn_ref(_layernorm(x, axis=-1), edge_index, L0_gnn_W1, L0_gnn_b1, L0_gnn_W2, L0_gnn_b2, L0_gnn_gamma1, L0_gnn_beta1, L0_gnn_gamma2, L0_gnn_beta2)
    x = x + _L0_ffn_ref(_layernorm(x, axis=-1)[None], L0_ffn_router_w1, L0_ffn_router_b1, L0_ffn_router_w2, L0_ffn_router_b2, L0_ffn_expert_w1, L0_ffn_expert_b1, L0_ffn_expert_w2, L0_ffn_expert_b2, L0_ffn_expert_w3, L0_ffn_expert_b3)[0]
    return x

_drawn_inputs = setup_inputs


def setup_inputs(seed=0):
    import zlib

    import numpy as np

    out = dict(_drawn_inputs(seed))
    spreads = {'L0_gnn_b1': (0.0, 0.8),
     'L0_gnn_b2': (0.0, 0.8),
     'L0_gnn_gamma1': (1.0, 0.2),
     'L0_gnn_beta1': (0.0, 0.1),
     'L0_gnn_gamma2': (1.0, 0.2),
     'L0_gnn_beta2': (0.0, 0.1),
     'L0_ffn_router_b1': (0.0, 0.363),
     'L0_ffn_router_b2': (0.0, 0.1),
     'L0_ffn_expert_b1': (0.0, 0.8),
     'L0_ffn_expert_b2': (0.0, 0.497),
     'L0_ffn_expert_b3': (0.0, 0.1)}
    factors = {}
    for name, (base, spread) in spreads.items():
        noise = np.random.default_rng([zlib.crc32(name.encode()), seed]).standard_normal(out[name].shape)
        drawn = base * np.exp(spread * noise) if base else spread * noise
        out[name] = jnp.asarray(drawn.astype(out[name].dtype))
    for name, factor in factors.items():
        out[name] = (out[name] * factor).astype(out[name].dtype)
    return out
```

```python
from contextlib import ExitStack

import numpy as np

import concourse.bass as bass
from concourse import mybir

F32 = mybir.dt.float32
BF16 = mybir.dt.bfloat16
I32 = mybir.dt.int32
U32 = mybir.dt.uint32
ALU = mybir.AluOpType
ACT = mybir.ActivationFunctionType
AX = mybir.AxisListType
RMAX = bass.bass_isa.ReduceOp.max

P = 128
RB = 112
BPC = 4
CH = RB * BPC
EC = P
CPG = 4
GE = EC * CPG
WIN = 64
GWIN = 256
DCH = 16
SLOTS = 8
BIG = float(1 << 20)
EPS = 1e-5


def sizes(n_nodes, n_edges):
    n_chunks = -(-n_nodes // CH)
    n_chunks += n_chunks % 2
    n_groups = -(-n_edges // GE)
    n_groups += -n_groups % 8
    n_tables = -(-(n_groups + 4) // P)
    return n_chunks, n_groups, n_tables


def wait(eng, sem, value):
    if not isinstance(value, int) or value > 0:
        eng.wait_ge(sem, value)


def hold(eng):
    eng.nop(nofuse=True)


class Chain:

    def __init__(self, eng, sem):
        self.eng, self.sem, self.base, self.n = eng, sem, 0, 0

    def begin(self, base):
        self.base, self.n = base, 0

    def step(self, instruction):
        self.n += 1
        instruction.then_inc(self.sem, 1)
        self.eng.wait_ge(self.sem, self.base + self.n)


def gnn_moe(nc, N, E, x, src, dst, W1, b1, W2, b2, gamma1, beta1, gamma2, beta2,
            rw1, rb1, rw2, rb2, ew1, eb1, ew2, eb2, ew3, eb3, out):
    D = x.shape[1]
    KH = D // P
    NX = ew1.shape[0]
    NCH, NG, NT = sizes(N, E)
    NPAD = NCH * CH
    NBLK = NCH * BPC
    NW = -(-NPAD // GWIN)
    WIDTH = max(NPAD, NW * GWIN)
    WMAX = NPAD - WIN
    TG = min(NT * P, NG + 32)
    TAIL = N - (NCH - 1) * CH
    PAIRS = NCH // 2
    PARTS = 3
    NHI = NPAD // P
    DSTEPS = NG * CPG // DCH
    DPER = DSTEPS // NCH
    assert D == 256 and NPAD % P == 0 and NHI <= P and NBLK <= P and NT <= 4 and 0 < TAIL <= CH and rw1.shape[1] == P

    t_dram = [nc.dram_tensor(f"messages_{n}", (NPAD, PARTS * D), BF16, kind="Internal").ap() for n in (1, 2)]
    w_dram = nc.dram_tensor("window_starts", (NT * P,), I32, kind="Internal").ap()
    dinv_dram = nc.dram_tensor("dinv_row", (NPAD,), F32, kind="Internal").ap()

    with ExitStack() as ctx:
        def sb(name, shape, dt=F32):
            return ctx.enter_context(nc.sbuf_tensor(name, shape, dt))

        def sem(name):
            return ctx.enter_context(nc.semaphore(name))

        def sems(name, n):
            return [sem(f"{name}{i}") for i in range(n)]

        acc = sb("acc", [P, KH, WIDTH])
        dinvT = sb("dinvT", [P, WIDTH])
        relT = sb("relT", [P, max(TG * CPG, KH * 2 * CH)])
        srcT = sb("srcT", [P, max(TG * CPG, KH * 2 * CH)])
        ring = sb("ring", [P, SLOTS * PARTS * D // 2])
        onehot_mem = sb("onehot_mem", [P, 2 * CPG * GWIN // 2])
        xbuf = sb("xbuf", [P, 2, BPC, D])
        rbuf = sb("rbuf", [P, 2, BPC, D])
        wconv = sb("wconv", [P, 2, KH, D])
        vec = sb("vec", [P, 6, KH])
        ident = sb("ident", [P, P])
        iota_bf = sb("iota_bf", [P, GWIN], BF16)
        idx_stage = sb("idx_stage", [P, 2, SLOTS], I32)
        relk = sb("relk", [P, CPG])
        wrow = sb("wrow", [1, NT * P], I32)
        bnst = sb("bnst", [P, KH, NCH, 6])
        lnst = sb("lnst", [RB, NBLK, 6])
        ln_mean = sb("ln_mean", [RB, NBLK])
        ln_rstd = sb("ln_rstd", [RB, NBLK])
        ln_tmp = sb("ln_tmp", [RB, 3, NBLK])
        dcol = sb("dcol", [RB, NBLK])
        dn = sb("dn", [NBLK, RB])
        wlo = sb("wlo", [P, NT])
        whi = sb("whi", [P, NT])
        w_int = sb("w_int", [P, NT], I32)
        flags = sb("flags", [P, 4])
        bad_int = sb("bad_int", [P, 1], I32)
        bn_mv = sb("bn_mv", [P, KH, 2])
        bn_sc = sb("bn_sc", [P, 4, KH])
        marker = sb("marker", [P, 2, 5])
        ps = ctx.enter_context(nc.psum_tensor("ps", [P, 8, 512], F32))

        accflat = acc[:, :, :].rearrange("p k n -> p (k n)")
        TE = NT * GE
        dst_i = accflat[:, 0:TE].bitcast(I32).rearrange("p (t e) -> p t e", t=NT)
        src_i = accflat[:, TE:2 * TE].bitcast(I32).rearrange("p (t e) -> p t e", t=NT)
        dst_f = accflat[:, 2 * TE:3 * TE].rearrange("p (t e) -> p t e", t=NT)
        src_f = accflat[:, 3 * TE:4 * TE].rearrange("p (t e) -> p t e", t=NT)
        tmp_f = accflat[:, 4 * TE:5 * TE].rearrange("p (t e) -> p t e", t=NT)
        iota_i = accflat[:, 5 * TE:5 * TE + GWIN].bitcast(I32)
        lent = [5 * TE + GWIN]

        def lend(n_bytes):
            a = accflat[:, lent[0]:lent[0] + n_bytes // 4]
            lent[0] += n_bytes // 4
            assert lent[0] <= KH * WIDTH
            return a

        dstT_i, digit_i = lend(4 * TG * CPG).bitcast(I32), lend(4 * TG * CPG).bitcast(I32)
        loT, hiT = lend(2 * TG * CPG).bitcast(BF16), lend(2 * TG * CPG).bitcast(BF16)
        iota_rep = lend(2 * P * DCH).bitcast(BF16).rearrange("p (w j) -> p w j", j=DCH)
        oh_lo = [lend(2 * P * DCH).bitcast(BF16).rearrange("p (w j) -> p w j", j=DCH) for _ in range(2)]
        oh_hi = [lend(2 * NHI * DCH).bitcast(BF16).rearrange("p (w j) -> p w j", j=DCH) for _ in range(2)]
        rel3 = relT[:, 0:TG * CPG].rearrange("p (g j) -> p g j", j=CPG)
        src3 = srcT[:, 0:TG * CPG].bitcast(I32).rearrange("p (g j) -> p g j", j=CPG)
        srcidx = srcT[:, 0:TG * CPG].bitcast(I32)
        dg = ring[0:NHI, 0:P]
        ring_bf = ring[:, :].bitcast(BF16)
        slots = ring_bf.rearrange("p (s f) -> p s f", s=SLOTS)
        split = ring_bf.rearrange("p (u b f) -> p u b f", u=2, b=BPC)
        onehot = onehot_mem[:, :].bitcast(BF16).rearrange("p (u j w) -> p u j w", u=2, j=CPG)
        lin_tmp = [rbuf[:, u, :, :].rearrange("p b f -> p (b f)")[:, 0:KH * CH].rearrange("p (k n) -> p k n", k=KH)
                   for u in range(2)]
        ybuf = [xbuf[:, u, :, :].rearrange("p b f -> p (b f)")[:, 0:KH * CH].rearrange("p (k n) -> p k n", k=KH)
                for u in range(2)]
        wx = dinvT[:, 0:3 * NX * KH * D].rearrange("p (m e k n) -> p m e k n", m=3, e=NX, k=KH)
        at = 3 * NX * KH * D
        b3_bc = dinvT[0:RB, at:at + NX * D].rearrange("p (e n) -> p e n", e=NX)
        at += NX * D
        rhT = dinvT[:, at:at + CH]
        at += CH
        rw1_sb = dinvT[:, at:at + KH * P].rearrange("p (k n) -> p k n", k=KH)
        at += KH * P
        eb1_sb = dinvT[:, at:at + NX * KH].rearrange("p (e k) -> p e k", k=KH)
        at += NX * KH
        eb2_sb = dinvT[:, at:at + NX * KH].rearrange("p (e k) -> p e k", k=KH)
        at += NX * KH
        rw2_sb = dinvT[:, at:at + NX]
        at += NX
        rb1_sb = dinvT[:, at:at + 1]
        at += 2
        small_at = [at]

        def small(*shape):
            n = int(np.prod(shape))
            a = dinvT[0:RB, small_at[0]:small_at[0] + n]
            small_at[0] += n
            if len(shape) == 1:
                return a
            names = "abc"[:len(shape)]
            return a.rearrange(f"p ({' '.join(names)}) -> p {' '.join(names)}", **dict(zip(names, shape)))

        st4, sum4, dif4, m24, mean4, var4, sd4, rstd4 = small(BPC, 6), *[small(BPC) for _ in range(7)]
        lg, ex, prob, top8 = small(BPC, NX), small(BPC, NX), small(BPC, 8), small(BPC, 8)
        idx8 = small(BPC, 8).bitcast(U32)
        idxf = small(BPC, 8)
        lmax, lsum, lrec, gap, e2, den, w1st, w2nd = [small(BPC, 1) for _ in range(8)]
        m1st, m2nd, wsel = small(BPC, NX), small(BPC, NX), small(2, BPC * NX)
        iota6, rb2_sb = small(NX), small(NX)
        assert small_at[0] <= WIDTH
        xfT = [ring[:, u * KH * CH:(u + 1) * KH * CH].rearrange("p (k n) -> p k n", k=KH) for u in range(2)]
        zb = ring[:, 2 * KH * CH:3 * KH * CH].rearrange("p (k n) -> p k n", k=KH)
        h1T = [relT[:, u * KH * CH:(u + 1) * KH * CH].rearrange("p (k n) -> p k n", k=KH) for u in range(2)]
        h2T = [srcT[:, u * KH * CH:(u + 1) * KH * CH].rearrange("p (k n) -> p k n", k=KH) for u in range(2)]
        trow = onehot_mem[0:RB, 0:BPC * D].rearrange("p (b f) -> p b f", b=BPC)

        edges_in, consts_in, w_row, dn_in, ffn_in = sem("edges_in"), sem("consts_in"), sem("w_row"), sem("dn_in"), sem("ffn_in")
        ident_ready, iota_ready, iota_bf_ready = sem("ident_ready"), sem("iota_ready"), sem("iota_bf_ready")
        span_ready, span_all, flag_ready, w_ready = sem("span_ready"), sem("span_all"), sem("flag_ready"), sem("w_ready")
        edges_ready, dst_turned, dst_kept = sem("edges_ready"), sem("dst_turned"), sem("dst_kept")
        rel_ready, tables_turned, tables_ready, src_kept = sem("rel_ready"), sem("tables_turned"), sem("tables_ready"), sem("src_kept")
        sqrt_done, dinv_in = sem("sqrt_done"), sem("dinv_in")
        deg_onehot, deg_summed, deg_done, dinv_ready = sem("deg_onehot"), sem("deg_summed"), sem("deg_done"), sem("dinv_ready")
        dn_turned, ln_var, ln_sd = sem("dn_turned"), sem("ln_var"), sem("ln_sd")
        stat_x_in, stats_done = sems("stat_x_in", 2), sem("stats_done")
        dve_chain, ffn_chain = sem("dve_chain"), sem("ffn_chain")
        got = sems("got", SLOTS)
        stage_ready, chunks_used = sem("stage_ready"), sem("chunks_used")
        oh_fast, ev_fast = sems("oh_fast", 2), sems("ev_fast", 2)
        oh_gen, mm_gen, ev_gen, rk_gen = sems("oh_gen", 2), sems("mm_gen", 2), sems("ev_gen", 2), sems("rk_gen", 2)
        agg_done = sem("agg_done")
        v_x_in = sems("v_x_in", 2)
        v_ready, v_turned, v_kept = sem("v_ready"), sem("v_turned"), sem("v_kept")
        hi_done, r1_done, mid_done, lo_done = sems("hi_done", 2), sems("r1_done", 2), sems("mid_done", 2), sems("lo_done", 2)
        stored = [sems("stored1_", 2), sems("stored2_", 2)]
        lin_done, lin_scaled, lin_biased = sems("lin_done", 2), sems("lin_scaled", 2), sems("lin_biased", 2)
        bn_var, bn_sd, bn_ready = sem("bn_var"), sem("bn_sd"), sem("bn_ready")
        relu_done, y_ready, y_kept, y_turned = sem("relu_done"), sem("y_ready"), sem("y_kept"), sem("y_turned")
        f_x_in, f_out = sems("f_x_in", 2), sems("f_out", 2)
        zb_done, z_turned, var_done, sd_done, xf_done = sem("zb_done"), sem("z_turned"), sem("var_done"), sem("sd_done"), sem("xf_done")
        x_turned, xfT_done, rh_done, rhT_done, lg_mm, lg_done = sem("x_turned"), sem("xfT_done"), sem("rh_done"), sem("rhT_done"), sem("lg_mm"), sem("lg_done")
        sh_done, ex_done, gap_done, e2_done = sem("sh_done"), sem("ex_done"), sem("gap_done"), sem("e2_done")
        l1_done, l2_done, l3_done = sem("l1_done"), sem("l2_done"), sem("l3_done")
        h1_act, h1_dve, h2_act, h2_dve, combined = sem("h1_act"), sem("h1_dve"), sem("h2_act"), sem("h2_dve"), sem("combined")

        NCONST = 2 + 6
        NFFN = 3 * NX + 1 + 4 + 2 * KH
        GATHERS = NG * CPG
        L1, L2 = 0, 1

        def nodes(ap, t):
            return ap[bass.ds(t * CH, CH), :].rearrange("(b p) f -> p b f", p=RB)

        def in_pairs(eng, body, last=PAIRS):
            for u in range(2):
                body(u, u)
            if last > 1:
                with eng.Fori(1, last) as i:
                    for u in range(2):
                        body(i * 2 + u, u)

        def half(t, u):
            return (t - u) // 2 if isinstance(t, int) else t // 2

        block = ctx.enter_context(nc.Block())

        @block.sync
        def _(sp):
            sp.dma_start(dst_i, dst.rearrange("(t q e) -> q t e", q=P, e=GE)).then_inc(edges_in, 16)
            sp.dma_start(src_i, src.rearrange("(t q e) -> q t e", q=P, e=GE)).then_inc(edges_in, 16)
            for n, w in enumerate((W1, W2)):
                sp.dma_start(wconv[:, n, :, :], w.rearrange("(k p) n -> p k n", p=P)).then_inc(consts_in, 16)
            with nc.allow_non_contiguous_dma(reason="small vectors, one feature a partition"):
                for n, v in enumerate((b1, gamma1, beta1, b2, gamma2, beta2)):
                    sp.dma_start(vec[:, n, :], v.rearrange("(k p) -> p k", p=P)).then_inc(consts_in, 16)

            def stat_load(t, u):
                wait(sp, stats_done, t - 1)
                sp.dma_start(xbuf[0:RB, u, :, :], nodes(x, t)).then_inc(stat_x_in[u], 16)

            in_pairs(sp, stat_load)

            sp.wait_ge(w_ready, 1)
            with nc.allow_non_contiguous_dma(reason="one window start a partition"):
                sp.dma_start(w_dram.rearrange("(t q) -> q t", q=P), w_int[:, :]).then_inc(w_row, 16)
            sp.wait_ge(w_row, 16)
            sp.dma_start(wrow[:, :], w_dram.rearrange("(o n) -> o n", o=1)).then_inc(w_row, 16)

            sp.wait_ge(dinv_ready, 1)
            sp.dma_start(dinv_dram.rearrange("(h l) -> h l", l=P), dg[:, :]).then_inc(dn_in, 16)
            sp.wait_ge(dn_in, 16)
            sp.dma_start(dn[:, :], dinv_dram.rearrange("(n p) -> n p", p=RB)).then_inc(dn_in, 16)

            sp.wait_ge(stats_done, NCH)

            def v_load(t, u):
                wait(sp, v_turned, t - 1)
                wait(sp, r1_done[0], t - 1)
                sp.dma_start(xbuf[0:RB, u, :, :], nodes(x, t)).then_inc(v_x_in[u], 16)

            def store(layer, t, u):
                sp.wait_ge(lo_done[layer], t + 1)
                sp.dma_start(nodes(t_dram[layer], t), split[0:RB, u, :, :]).then_inc(stored[layer][u], 16)

            v_load(0, 0)
            v_load(1, 1)
            with sp.Fori(1, PAIRS) as i:
                for u in range(2):
                    store(0, i * 2 + u - 2, u)
                    v_load(i * 2 + u, u)
            for u in range(2):
                store(0, NCH - 2 + u, u)

            sp.dma_start(dinvT[:, 0:NPAD], dinv_dram.rearrange("(o n) -> o n", o=1).to_broadcast([P, NPAD])).then_inc(dinv_in, 16)

            in_pairs(sp, lambda t, u: store(1, t, u))

            sp.wait_ge(lin_scaled[1], NCH)
            for m, w in enumerate((ew1, ew2, ew3)):
                for e in range(NX):
                    sp.dma_start(wx[:, m, e, :, :], w[e, :, :].rearrange("(k p) n -> p k n", p=P)).then_inc(ffn_in, 16)
            sp.dma_start(b3_bc, eb3.rearrange("(o e) n -> o e n", o=1).to_broadcast([RB, NX, D])).then_inc(ffn_in, 16)

            with nc.allow_non_contiguous_dma(reason="small vectors, one feature a partition"):
                sp.dma_start(rw1_sb, rw1.rearrange("(k p) n -> p k n", p=P)).then_inc(ffn_in, 16)
                sp.dma_start(rb1_sb, rb1.rearrange("(p o) -> p o", o=1)).then_inc(ffn_in, 16)
                sp.dma_start(rw2_sb, rw2).then_inc(ffn_in, 16)
                sp.dma_start(rb2_sb, rb2.rearrange("(o n) -> o n", o=1).to_broadcast([RB, NX])).then_inc(ffn_in, 16)
                for b_sb, b_d in ((eb1_sb, eb1), (eb2_sb, eb2)):
                    for k in range(KH):
                        sp.dma_start(b_sb[:, :, k], b_d[:, k * P:(k + 1) * P].rearrange("e p -> p e")).then_inc(ffn_in, 16)

            def f_load(t, u):
                wait(sp, xf_done, t - 1)
                sp.dma_start(xbuf[0:RB, u, :, :], nodes(x, t)).then_inc(f_x_in[u], 16)

            def f_store(t, u):
                sp.wait_ge(combined, NX * (t + 1))
                sp.dma_start(nodes(out, t), rbuf[0:RB, u, :, :]).then_inc(f_out[u], 16)

            f_load(0, 0)
            f_load(1, 1)
            with sp.Fori(1, PAIRS) as i:
                for u in range(2):
                    f_load(i * 2 + u, u)
                    f_store(i * 2 + u - 2, u)
            for u in range(2):
                f_store(NCH - 2 + u, u)
            for u in range(2):
                sp.wait_ge(f_out[u], 16 * PAIRS)

        @block.gpsimd
        def _(pool):
            pool.memset(ident[:, :], 0.0).then_inc(ident_ready, 1)
            pool.iota(iota_i, pattern=[[1, GWIN]], base=0, channel_multiplier=0).then_inc(iota_ready, 1)
            pool.wait_ge(ident_ready, 1)
            pool.affine_select(out=ident[:, :], in_=ident[:, :], compare_op=ALU.not_equal, fill=1.0, base=0,
                               pattern=[[-1, P]], channel_multiplier=1).then_inc(ident_ready, 1)
            pool.wait_ge(span_ready, 1)
            pool.partition_all_reduce(flags[:, 1:2], flags[:, 0:1], P, RMAX).then_inc(span_all, 1)

            def gathers(layer):
                done = layer * GATHERS
                for u in range(2):
                    pool.wait_ge(stored[layer][u], 16 * PAIRS)

                def gather(i, u, first):
                    c0 = i * (2 * SLOTS) + u * SLOTS
                    pool.wait_ge(stage_ready, i * 2 + u + 1 + done // SLOTS)
                    for s in range(SLOTS):
                        wait(pool, chunks_used, c0 + s - SLOTS + 1 + done)
                        hold(pool)
                        pool.indirect_dma_start(
                            out=slots[:, s, :], out_offset=None, in_=t_dram[layer],
                            in_offset=bass.IndirectOffsetOnAxis(ap=idx_stage[:, u, s:s + 1], axis=0),
                        ).then_inc(got[s], 16)

                for u in range(2):
                    gather(0, u, True)
                if GATHERS > 2 * SLOTS:
                    with pool.Fori(1, GATHERS // (2 * SLOTS)) as i:
                        for u in range(2):
                            gather(i, u, False)

            gathers(L1)

            def keep_y(t, u):
                pool.wait_ge(y_ready, t + 1)
                hold(pool)
                pool.tensor_copy(acc[:, :, bass.ds(t * CH, CH)], ybuf[u]).then_inc(y_kept, 1)

            in_pairs(pool, keep_y)
            gathers(L2)

        @block.scalar
        def _(act):
            act.wait_ge(dst_turned, 1)
            for n in range(NT):
                ng = min(P, TG - n * P)
                turned = ps[:, NT + n, :].rearrange("p (j g) -> p g j", j=CPG)
                last = act.activation(src3[:, n * P:n * P + ng, :], turned[:, 0:ng, :], ACT.Copy)
            last.then_inc(src_kept, 1)
            act.wait_ge(ln_var, 1)
            act.activation(ln_rstd[:, :], ln_tmp[:, 0, :], ACT.Sqrt).then_inc(ln_sd, 1)
            act.wait_ge(deg_done, 1)
            act.activation(dg[:, :], dg[:, :], ACT.Sqrt).then_inc(sqrt_done, 1)

            def split_rows(layer, t, u, rows):
                wait(act, stored[layer][u], 16 * half(t, u))
                hold(act)
                act.activation(split[0:RB, u, :, 0:D], rows, ACT.Copy).then_inc(hi_done[layer], 1)
                act.wait_ge(r1_done[layer], t + 1)
                hold(act)
                act.activation(split[0:RB, u, :, D:2 * D], rbuf[0:RB, u, :, :], ACT.Copy).then_inc(mid_done[layer], 1)

            def v_split(t, u):
                act.wait_ge(v_ready, t + 1)
                split_rows(0, t, u, xbuf[0:RB, u, :, :])
                act.wait_ge(v_turned, t + 1)
                hold(act)
                act.activation(acc[:, :, bass.ds(t * CH, CH)], ps[:, 2 * u:2 * u + KH, 0:CH], ACT.Copy).then_inc(v_kept, 1)

            in_pairs(act, v_split)

            def stage_indices(layer):
                done = layer * GATHERS

                def stage(i, u):
                    wait(act, chunks_used, (i - 1) * (2 * SLOTS) + u * SLOTS + SLOTS + done)
                    hold(act)
                    act.activation(idx_stage[:, u, :], srcidx[:, bass.ds(i * (2 * SLOTS) + u * SLOTS, SLOTS)],
                                   ACT.Copy).then_inc(stage_ready, 1)

                for u in range(2):
                    stage(0, u)
                if GATHERS > 2 * SLOTS:
                    with act.Fori(1, GATHERS // (2 * SLOTS)) as i:
                        for u in range(2):
                            stage(i, u)

            def linear_bias(layer):
                def add_bias(t, u):
                    act.wait_ge(lin_scaled[layer], t + 1)
                    hold(act)
                    for k in range(KH):
                        last = act.activation(acc[:, k, bass.ds(t * CH, CH)], lin_tmp[u][:, k, :], ACT.Identity,
                                              bias=vec[:, 3 * layer, k:k + 1])
                    last.then_inc(lin_biased[layer], 1)

                in_pairs(act, add_bias)
                act.wait_ge(bn_var, layer + 1)
                act.activation(bn_sc[:, 0, :], bn_sc[:, 1, :], ACT.Sqrt).then_inc(bn_sd, 1)

            act.wait_ge(src_kept, 1)
            act.wait_ge(consts_in, 16 * NCONST)
            stage_indices(L1)
            linear_bias(0)
            act.wait_ge(bn_ready, 1)

            def relu(t):
                for k in range(KH):
                    part = acc[:, k, bass.ds(t * CH, CH)]
                    last = act.activation(part, part, ACT.Relu, bias=bn_sc[:, 3, k:k + 1], scale=bn_sc[:, 2, k:k + 1])
                last.then_inc(relu_done, 1)

            def y_split(t, u):
                act.wait_ge(y_turned, t + 1)
                split_rows(1, t, u, ps[0:RB, 2 * u:2 * u + 2, :].rearrange("p a (b f) -> p (a b) f", b=2))

            relu(0)
            relu(1)
            y_split(0, 0)
            with act.Fori(1, PAIRS) as i:
                relu(i * 2)
                y_split(i * 2 - 1, 1)
                relu(i * 2 + 1)
                y_split(i * 2, 0)
            y_split(NCH - 1, 1)

            stage_indices(L2)
            linear_bias(1)
            act.wait_ge(bn_ready, 2)
            act.wait_ge(ffn_in, 16 * NFFN)

            def piece(p, t, u):
                if p == 0:
                    wait(act, z_turned, t)
                    hold(act)
                    for k in range(KH):
                        last = act.activation(zb[:, k, :], acc[:, k, bass.ds(t * CH, CH)], ACT.Identity,
                                              bias=bn_sc[:, 3, k:k + 1], scale=bn_sc[:, 2, k:k + 1])
                    last.then_inc(zb_done, 1)
                elif p == 2:
                    act.wait_ge(var_done, t + 1)
                    act.activation(sd4, var4, ACT.Sqrt).then_inc(sd_done, 1)
                elif p == 3:
                    act.wait_ge(x_turned, t + 1)
                    act.activation(xfT[u], ps[:, 6:6 + KH, 0:CH], ACT.Copy).then_inc(xfT_done, 1)
                elif p == 4:
                    act.wait_ge(rh_done, t + 1)
                    act.activation(rhT, ps[:, 6, 0:CH], ACT.Relu, bias=rb1_sb[:, 0:1]).then_inc(rhT_done, 1)
                elif p == 5:
                    act.wait_ge(sh_done, t + 1)
                    act.activation(ex, lg, ACT.Exp).then_inc(ex_done, 1)
                    act.wait_ge(gap_done, t + 1)
                    act.activation(e2, gap, ACT.Exp).then_inc(e2_done, 1)

            def hidden(layer, t, e):
                q = t * NX + e
                done, free, hT, bias, out_sem, bank = (
                    (l1_done, (l2_done, 2 * q - 2), h1T, eb1_sb, h1_act, 0),
                    (l2_done, (l3_done, q - 1), h2T, eb2_sb, h2_act, 2))[layer]
                wait(act, *free)
                act.wait_ge(done, 2 * q + 1)
                act.activation(hT[e % 2][:, 0, :], ps[:, bank, 0:CH], ACT.Relu, bias=bias[:, e, 0:1]).then_inc(out_sem, 1)

            def experts(t, u, more):
                for e in range(NX):
                    if e == 0:
                        hidden(0, t, 0)
                    hidden(1, t, e)
                    if e + 1 < NX:
                        hidden(0, t, e + 1)
                    if more:
                        piece(e, t + 1, 1 - u)

            for p in range(6):
                piece(p, 0, 0)
            in_pairs(act, lambda t, u: experts(t, u, True), PAIRS - 1)
            experts(NCH - 2, 0, True)
            experts(NCH - 1, 1, False)

        @block.vector
        def _(dve):
            chain = Chain(dve, dve_chain)
            step = chain.step
            dve.wait_ge(iota_ready, 1)
            dve.tensor_copy(iota_bf[:, :], iota_i).then_inc(iota_bf_ready, 1)

            dve.wait_ge(edges_in, 32)
            dve.tensor_copy(src_f, src_i)
            step(dve.tensor_copy(dst_f, dst_i))
            dve.memset(marker[:, 0, 3:4], 0.0).then_inc(edges_ready, 1)
            step(dve.tensor_scalar(tmp_f, dst_f, 0.0, BIG, ALU.is_lt, ALU.mult))
            step(dve.tensor_tensor(tmp_f, tmp_f, dst_f, ALU.add))
            step(dve.tensor_reduce(wlo[:, :], tmp_f, AX.X, ALU.min))
            step(dve.tensor_reduce(whi[:, :], dst_f, AX.X, ALU.max))
            step(dve.tensor_scalar(wlo[:, :], wlo[:, :], float(WMAX), None, ALU.min))
            step(dve.tensor_tensor(whi[:, :], whi[:, :], wlo[:, :], ALU.subtract))
            dve.tensor_reduce(flags[:, 0:1], whi[:, :], AX.X, ALU.max).then_inc(span_ready, 1)
            dve.wait_ge(span_all, 1)
            step(dve.tensor_scalar(flags[:, 2:3], flags[:, 1:2], float(WIN), None, ALU.is_lt))
            step(dve.tensor_scalar(flags[:, 3:4], flags[:, 2:3], -1.0, 1.0, ALU.mult, ALU.add))
            dve.tensor_copy(bad_int[:, :], flags[:, 3:4]).then_inc(flag_ready, 1)
            step(dve.tensor_scalar(wlo[:, :], wlo[:, :], flags[:, 2:3], None, ALU.mult))
            dve.tensor_copy(w_int[:, :], wlo[:, :]).then_inc(w_ready, 1)
            def keep_table(table):
                for n in range(NT):
                    ng = min(P, TG - n * P)
                    turned = ps[:, n, :].rearrange("p (j g) -> p g j", j=CPG)
                    last = dve.tensor_copy(table[:, n * P:n * P + ng, :], turned[:, 0:ng, :])
                return last

            dve.wait_ge(dst_turned, 1)
            for n in range(NT):
                last = dve.tensor_scalar(dst_f[:, n, :], dst_f[:, n, :], wlo[:, n:n + 1], None, ALU.subtract)
            last.then_inc(rel_ready, 1)
            keep_table(dstT_i.rearrange("p (g j) -> p g j", j=CPG)).then_inc(dst_kept, 1)
            dve.wait_ge(dst_kept, 1)
            step(dve.tensor_scalar(digit_i, dstT_i, P - 1, None, ALU.bitwise_and))
            step(dve.tensor_copy(loT, digit_i))
            step(dve.tensor_scalar(digit_i, dstT_i, P.bit_length() - 1, None, ALU.arith_shift_right))
            dve.tensor_copy(hiT, digit_i)
            dve.wait_ge(iota_bf_ready, 1)
            step(dve.tensor_copy(iota_rep, iota_bf[:, 0:P].unsqueeze(2).to_broadcast([P, P, DCH])))
            dve.wait_ge(tables_turned, 1)
            keep_table(rel3).then_inc(tables_ready, 1)

            def row_stats(t, u):
                dve.wait_ge(stat_x_in[u], 16 * (half(t, u) + 1))
                hold(dve)
                for b in range(BPC):
                    last = dve.bn_stats(lnst[:, bass.ds(t * BPC + b, 1), :].rearrange("p o s -> p (o s)"), xbuf[0:RB, u, b, :])
                last.then_inc(stats_done, 1)

            def deg_step(d, u):
                wait(dve, deg_summed, d - 1)
                for table, oh, n in ((loT, oh_lo, P), (hiT, oh_hi, NHI)):
                    digit = table[:, bass.ds(d * DCH, DCH)].unsqueeze(1).to_broadcast([P, n, DCH])
                    last = dve.tensor_tensor(oh[u], iota_rep[:, 0:n, :], digit, ALU.is_equal)
                last.then_inc(deg_onehot, 1)

            def stats_and_degrees(t, u):
                row_stats(t, u)
                for k in range(DPER):
                    deg_step(t * DPER + k, (u * DPER + k) % 2)

            in_pairs(dve, stats_and_degrees)
            for d in range(NCH * DPER, DSTEPS):
                deg_step(d, d % 2)

            def mean_var(st, sm, df, m2, mean, var, step):
                step(dve.tensor_tensor(sm, st[:, :, 1], st[:, :, 4], ALU.add))
                step(dve.tensor_tensor(df, st[:, :, 1], st[:, :, 4], ALU.subtract))
                step(dve.tensor_tensor(m2, st[:, :, 2], st[:, :, 5], ALU.add))
                step(dve.tensor_scalar(mean, sm, 0.5, None, ALU.mult))
                step(dve.tensor_tensor(df, df, df, ALU.mult))
                step(dve.scalar_tensor_tensor(out=m2, in0=df, scalar=D / 4.0, in1=m2, op0=ALU.mult, op1=ALU.add))
                return dve.tensor_scalar(var, m2, 1.0 / D, EPS, ALU.mult, ALU.add)

            dve.wait_ge(stats_done, NCH)
            mean_var(lnst[:, :, :], ln_tmp[:, 0, :], ln_tmp[:, 1, :], ln_tmp[:, 2, :], ln_mean[:, :], ln_tmp[:, 0, :],
                     step).then_inc(ln_var, 1)
            dve.wait_ge(ln_sd, 1)
            step(dve.reciprocal(ln_rstd[:, :], ln_rstd[:, :]))

            dve.wait_ge(deg_summed, DSTEPS)
            dve.tensor_scalar(dg[:, :], ps[0:NHI, NT, 0:P], 1.0, None, ALU.add).then_inc(deg_done, 1)
            dve.wait_ge(sqrt_done, 1)
            dve.reciprocal(dg[:, :], dg[:, :]).then_inc(dinv_ready, 1)

            dve.wait_ge(flag_ready, 1)
            dve.wait_ge(w_row, 32)
            bad = dve.value_load(bad_int[0:1, 0:1], min_val=0, max_val=1)

            def aggregate(run):
                def sums(at, width):
                    return acc[:, :, bass.ds(at, width)]

                def partial(u, width):
                    return ps[:, 2 * u:2 * u + KH, 0:width]

                def product_done(n):
                    wait(dve, chunks_used, n * CPG + run * GATHERS if not isinstance(n, int) or n > 0 else 0)

                def make_onehot(g, u):
                    for j in range(CPG):
                        last = dve.tensor_scalar(onehot[:, u, j, 0:WIN], iota_bf[:, 0:WIN],
                                                 relT[:, bass.ds(g * CPG + j, 1)], None, ALU.is_equal)
                    last.then_inc(oh_fast[run], 1)

                def fast(g, u):
                    product_done(g)
                    hold(dve)
                    make_onehot(g + 1, 1 - u)
                    w = dve.value_load(wrow[0:1, bass.ds(g, 1)], min_val=0, max_val=WMAX)
                    product_done(g + 1)
                    wait(dve, ev_fast[run], g)
                    dve.tensor_tensor(sums(w, WIN), sums(w, WIN), partial(u, WIN), ALU.add).then_inc(ev_fast[run], 1)

                def general(g):
                    dve.wait_ge(rk_gen[run], g * (NW + 1) + 1)
                    hold(dve)
                    dve.tensor_copy(relk[:, :], relT[:, bass.ds(g * CPG, CPG)]).then_inc(rk_gen[run], 1)
                    with dve.Fori(0, NW) as k:
                        s = g * NW + k
                        dve.wait_ge(rk_gen[run], g * (NW + 1) + k + 2)
                        dve.wait_ge(mm_gen[run], s + 1)
                        hold(dve)
                        for j in range(CPG):
                            last = dve.tensor_scalar(onehot[:, 0, j, :], iota_bf[:, :], relk[:, j:j + 1], None, ALU.is_equal)
                        last.then_inc(oh_gen[run], 1)
                        dve.wait_ge(oh_gen[run], s + 1)
                        dve.tensor_scalar(relk[:, :], relk[:, :], float(GWIN), None, ALU.subtract).then_inc(rk_gen[run], 1)
                        dve.wait_ge(mm_gen[run], s + 2)
                        dve.wait_ge(ev_gen[run], s + 1)
                        hold(dve)
                        dve.tensor_tensor(sums(k * GWIN, GWIN), sums(k * GWIN, GWIN), partial(0, GWIN),
                                          ALU.add).then_inc(ev_gen[run], 1)
                    dve.memset(marker[:, run, 2:3], 0.0).then_inc(chunks_used, CPG)

                with dve.If(bad == 0):
                    make_onehot(0, 0)
                    for g in range(4):
                        fast(g, g % 2)
                    with dve.Fori(1, NG // 4) as i:
                        for q in range(4):
                            fast(i * 4 + q, q % 2)
                    dve.wait_ge(ev_fast[run], NG)
                with dve.Else():
                    dve.memset(marker[:, run, 0:1], 0.0).then_inc(mm_gen[run], 1)
                    dve.memset(marker[:, run, 1:2], 0.0).then_inc(ev_gen[run], 1)
                    dve.memset(marker[:, run, 4:5], 0.0).then_inc(rk_gen[run], 1)
                    with dve.Fori(0, NG) as g:
                        general(g)
                    dve.wait_ge(ev_gen[run], NG * NW + 1)

            dve.wait_ge(dn_turned, 1)
            step(dve.tensor_copy(dcol[:, :], ps[0:RB, 7, 0:NBLK]))
            step(dve.tensor_tensor(dcol[:, :], dcol[:, :], ln_rstd[:, :], ALU.mult))

            def split_rows(layer, t, u, rows):
                dve.wait_ge(hi_done[layer], t + 1)
                dve.tensor_tensor(rbuf[0:RB, u, :, :], rows, split[0:RB, u, :, 0:D], ALU.subtract).then_inc(r1_done[layer], 1)
                dve.wait_ge(mid_done[layer], t + 1)
                dve.tensor_tensor(split[0:RB, u, :, 2 * D:3 * D], rbuf[0:RB, u, :, :], split[0:RB, u, :, D:2 * D],
                                  ALU.subtract).then_inc(lo_done[layer], 1)

            def v_rows(t, u):
                dve.wait_ge(v_x_in[u], 16 * (half(t, u) + 1))
                hold(dve)
                for b in range(BPC):
                    at = t * BPC + b
                    last = dve.tensor_scalar(xbuf[0:RB, u, b, :], xbuf[0:RB, u, b, :], ln_mean[:, bass.ds(at, 1)],
                                             dcol[:, bass.ds(at, 1)], ALU.subtract, ALU.mult)
                last.then_inc(v_ready, 1)

            def v_split(t, u):
                split_rows(0, t, u, xbuf[0:RB, u, :, :])

            v_rows(0, 0)
            v_rows(1, 1)
            v_split(0, 0)
            with dve.Fori(1, PAIRS) as i:
                v_rows(i * 2, 0)
                v_split(i * 2 - 1, 1)
                v_rows(i * 2 + 1, 1)
                v_split(i * 2, 0)
            v_split(NCH - 1, 1)

            def linear(layer):
                dve.wait_ge(dinv_in, 16)

                def dinv_part(t):
                    return dinvT[:, bass.ds(t * CH, CH)].unsqueeze(1).to_broadcast([P, KH, CH])

                def scale(t, u):
                    dve.wait_ge(lin_done[layer], t + 1)
                    wait(dve, lin_biased[layer], t - 1)
                    hold(dve)
                    dve.tensor_tensor(lin_tmp[u], ps[:, 2 * u:2 * u + KH, 0:CH], dinv_part(t), ALU.mult).then_inc(lin_scaled[layer], 1)

                def stats(t, width=CH):
                    dve.wait_ge(lin_biased[layer], t + 1)
                    hold(dve)
                    for k in range(KH):
                        last = dve.bn_stats(bnst[:, k, bass.ds(t, 1), :].rearrange("p o s -> p (o s)"),
                                            acc[:, k, bass.ds(t * CH, width)])
                    return last

                scale(0, 0)
                scale(1, 1)
                stats(0)
                with dve.Fori(1, PAIRS) as i:
                    scale(i * 2, 0)
                    stats(i * 2 - 1)
                    scale(i * 2 + 1, 1)
                    stats(i * 2)
                step(stats(NCH - 1, TAIL))
                for k in range(KH):
                    last = dve.bn_aggr(bn_mv[:, k, :], bnst[:, k, :, :].rearrange("p t s -> p (t s)"))
                step(last)
                dve.tensor_scalar(bn_sc[:, 1, :], bn_mv[:, :, 1], EPS, None, ALU.add).then_inc(bn_var, 1)
                dve.wait_ge(bn_sd, layer + 1)
                step(dve.reciprocal(bn_sc[:, 1, :], bn_sc[:, 0, :]))
                step(dve.tensor_tensor(bn_sc[:, 2, :], vec[:, 3 * layer + 1, :], bn_sc[:, 1, :], ALU.mult))
                step(dve.tensor_tensor(bn_sc[:, 3, :], bn_mv[:, :, 0], bn_sc[:, 2, :], ALU.mult))
                dve.tensor_tensor(bn_sc[:, 3, :], vec[:, 3 * layer + 2, :], bn_sc[:, 3, :], ALU.subtract).then_inc(bn_ready, 1)

            dve.wait_ge(consts_in, 16 * NCONST)
            dve.wait_ge(v_kept, NCH)
            aggregate(L1)
            dve.memset(marker[:, L1, 3:4], 0.0).then_inc(agg_done, 1)
            linear(0)

            def y_cols(t, u):
                dve.wait_ge(relu_done, t + 1)
                wait(dve, y_turned, t - 1)
                wait(dve, y_kept, t - 1)
                dve.tensor_tensor(ybuf[u], acc[:, :, bass.ds(t * CH, CH)],
                                  dinvT[:, bass.ds(t * CH, CH)].unsqueeze(1).to_broadcast([P, KH, CH]), ALU.mult).then_inc(y_ready, 1)

            def y_split(t, u):
                dve.wait_ge(y_turned, t + 1)
                split_rows(1, t, u, ps[0:RB, 2 * u:2 * u + 2, :].rearrange("p a (b f) -> p (a b) f", b=2))

            y_cols(0, 0)
            y_cols(1, 1)
            y_split(0, 0)
            with dve.Fori(1, PAIRS) as i:
                y_cols(i * 2, 0)
                y_split(i * 2 - 1, 1)
                y_cols(i * 2 + 1, 1)
                y_split(i * 2, 0)
            y_split(NCH - 1, 1)

            dve.wait_ge(y_kept, NCH)
            aggregate(L2)
            dve.memset(marker[:, L2, 3:4], 0.0).then_inc(agg_done, 1)
            linear(1)

            dve.wait_ge(ffn_in, 16 * NFFN)
            step(dve.memset(prob, -1.0))
            step(dve.tensor_copy(iota6, iota_bf[0:RB, 0:NX]))
            fchain = Chain(dve, ffn_chain)
            fstep = fchain.step
            FSTEPS = (10, 1, 13 + NX)

            def piece(p, t, u):
                xrow, x1 = xbuf[0:RB, u, :, :], rbuf[0:RB, u, :, :]
                base = t * sum(FSTEPS)
                if p == 1:
                    fchain.begin(base)
                    dve.wait_ge(f_x_in[u], 16 * (half(t, u) + 1))
                    wait(dve, x_turned, t)
                    hold(dve)
                    for b in range(BPC):
                        at = t * BPC + b
                        last = dve.tensor_scalar(trow[:, b, :], xrow[:, b, :], ln_mean[:, bass.ds(at, 1)],
                                                 ln_rstd[:, bass.ds(at, 1)], ALU.subtract, ALU.mult)
                    fstep(last)
                    dve.wait_ge(z_turned, t + 1)
                    rows = ps[0:RB, 6:8, :].rearrange("p a (b f) -> p (a b) f", b=2)
                    fstep(dve.tensor_tensor(trow, rows, trow, ALU.add))
                    wait(dve, f_out[u], 16 * half(t, u))
                    hold(dve)
                    fstep(dve.scalar_tensor_tensor(out=x1, in0=trow, scalar=0.0, in1=xrow, op0=ALU.max, op1=ALU.add))
                    for b in range(BPC):
                        last = dve.bn_stats(st4[:, b, :], x1[:, b, :])
                    fstep(last)
                    mean_var(st4, sum4, dif4, m24, mean4, var4, fstep).then_inc(var_done, 1)
                    assert fchain.n == FSTEPS[0]
                elif p == 2:
                    fchain.begin(base + FSTEPS[0])
                    dve.wait_ge(sd_done, t + 1)
                    fstep(dve.reciprocal(rstd4, sd4))
                    for b in range(BPC):
                        last = dve.tensor_scalar(trow[:, b, :], x1[:, b, :], mean4[:, b:b + 1], rstd4[:, b:b + 1],
                                                 ALU.subtract, ALU.mult)
                    last.then_inc(xf_done, 1)
                elif p == 5:
                    fchain.begin(base + FSTEPS[0] + FSTEPS[1])

                    def over(a):
                        return a.to_broadcast([RB, BPC, NX])

                    dve.wait_ge(lg_mm, t + 1)
                    logits = ps[0:RB, 7, 0:BPC * 8].rearrange("p (b n) -> p b n", b=BPC)[:, :, 0:NX]
                    dve.tensor_tensor(lg, logits, rb2_sb.unsqueeze(1).to_broadcast([RB, BPC, NX]), ALU.add).then_inc(lg_done, 1)
                    dve.wait_ge(lg_done, t + 1)
                    fstep(dve.tensor_reduce(lmax.rearrange("p b o -> p (b o)"), lg, AX.X, ALU.max))
                    dve.tensor_tensor(lg, lg, over(lmax), ALU.subtract).then_inc(sh_done, 1)
                    dve.wait_ge(ex_done, t + 1)
                    fstep(dve.tensor_reduce(lsum.rearrange("p b o -> p (b o)"), ex, AX.X, ALU.add))
                    fstep(dve.reciprocal(lrec, lsum))
                    fstep(dve.tensor_tensor(prob[:, :, 0:NX], ex, over(lrec), ALU.mult))
                    hold(dve)
                    for b in range(BPC):
                        last = dve.max(top8[:, b, :], prob[:, b, :])
                    fstep(last)
                    hold(dve)
                    for b in range(BPC):
                        last = dve.max_index(idx8[:, b, :], top8[:, b, :], prob[:, b, :])
                    fstep(last)
                    fstep(dve.tensor_copy(idxf, idx8))
                    dve.tensor_tensor(gap, top8[:, :, 1:2], top8[:, :, 0:1], ALU.subtract).then_inc(gap_done, 1)
                    dve.wait_ge(e2_done, t + 1)
                    fstep(dve.tensor_scalar(den, e2, 1.0, None, ALU.add))
                    fstep(dve.reciprocal(w1st, den))
                    fstep(dve.tensor_tensor(w2nd, e2, w1st, ALU.mult))
                    which = iota6.unsqueeze(1).to_broadcast([RB, BPC, NX])
                    dve.tensor_tensor(m1st, which, over(idxf[:, :, 0:1]), ALU.is_equal)
                    fstep(dve.tensor_tensor(m2nd, which, over(idxf[:, :, 1:2]), ALU.is_equal))
                    dve.tensor_tensor(m1st, m1st, over(w1st), ALU.mult)
                    fstep(dve.tensor_tensor(m2nd, m2nd, over(w2nd), ALU.mult))
                    wv = wsel[:, u, :].rearrange("p (b e) -> p b e", e=NX)
                    fstep(dve.tensor_tensor(wv, m1st, m2nd, ALU.add))
                    for e in range(NX):
                        for b in range(BPC):
                            last = dve.scalar_tensor_tensor(out=x1[:, b, :], in0=b3_bc[:, e, :], scalar=wv[:, b, e:e + 1],
                                                            in1=x1[:, b, :], op0=ALU.mult, op1=ALU.add)
                        fstep(last)
                    assert fchain.n == FSTEPS[2], fchain.n

            def hidden(layer, t, e):
                q = t * NX + e
                done, free, hT, bias, out_sem, bank = (
                    (l1_done, (l2_done, 2 * q - 2), h1T, eb1_sb, h1_dve, 1),
                    (l2_done, (l3_done, q - 1), h2T, eb2_sb, h2_dve, 3))[layer]
                wait(dve, *free)
                dve.wait_ge(done, 2 * q + 2)
                dve.tensor_scalar(hT[e % 2][:, 1, :], ps[:, bank, 0:CH], bias[:, e, 1:2], 0.0, ALU.add, ALU.max).then_inc(out_sem, 1)

            def combine(t, u, e):
                q = t * NX + e
                wv = wsel[:, u, :].rearrange("p (b e) -> p b e", e=NX)
                dve.wait_ge(l3_done, q + 1)
                wait(dve, combined, q)
                for b in range(BPC):
                    row = rbuf[0:RB, u, b, :]
                    last = dve.scalar_tensor_tensor(out=row, in0=ps[0:RB, 4 + b // 2, (b % 2) * D:(b % 2 + 1) * D],
                                                    scalar=wv[:, b, e:e + 1], in1=row, op0=ALU.mult, op1=ALU.add)
                last.then_inc(combined, 1)

            def experts(t, u, more):
                for e in range(NX):
                    if e == 0:
                        hidden(0, t, 0)
                    hidden(1, t, e)
                    if e + 1 < NX:
                        hidden(0, t, e + 1)
                    combine(t, u, e)
                    if more:
                        piece(e, t + 1, 1 - u)

            for p in range(6):
                piece(p, 0, 0)
            in_pairs(dve, lambda t, u: experts(t, u, True), PAIRS - 1)
            experts(NCH - 2, 0, True)
            experts(NCH - 1, 1, False)

        @block.tensor
        def _(pe):
            def turn(out, in_, last_sem=None):
                n = in_.shape[0]
                return pe.transpose(out, in_, ident[0:n, 0:n])

            def turn_table(table, bank):
                for n in range(NT):
                    for j in range(CPG):
                        last = turn(ps[:, bank + n, j * P:(j + 1) * P], table[:, n, j * P:(j + 1) * P])
                return last

            pe.wait_ge(ident_ready, 2)
            pe.wait_ge(edges_ready, 1)
            turn_table(dst_f, 0)
            turn_table(src_f, NT).then_inc(dst_turned, 1)
            pe.wait_ge(rel_ready, 1)
            pe.wait_ge(dst_kept, 1)
            turn_table(dst_f, 0).then_inc(tables_turned, 1)

            pe.wait_ge(src_kept, 1)

            def deg_product(d, u, first=False, final=False):
                pe.wait_ge(deg_onehot, d + 1)
                for j in range(DCH):
                    last = pe.matmul(ps[0:NHI, NT, 0:P], oh_hi[u][:, :, j], oh_lo[u][:, :, j],
                                     start=first and j == 0, stop=final and j == DCH - 1)
                last.then_inc(deg_summed, 1)

            for u in range(2):
                deg_product(u, u, first=u == 0)
            with pe.Fori(1, DSTEPS // 2 - 1) as i:
                for u in range(2):
                    deg_product(i * 2 + u, u)
            for u in range(2):
                deg_product(DSTEPS - 2 + u, u, final=u == 1)

            pe.wait_ge(flag_ready, 1)
            pe.wait_ge(tables_ready, 1)
            bad = pe.value_load(bad_int[0:1, 0:1], min_val=0, max_val=1)

            def aggregate(run):
                done = run * GATHERS

                def product(u, ohu, j, s, width):
                    for k in range(KH):
                        for n in range(PARTS):
                            last = pe.matmul(ps[:, 2 * u + k, 0:width], slots[:, s, n * D + k * P:n * D + (k + 1) * P],
                                             onehot[:, ohu, j, 0:width], start=j == 0 and n == 0,
                                             stop=j == CPG - 1 and n == PARTS - 1)
                    return last

                def landed(s, use):
                    pe.wait_ge(got[s], 16 * (use + done // SLOTS + 1))

                def fast(i, q):
                    g, u = i * 4 + q, q % 2
                    pe.wait_ge(oh_fast[run], g + 1)
                    wait(pe, ev_fast[run], g - 1)
                    for j in range(CPG):
                        s = (q * CPG + j) % SLOTS
                        landed(s, i * 2 + (q * CPG + j) // SLOTS)
                        product(u, u, j, s, WIN).then_inc(chunks_used, 1)

                def general(i, u):
                    g = i * 2 + u

                    for j in range(CPG):
                        landed(u * CPG + j, i)
                    hold(pe)
                    with pe.Fori(0, NW) as k:
                        s = g * NW + k
                        pe.wait_ge(oh_gen[run], s + 1)
                        pe.wait_ge(ev_gen[run], s + 1)
                        for j in range(CPG):
                            last = product(0, 0, j, u * CPG + j, GWIN)
                        last.then_inc(mm_gen[run], 1)

                with pe.If(bad == 0):
                    for q in range(4):
                        fast(0, q)
                    with pe.Fori(1, NG // 4) as i:
                        for q in range(4):
                            fast(i, q)
                with pe.Else():
                    with pe.Fori(0, NG // 2) as i:
                        for u in range(2):
                            general(i, u)

            pe.wait_ge(dn_in, 32)
            turn(ps[0:RB, 7, 0:NBLK], dn[:, :]).then_inc(dn_turned, 1)

            def v_turn(t, u):
                pe.wait_ge(v_ready, t + 1)
                wait(pe, v_kept, t - 1)
                for b in range(BPC):
                    for k in range(KH):
                        last = turn(ps[:, 2 * u + k, b * RB:(b + 1) * RB], xbuf[0:RB, u, b, k * P:(k + 1) * P])
                last.then_inc(v_turned, 1)

            in_pairs(pe, v_turn)

            def linear(layer):
                pe.wait_ge(agg_done, layer + 1)

                def lin(t, u):
                    wait(pe, lin_scaled[layer], t - 1)
                    for m in range(KH):
                        for k in range(KH):
                            last = pe.matmul(ps[:, 2 * u + m, 0:CH], wconv[:, layer, k, m * P:(m + 1) * P],
                                             acc[:, k, bass.ds(t * CH, CH)], start=k == 0, stop=k == KH - 1)
                    last.then_inc(lin_done[layer], 1)

                in_pairs(pe, lin)

            pe.wait_ge(consts_in, 16 * NCONST)
            pe.wait_ge(v_kept, NCH)
            aggregate(L1)
            linear(0)

            def y_turn(t, u):
                pe.wait_ge(y_ready, t + 1)
                wait(pe, r1_done[1], t - 1)
                for b in range(BPC):
                    for k in range(KH):
                        at = (b % 2) * D + k * P
                        last = turn(ps[0:RB, 2 * u + b // 2, at:at + P], ybuf[u][:, k, b * RB:(b + 1) * RB])
                last.then_inc(y_turned, 1)

            in_pairs(pe, y_turn)
            pe.wait_ge(r1_done[1], NCH)
            aggregate(L2)
            linear(1)
            pe.wait_ge(ffn_in, 16 * NFFN)

            def piece(p, t, u):
                if p == 1:
                    pe.wait_ge(zb_done, t + 1)
                    wait(pe, lg_done, t)
                    for b in range(BPC):
                        for k in range(KH):
                            at = (b % 2) * D + k * P
                            last = turn(ps[0:RB, 6 + b // 2, at:at + P], zb[:, k, b * RB:(b + 1) * RB])
                    last.then_inc(z_turned, 1)
                elif p == 3:
                    pe.wait_ge(xf_done, t + 1)
                    for b in range(BPC):
                        for k in range(KH):
                            last = turn(ps[:, 6 + k, b * RB:(b + 1) * RB], trow[:, b, k * P:(k + 1) * P])
                    last.then_inc(x_turned, 1)
                elif p == 4:
                    pe.wait_ge(xfT_done, t + 1)
                    for k in range(KH):
                        last = pe.matmul(ps[:, 6, 0:CH], rw1_sb[:, k, :], xfT[u][:, k, :], start=k == 0, stop=k == KH - 1)
                    last.then_inc(rh_done, 1)
                elif p == 5:
                    pe.wait_ge(rhT_done, t + 1)
                    for b in range(BPC):
                        last = pe.matmul(ps[0:RB, 7, b * 8:b * 8 + NX], rhT[:, b * RB:(b + 1) * RB], rw2_sb,
                                         start=True, stop=True)
                    last.then_inc(lg_mm, 1)

            def hidden(layer, t, u, e):
                q = t * NX + e
                if layer == 0:
                    pe.wait_ge(xfT_done, t + 1)
                    rhs, done, free, bank = xfT[u], l1_done, (h1_act, h1_dve), 0
                else:
                    pe.wait_ge(h1_act, q + 1)
                    pe.wait_ge(h1_dve, q + 1)
                    rhs, done, free, bank = h1T[e % 2], l2_done, (h2_act, h2_dve), 2
                for f in free:
                    wait(pe, f, q)
                for m in range(KH):
                    for k in range(KH):
                        last = pe.matmul(ps[:, bank + m, 0:CH], wx[:, layer, e, k, m * P:(m + 1) * P], rhs[:, k, :],
                                         start=k == 0, stop=k == KH - 1)
                    last.then_inc(done, 1)

            def rows_out(t, e):
                q = t * NX + e
                pe.wait_ge(h2_act, q + 1)
                pe.wait_ge(h2_dve, q + 1)
                wait(pe, combined, q)
                for b in range(BPC):
                    for k in range(KH):
                        last = pe.matmul(ps[0:RB, 4 + b // 2, (b % 2) * D:(b % 2 + 1) * D], h2T[e % 2][:, k, b * RB:(b + 1) * RB],
                                         wx[:, 2, e, k, :], start=k == 0, stop=k == KH - 1)
                last.then_inc(l3_done, 1)

            def experts(t, u, more):
                for e in range(NX):
                    if e == 0:
                        hidden(0, t, u, 0)
                    hidden(1, t, u, e)
                    if e + 1 < NX:
                        hidden(0, t, u, e + 1)
                    rows_out(t, e)
                    if more:
                        piece(e, t + 1, 1 - u)

            for p in range(6):
                piece(p, 0, 0)
            in_pairs(pe, lambda t, u: experts(t, u, True), PAIRS - 1)
            experts(NCH - 2, 0, True)
            experts(NCH - 1, 1, False)


_INS = ["x", "src", "dst", "L0_gnn_W1", "L0_gnn_b1", "L0_gnn_W2", "L0_gnn_b2", "L0_gnn_gamma1", "L0_gnn_beta1",
        "L0_gnn_gamma2", "L0_gnn_beta2", "L0_ffn_router_w1", "L0_ffn_router_b1", "L0_ffn_router_w2", "L0_ffn_router_b2",
        "L0_ffn_expert_w1", "L0_ffn_expert_b1", "L0_ffn_expert_w2", "L0_ffn_expert_b2", "L0_ffn_expert_w3", "L0_ffn_expert_b3"]


def kernel(**inputs):
    import numpy as _np
    import concourse.bacc as _bacc
    from concourse import mybir as _mybir
    from concourse.bass_utils import run_bass_kernel_spmd as _run

    nc = _bacc.Bacc("TRN2", target_bir_lowering=False, num_devices=1)
    n_nodes, n_edges = inputs["x"].shape[0], inputs["src"].shape[0]
    n_chunks, _, n_tables = sizes(n_nodes, n_edges)
    pads = {"x": (n_chunks * CH, 0), "src": (n_tables * P * GE, 0), "dst": (n_tables * P * GE, -1)}
    arrays, args = {}, []
    for name in _INS:
        a = _np.ascontiguousarray(inputs[name])
        if name in pads:
            rows, fill = pads[name]
            padded = _np.full((rows,) + a.shape[1:], fill, a.dtype)
            padded[:a.shape[0]] = a
            a = padded
        arrays[f"in_{name}_dram"] = a
        args.append(nc.dram_tensor(f"in_{name}_dram", a.shape, _mybir.dt.from_np(a.dtype), kind="ExternalInput").ap())
    shape = (n_chunks * CH, inputs["x"].shape[1])
    args.append(nc.dram_tensor("out_0_dram", shape, _mybir.dt.float32, kind="ExternalOutput").ap())
    gnn_moe(nc, n_nodes, n_edges, *args)
    r = _run(nc, [arrays], core_ids=[0])
    return r.results[0]["out_0_dram"][:n_nodes]
```

```python
from contextlib import ExitStack

import numpy as np

import concourse.bass as bass
from concourse import mybir

F32 = mybir.dt.float32
BF16 = mybir.dt.bfloat16
I32 = mybir.dt.int32
U32 = mybir.dt.uint32
ALU = mybir.AluOpType
ACT = mybir.ActivationFunctionType
AX = mybir.AxisListType
RMAX = bass.bass_isa.ReduceOp.max

P = 128
RB = 112
BPC = 4
CH = RB * BPC
EC = P
CPG = 4
GE = EC * CPG
WIN = 64
GWIN = 256
DCH = 16
TB = 4
TOK = P * TB
SLOTS = 8
BIG = float(1 << 20)
EPS = 1e-5


def sizes(n_nodes, n_edges):
    n_chunks = -(-n_nodes // CH)
    n_chunks += -n_chunks % 4
    n_groups = -(-n_edges // GE)
    n_groups += -n_groups % 8
    n_tables = -(-(n_groups + 4) // P)
    return n_chunks, n_groups, n_tables


def wait(eng, sem, value):
    if not isinstance(value, int) or value > 0:
        eng.wait_ge(sem, value)


def hold(eng):
    eng.nop(nofuse=True)


class Chain:

    def __init__(self, eng, sem):
        self.eng, self.sem, self.base, self.n = eng, sem, 0, 0

    def begin(self, base):
        self.base, self.n = base, 0

    def step(self, instruction):
        self.n += 1
        instruction.then_inc(self.sem, 1)
        self.eng.wait_ge(self.sem, self.base + self.n)


def gnn_moe(nc, N, E, x, src, dst, W1, b1, W2, b2, gamma1, beta1, gamma2, beta2,
            rw1, rb1, rw2, rb2, ew1, eb1, ew2, eb2, ew3, eb3, out):
    D = x.shape[1]
    KH = D // P
    NX = ew1.shape[0]
    NCH, NG, NT = sizes(N, E)
    NPAD = NCH * CH
    NBLK = NCH * BPC
    NW = -(-NPAD // GWIN)
    WIDTH = max(NPAD, NW * GWIN)
    WMAX = NPAD - WIN
    TG = min(NT * P, NG + 32)
    TAIL = N - (NCH - 1) * CH
    PAIRS = NCH // 2
    PARTS = 3
    NHI = NPAD // P
    DSTEPS = NG * CPG // DCH
    DPER = DSTEPS // NCH
    ROW = D + 4
    XR = NPAD + TOK
    TILES = (2 * NPAD + NX * (TOK - 1)) // TOK
    TILES += TILES % 2
    LEVELS = -(-NPAD // TOK)
    assert D == 256 and NPAD % P == 0 and NHI <= P and NBLK <= P and NT <= 4 and 0 < TAIL <= CH and rw1.shape[1] == P and TILES <= GWIN

    t_dram = [nc.dram_tensor(f"messages_{n}", (NPAD, PARTS * D), BF16, kind="Internal").ap() for n in (1, 2)]
    routed = nc.dram_tensor("routed_rows", (NX * XR + TOK, ROW), F32, kind="Internal").ap()
    w_dram = nc.dram_tensor("window_starts", (NT * P,), I32, kind="Internal").ap()
    dinv_dram = nc.dram_tensor("dinv_row", (NPAD,), F32, kind="Internal").ap()

    with ExitStack() as ctx:
        def sb(name, shape, dt=F32):
            return ctx.enter_context(nc.sbuf_tensor(name, shape, dt))

        def sem(name):
            return ctx.enter_context(nc.semaphore(name))

        def sems(name, n):
            return [sem(f"{name}{i}") for i in range(n)]

        acc = sb("acc", [P, KH, WIDTH])
        dinvT = sb("dinvT", [P, WIDTH])
        tables = sb("tables", [P, 2 * max(TG * CPG, KH * 2 * CH)])
        relT = tables[:, 0:TG * CPG]
        srcT = tables[:, TG * CPG:2 * TG * CPG]
        ring = sb("ring", [P, SLOTS * PARTS * D // 2])
        onehot_mem = sb("onehot_mem", [P, 2 * CPG * GWIN // 2])
        xbuf = sb("xbuf", [P, 2, BPC, D])
        rbuf = sb("rbuf", [P, 2, BPC, D])
        wconv = sb("wconv", [P, 2, KH, D])
        vec = sb("vec", [P, 6, KH])
        ident = sb("ident", [P, P])
        iota_bf = sb("iota_bf", [P, GWIN], BF16)
        idx_stage = sb("idx_stage", [P, 2, SLOTS], I32)
        relk = sb("relk", [P, CPG])
        wrow = sb("wrow", [1, NT * P], I32)
        bnst = sb("bnst", [P, KH, NCH, 6])
        lnst = sb("lnst", [RB, NBLK, 6])
        ln_mean = sb("ln_mean", [RB, NBLK])
        ln_rstd = sb("ln_rstd", [RB, NBLK])
        ln_tmp = sb("ln_tmp", [RB, 3, NBLK])
        dcol = sb("dcol", [RB, NBLK])
        dn = sb("dn", [NBLK, RB])
        wlo = sb("wlo", [P, NT])
        whi = sb("whi", [P, NT])
        w_int = sb("w_int", [P, NT], I32)
        flags = sb("flags", [P, 4])
        bad_int = sb("bad_int", [P, 1], I32)
        bn_mv = sb("bn_mv", [P, KH, 2])
        bn_sc = sb("bn_sc", [P, 4, KH])
        marker = sb("marker", [P, 2, 5])
        ps = ctx.enter_context(nc.psum_tensor("ps", [P, 8, 512], F32))

        accflat = acc[:, :, :].rearrange("p k n -> p (k n)")
        TE = NT * GE
        dst_i = accflat[:, 0:TE].bitcast(I32).rearrange("p (t e) -> p t e", t=NT)
        src_i = accflat[:, TE:2 * TE].bitcast(I32).rearrange("p (t e) -> p t e", t=NT)
        dst_f = accflat[:, 2 * TE:3 * TE].rearrange("p (t e) -> p t e", t=NT)
        src_f = accflat[:, 3 * TE:4 * TE].rearrange("p (t e) -> p t e", t=NT)
        tmp_f = accflat[:, 4 * TE:5 * TE].rearrange("p (t e) -> p t e", t=NT)
        iota_i = accflat[:, 5 * TE:5 * TE + GWIN].bitcast(I32)
        lent = [5 * TE + GWIN]

        def lend(n_bytes):
            a = accflat[:, lent[0]:lent[0] + n_bytes // 4]
            lent[0] += n_bytes // 4
            assert lent[0] <= KH * WIDTH
            return a

        dstT_i, digit_i = lend(4 * TG * CPG).bitcast(I32), lend(4 * TG * CPG).bitcast(I32)
        loT, hiT = lend(2 * TG * CPG).bitcast(BF16), lend(2 * TG * CPG).bitcast(BF16)
        iota_rep = lend(2 * P * DCH).bitcast(BF16).rearrange("p (w j) -> p w j", j=DCH)
        oh_lo = [lend(2 * P * DCH).bitcast(BF16).rearrange("p (w j) -> p w j", j=DCH) for _ in range(2)]
        oh_hi = [lend(2 * NHI * DCH).bitcast(BF16).rearrange("p (w j) -> p w j", j=DCH) for _ in range(2)]
        rel3 = relT.rearrange("p (g j) -> p g j", j=CPG)
        src3 = srcT.bitcast(I32).rearrange("p (g j) -> p g j", j=CPG)
        srcidx = srcT.bitcast(I32)
        dg = ring[0:NHI, 0:P]
        ring_bf = ring[:, :].bitcast(BF16)
        slots = ring_bf.rearrange("p (s f) -> p s f", s=SLOTS)
        split = ring_bf.rearrange("p (u b f) -> p u b f", u=2, b=BPC)
        onehot = onehot_mem[:, :].bitcast(BF16).rearrange("p (u j w) -> p u j w", u=2, j=CPG)
        lin_tmp = [rbuf[:, u, :, :].rearrange("p b f -> p (b f)")[:, 0:KH * CH].rearrange("p (k n) -> p k n", k=KH)
                   for u in range(2)]
        ybuf = [xbuf[:, u, :, :].rearrange("p b f -> p (b f)")[:, 0:KH * CH].rearrange("p (k n) -> p k n", k=KH)
                for u in range(2)]
        class Region:

            def __init__(self, mem, start=0):
                self.mem, self.at = mem, start

            def take(self, parts, *shape):
                n = int(np.prod(shape))
                a = self.mem[0:parts, self.at:self.at + n]
                self.at += n
                assert self.at <= self.mem.shape[1]
                if len(shape) == 1:
                    return a
                names = "abcd"[:len(shape)]
                return a.rearrange(f"p ({' '.join(names)}) -> p {' '.join(names)}", **dict(zip(names, shape)))

        B2 = 2 * BPC
        EA, EB = 2 * KH * D + 2 * KH + 1, KH * D + D
        old_dinv = Region(dinvT)
        wx = old_dinv.take(P, NX, EA + EB)
        rhT = old_dinv.take(P, CH)
        rw1_sb = old_dinv.take(P, KH, P)
        rw2_sb, rb1_sb, rb2_sb = old_dinv.take(P, NX), old_dinv.take(P, 1), old_dinv.take(RB, NX)
        iota6, region_start = old_dinv.take(RB, NX), old_dinv.take(RB, NX)
        tri_bf = old_dinv.take(RB, RB // 2).bitcast(BF16)
        ones_bf = old_dinv.take(RB, P // 2).bitcast(BF16)
        st4 = [old_dinv.take(RB, BPC, 6) for _ in range(2)]
        sum4, dif4, m24, mean4, var4, sd4, rstd4 = [[old_dinv.take(RB, BPC) for _ in range(2)] for _ in range(7)]
        lg, ex, prob, eq, cand, m1st, m2nd, rest, pos, at1, at2 = [old_dinv.take(RB, B2, NX) for _ in range(11)]
        lmax, lsum, lrec, pmax, which1, pmax2, which2, gap, e2, den = [old_dinv.take(RB, B2, 1) for _ in range(10)]
        node_ids, addr1, addr2 = old_dinv.take(RB, B2), old_dinv.take(RB, B2), old_dinv.take(RB, B2)
        mb_bf = old_dinv.take(RB, B2 * NX // 2).bitcast(BF16).rearrange("p (b e) -> p b e", e=NX)
        run_bf = old_dinv.take(RB, NX // 2).bitcast(BF16)
        run_add = old_dinv.take(RB, NX)
        old_ring, old_tables = Region(ring), Region(tables)
        xrow = [old_ring.take(RB, B2, ROW), old_tables.take(RB, B2, ROW)]
        zb, xfT = old_ring.take(P, KH, CH), old_tables.take(P, KH, CH)
        tri_f = old_tables.take(RB, RB)
        iota_pb = old_tables.take(P, B2).bitcast(I32)
        addr_int = old_tables.take(RB, 2, 2, B2).bitcast(I32)
        trow = onehot_mem[0:RB, 0:BPC * D].rearrange("p (b f) -> p b f", b=BPC)
        old_acc = Region(accflat)
        we = [old_acc.take(P, EA + EB) for _ in range(2)]
        tile_rows = [old_acc.take(P, TB, ROW) for _ in range(2)]
        xT, h1T, h2T = [old_acc.take(P, KH, TOK) for _ in range(3)]
        yrow = [old_acc.take(P, TB, D) for _ in range(2)]
        fill = old_acc.take(P, TB, ROW)
        out_idx, wsel, wsel2 = old_acc.take(P, 2, TB).bitcast(I32), old_acc.take(P, 2, TB), old_acc.take(P, 2, TB)
        count, n_tiles, last_tile, skip = [old_acc.take(1, NX) for _ in range(4)]
        levels = old_acc.take(1, LEVELS)
        reached = old_acc.take(1, NX, LEVELS)
        behind, jump = old_acc.take(1, TILES, NX), old_acc.take(1, TILES, NX)
        tile_no, tile_e, tile_at = [old_acc.take(1, TILES) for _ in range(3)]
        tail_int, tile_e_int, tile_at_int = old_acc.take(1, NX).bitcast(I32), old_acc.take(1, TILES).bitcast(I32), old_acc.take(1, TILES).bitcast(I32)

        def w_of(u, m, k, n0, n1):
            at = (0, KH * D, EA)[m] + k * D
            return we[u][:, at + n0:at + n1]

        edges_in, consts_in, w_row, dn_in, ffn_in = sem("edges_in"), sem("consts_in"), sem("w_row"), sem("dn_in"), sem("ffn_in")
        ident_ready, iota_ready, iota_bf_ready = sem("ident_ready"), sem("iota_ready"), sem("iota_bf_ready")
        span_ready, span_all, flag_ready, w_ready = sem("span_ready"), sem("span_all"), sem("flag_ready"), sem("w_ready")
        edges_ready, dst_turned, dst_kept = sem("edges_ready"), sem("dst_turned"), sem("dst_kept")
        rel_ready, tables_turned, tables_ready, src_kept = sem("rel_ready"), sem("tables_turned"), sem("tables_ready"), sem("src_kept")
        sqrt_done, dinv_in = sem("sqrt_done"), sem("dinv_in")
        deg_onehot, deg_summed, deg_done, dinv_ready = sem("deg_onehot"), sem("deg_summed"), sem("deg_done"), sem("dinv_ready")
        dn_turned, ln_var, ln_sd = sem("dn_turned"), sem("ln_var"), sem("ln_sd")
        stat_x_in, stats_done = sems("stat_x_in", 2), sem("stats_done")
        dve_chain = sem("dve_chain")
        got = sems("got", SLOTS)
        stage_ready, chunks_used = sem("stage_ready"), sem("chunks_used")
        oh_fast, ev_fast = sems("oh_fast", 2), sems("ev_fast", 2)
        oh_gen, mm_gen, ev_gen, rk_gen = sems("oh_gen", 2), sems("mm_gen", 2), sems("ev_gen", 2), sems("rk_gen", 2)
        agg_done = sem("agg_done")
        v_x_in = sems("v_x_in", 2)
        v_ready, v_turned, v_kept = sem("v_ready"), sem("v_turned"), sem("v_kept")
        hi_done, r1_done, mid_done, lo_done = sems("hi_done", 2), sems("r1_done", 2), sems("mid_done", 2), sems("lo_done", 2)
        stored = [sems("stored1_", 2), sems("stored2_", 2)]
        lin_done, lin_scaled, lin_biased = sems("lin_done", 2), sems("lin_scaled", 2), sems("lin_biased", 2)
        bn_var, bn_sd, bn_ready = sem("bn_var"), sem("bn_sd"), sem("bn_ready")
        relu_done, y_ready, y_kept, y_turned = sem("relu_done"), sem("y_ready"), sem("y_kept"), sem("y_turned")
        f_x_in, x1_out = sems("f_x_in", 2), sems("x1_out", 2)
        zb_done, z_turned, z_added, x1_done = sem("zb_done"), sem("z_turned"), sem("z_added"), sem("x1_done")
        var_done, sd_done, xf_done, x_turned, xfT_done = sem("var_done"), sem("sd_done"), sem("xf_done"), sem("x_turned"), sem("xfT_done")
        rh_done, rhT_done, lg_mm, lg_read = sem("rh_done"), sem("rhT_done"), sem("lg_mm"), sem("lg_read")
        sh_done, ex_done, gap_done, e2_done = sem("sh_done"), sem("ex_done"), sem("gap_done"), sem("e2_done")
        x1_chain, xf_chain, route_chain = sem("x1_chain"), sem("xf_chain"), sem("route_chain")
        mb_ready, ranked, run_ready, rows_ready = sem("mb_ready"), sem("ranked"), sem("run_ready"), sem("rows_ready")
        routed_out = sems("routed_out", 2)
        masks_made, ones_made, counted, fill_ready, filled = sem("masks_made"), sem("ones_made"), sem("counted"), sem("fill_ready"), sem("filled")
        tiles_known, rows_in = sem("tiles_known"), sems("rows_in", 2)
        tile_turned, xT_done, expert_a, expert_b = sem("tile_turned"), sem("xT_done"), sem("expert_a"), sem("expert_b")
        l1_done, l2_done, l3_done = sem("l1_done"), sem("l2_done"), sem("l3_done")
        h1_act, h1_dve, h2_act, h2_dve = sem("h1_act"), sem("h1_dve"), sem("h2_act"), sem("h2_dve")
        y_biased, y_weighted, ids_ready, added = sem("y_biased"), sem("y_weighted"), sem("ids_ready"), sems("added", 2)

        NCONST = 2 + 6
        NFFN = 4 * NX + 4 + 2 * KH
        GATHERS = NG * CPG
        L1, L2 = 0, 1

        def nodes(ap, t):
            return ap[bass.ds(t * CH, CH), :].rearrange("(b p) f -> p b f", p=RB)

        def in_pairs(eng, body, last=PAIRS):
            for u in range(2):
                body(u, u)
            if last > 1:
                with eng.Fori(1, last) as i:
                    for u in range(2):
                        body(i * 2 + u, u)

        def half(t, u):
            return (t - u) // 2 if isinstance(t, int) else t // 2

        def routing(eng, body):
            body(-1, 1, True)
            body(0, 0, True)
            if PAIRS > 2:
                with eng.Fori(1, PAIRS // 2) as j:
                    body(j * 2 - 1, 1, True)
                    body(j * 2, 0, True)
            body(PAIRS - 1, 1, False)

        def tiles(eng, body):
            for u in range(2):
                body(u, u, TILES > u + 1, TILES > u + 2)
            if TILES > 4:
                with eng.Fori(1, TILES // 2 - 1) as i:
                    for u in range(2):
                        body(i * 2 + u, u, True, True)
            body(TILES - 2, 0, True, False)
            body(TILES - 1, 1, False, False)

        block = ctx.enter_context(nc.Block())

        @block.sync
        def _(sp):
            sp.dma_start(dst_i, dst.rearrange("(t q e) -> q t e", q=P, e=GE)).then_inc(edges_in, 16)
            sp.dma_start(src_i, src.rearrange("(t q e) -> q t e", q=P, e=GE)).then_inc(edges_in, 16)
            for n, w in enumerate((W1, W2)):
                sp.dma_start(wconv[:, n, :, :], w.rearrange("(k p) n -> p k n", p=P)).then_inc(consts_in, 16)
            with nc.allow_non_contiguous_dma(reason="small vectors, one feature a partition"):
                for n, v in enumerate((b1, gamma1, beta1, b2, gamma2, beta2)):
                    sp.dma_start(vec[:, n, :], v.rearrange("(k p) -> p k", p=P)).then_inc(consts_in, 16)

            def stat_load(t, u):
                wait(sp, stats_done, t - 1)
                sp.dma_start(xbuf[0:RB, u, :, :], nodes(x, t)).then_inc(stat_x_in[u], 16)

            in_pairs(sp, stat_load)

            sp.wait_ge(w_ready, 1)
            with nc.allow_non_contiguous_dma(reason="one window start a partition"):
                sp.dma_start(w_dram.rearrange("(t q) -> q t", q=P), w_int[:, :]).then_inc(w_row, 16)
            sp.wait_ge(w_row, 16)
            sp.dma_start(wrow[:, :], w_dram.rearrange("(o n) -> o n", o=1)).then_inc(w_row, 16)

            sp.wait_ge(dinv_ready, 1)
            sp.dma_start(dinv_dram.rearrange("(h l) -> h l", l=P), dg[:, :]).then_inc(dn_in, 16)
            sp.wait_ge(dn_in, 16)
            sp.dma_start(dn[:, :], dinv_dram.rearrange("(n p) -> n p", p=RB)).then_inc(dn_in, 16)

            sp.wait_ge(stats_done, NCH)

            def v_load(t, u):
                wait(sp, v_turned, t - 1)
                wait(sp, r1_done[0], t - 1)
                sp.dma_start(xbuf[0:RB, u, :, :], nodes(x, t)).then_inc(v_x_in[u], 16)

            def store(layer, t, u):
                sp.wait_ge(lo_done[layer], t + 1)
                sp.dma_start(nodes(t_dram[layer], t), split[0:RB, u, :, :]).then_inc(stored[layer][u], 16)

            v_load(0, 0)
            v_load(1, 1)
            with sp.Fori(1, PAIRS) as i:
                for u in range(2):
                    store(0, i * 2 + u - 2, u)
                    v_load(i * 2 + u, u)
            for u in range(2):
                store(0, NCH - 2 + u, u)

            sp.dma_start(dinvT[:, 0:NPAD], dinv_dram.rearrange("(o n) -> o n", o=1).to_broadcast([P, NPAD])).then_inc(dinv_in, 16)

            in_pairs(sp, lambda t, u: store(1, t, u))

            sp.wait_ge(lin_scaled[1], NCH)
            with nc.allow_non_contiguous_dma(reason="small vectors, one feature a partition"):
                sp.dma_start(rw1_sb, rw1.rearrange("(k p) n -> p k n", p=P)).then_inc(ffn_in, 16)
                sp.dma_start(rb1_sb, rb1.rearrange("(p o) -> p o", o=1)).then_inc(ffn_in, 16)
                sp.dma_start(rw2_sb, rw2).then_inc(ffn_in, 16)
                sp.dma_start(rb2_sb, rb2.rearrange("(o n) -> o n", o=1).to_broadcast([RB, NX])).then_inc(ffn_in, 16)

            def x_load(t, u):
                wait(sp, x1_done, t - 1)
                sp.dma_start(xbuf[0:RB, u, :, :], nodes(x, t)).then_inc(f_x_in[u], 16)

            def x1_store(t, u):
                sp.wait_ge(x1_done, t + 1)
                sp.dma_start(nodes(out, t), rbuf[0:RB, u, :, :]).then_inc(x1_out[u], 16)

            x_load(0, 0)
            x_load(1, 1)
            for e in range(NX):
                for w, at in ((ew1, 0), (ew2, KH * D), (ew3, EA)):
                    sp.dma_start(wx[:, e, at:at + KH * D].rearrange("p (k n) -> p k n", k=KH),
                                 w[e, :, :].rearrange("(k p) n -> p k n", p=P)).then_inc(ffn_in, 16)
                sp.dma_start(wx[:, e, EA + KH * D:EA + EB], eb3[e:e + 1, :].to_broadcast([P, D])).then_inc(ffn_in, 16)
            with nc.allow_non_contiguous_dma(reason="small vectors, one feature a partition"):
                for b_d, at in ((eb1, 2 * KH * D), (eb2, 2 * KH * D + KH)):
                    for k in range(KH):
                        sp.dma_start(wx[:, :, at + k], b_d[:, k * P:(k + 1) * P].rearrange("e p -> p e")).then_inc(ffn_in, 16)
            with sp.Fori(1, PAIRS) as i:
                for u in range(2):
                    x1_store(i * 2 + u - 2, u)
                    x_load(i * 2 + u, u)
            for u in range(2):
                x1_store(NCH - 2 + u, u)

            sp.wait_ge(fill_ready, 1)
            for u in range(2):
                sp.wait_ge(routed_out[u], 16 * 2 * B2 * PAIRS // 2)
            whole = "(p b) f -> p (b f)"
            fill_flat = fill.rearrange("p b f -> p (b f)")
            sp.dma_start(out[NPAD:NPAD + P, :], fill[:, 0, 0:D]).then_inc(filled, 16)
            sp.dma_start(routed[NX * XR:NX * XR + TOK, :].rearrange(whole, b=TB), fill_flat).then_inc(filled, 16)
            sp.wait_ge(tiles_known, 1)
            for e in range(NX):
                tail = sp.value_load(tail_int[0:1, e:e + 1], min_val=e * XR, max_val=e * XR + NPAD)
                sp.dma_start(routed[bass.ds(tail, TOK), :].rearrange(whole, b=TB), fill_flat).then_inc(filled, 16)
            sp.wait_ge(filled, 16 * (NX + 2))

            def tile_load(s, u):
                wait(sp, tile_turned, s - 1)
                wait(sp, ids_ready, s - 1)
                hold(sp)
                at = sp.value_load(tile_at_int[0:1, bass.ds(s, 1)], min_val=0, max_val=NX * XR)
                sp.dma_start(tile_rows[u].rearrange("p b f -> p (b f)"),
                             routed[bass.ds(at, TOK), :].rearrange(whole, b=TB)).then_inc(rows_in[u], 16)

            in_pairs(sp, tile_load, TILES // 2)
            for u in range(2):
                sp.wait_ge(added[u], 16 * TB * TILES // 2)

        @block.gpsimd
        def _(pool):
            pool.memset(ident[:, :], 0.0).then_inc(ident_ready, 1)
            pool.iota(iota_i, pattern=[[1, GWIN]], base=0, channel_multiplier=0).then_inc(iota_ready, 1)
            pool.wait_ge(ident_ready, 1)
            pool.affine_select(out=ident[:, :], in_=ident[:, :], compare_op=ALU.not_equal, fill=1.0, base=0,
                               pattern=[[-1, P]], channel_multiplier=1).then_inc(ident_ready, 1)
            pool.wait_ge(span_ready, 1)
            pool.partition_all_reduce(flags[:, 1:2], flags[:, 0:1], P, RMAX).then_inc(span_all, 1)

            def gathers(layer):
                done = layer * GATHERS
                for u in range(2):
                    pool.wait_ge(stored[layer][u], 16 * PAIRS)

                def gather(i, u, first):
                    c0 = i * (2 * SLOTS) + u * SLOTS
                    pool.wait_ge(stage_ready, i * 2 + u + 1 + done // SLOTS)
                    for s in range(SLOTS):
                        wait(pool, chunks_used, c0 + s - SLOTS + 1 + done)
                        hold(pool)
                        pool.indirect_dma_start(
                            out=slots[:, s, :], out_offset=None, in_=t_dram[layer],
                            in_offset=bass.IndirectOffsetOnAxis(ap=idx_stage[:, u, s:s + 1], axis=0),
                        ).then_inc(got[s], 16)

                for u in range(2):
                    gather(0, u, True)
                if GATHERS > 2 * SLOTS:
                    with pool.Fori(1, GATHERS // (2 * SLOTS)) as i:
                        for u in range(2):
                            gather(i, u, False)

            gathers(L1)

            def keep_y(t, u):
                pool.wait_ge(y_ready, t + 1)
                hold(pool)
                pool.tensor_copy(acc[:, :, bass.ds(t * CH, CH)], ybuf[u]).then_inc(y_kept, 1)

            in_pairs(pool, keep_y)
            gathers(L2)

            pool.wait_ge(agg_done, 2)
            pool.iota(iota_pb, pattern=[[RB, B2]], base=0, channel_multiplier=1).then_inc(masks_made, 1)
            pool.memset(tri_f, 1.0).then_inc(masks_made, 1)
            pool.wait_ge(masks_made, 2)
            pool.affine_select(out=tri_f, in_=tri_f, compare_op=ALU.is_gt, fill=0.0, base=0, pattern=[[1, RB]],
                               channel_multiplier=-1).then_inc(masks_made, 1)

            def route(i, par):
                pool.wait_ge(rows_ready, i + 1)
                hold(pool)
                for c in range(2):
                    for b in range(B2):
                        pool.indirect_dma_start(
                            out=routed, out_offset=bass.IndirectOffsetOnAxis(ap=addr_int[:, par, c, b:b + 1], axis=0),
                            in_=xrow[par][:, b, :], in_offset=None).then_inc(routed_out[par], 16)

            in_pairs(pool, route, PAIRS // 2)

            for u in range(2):
                pool.wait_ge(x1_out[u], 16 * PAIRS)

            def add_rows(s, u):
                pool.wait_ge(y_weighted, s + 1)
                wait(pool, added[1 - u], 16 * TB * (half(s - 1, 1 - u) + 1) if not isinstance(s, int) or s > 0 else 0)
                hold(pool)
                for b in range(TB):
                    pool.indirect_dma_start(
                        out=out, out_offset=bass.IndirectOffsetOnAxis(ap=out_idx[:, u, b:b + 1], axis=0),
                        in_=yrow[u][:, b, :], in_offset=None, compute_op=ALU.add).then_inc(added[u], 16)
                    pool.wait_ge(added[u], 16 * TB * half(s, u) + 16 * b + 16)
                    hold(pool)

            in_pairs(pool, add_rows, TILES // 2)

        @block.scalar
        def _(act):
            act.wait_ge(dst_turned, 1)
            for n in range(NT):
                ng = min(P, TG - n * P)
                turned = ps[:, NT + n, :].rearrange("p (j g) -> p g j", j=CPG)
                last = act.activation(src3[:, n * P:n * P + ng, :], turned[:, 0:ng, :], ACT.Copy)
            last.then_inc(src_kept, 1)
            act.wait_ge(ln_var, 1)
            act.activation(ln_rstd[:, :], ln_tmp[:, 0, :], ACT.Sqrt).then_inc(ln_sd, 1)
            act.wait_ge(deg_done, 1)
            act.activation(dg[:, :], dg[:, :], ACT.Sqrt).then_inc(sqrt_done, 1)

            def split_rows(layer, t, u, rows):
                wait(act, stored[layer][u], 16 * half(t, u))
                hold(act)
                act.activation(split[0:RB, u, :, 0:D], rows, ACT.Copy).then_inc(hi_done[layer], 1)
                act.wait_ge(r1_done[layer], t + 1)
                hold(act)
                act.activation(split[0:RB, u, :, D:2 * D], rbuf[0:RB, u, :, :], ACT.Copy).then_inc(mid_done[layer], 1)

            def v_split(t, u):
                act.wait_ge(v_ready, t + 1)
                split_rows(0, t, u, xbuf[0:RB, u, :, :])
                act.wait_ge(v_turned, t + 1)
                hold(act)
                act.activation(acc[:, :, bass.ds(t * CH, CH)], ps[:, 2 * u:2 * u + KH, 0:CH], ACT.Copy).then_inc(v_kept, 1)

            in_pairs(act, v_split)

            def stage_indices(layer):
                done = layer * GATHERS

                def stage(i, u):
                    wait(act, chunks_used, (i - 1) * (2 * SLOTS) + u * SLOTS + SLOTS + done)
                    hold(act)
                    act.activation(idx_stage[:, u, :], srcidx[:, bass.ds(i * (2 * SLOTS) + u * SLOTS, SLOTS)],
                                   ACT.Copy).then_inc(stage_ready, 1)

                for u in range(2):
                    stage(0, u)
                if GATHERS > 2 * SLOTS:
                    with act.Fori(1, GATHERS // (2 * SLOTS)) as i:
                        for u in range(2):
                            stage(i, u)

            def linear_bias(layer):
                def add_bias(t, u):
                    act.wait_ge(lin_scaled[layer], t + 1)
                    hold(act)
                    for k in range(KH):
                        last = act.activation(acc[:, k, bass.ds(t * CH, CH)], lin_tmp[u][:, k, :], ACT.Identity,
                                              bias=vec[:, 3 * layer, k:k + 1])
                    last.then_inc(lin_biased[layer], 1)

                in_pairs(act, add_bias)
                act.wait_ge(bn_var, layer + 1)
                act.activation(bn_sc[:, 0, :], bn_sc[:, 1, :], ACT.Sqrt).then_inc(bn_sd, 1)

            act.wait_ge(src_kept, 1)
            act.wait_ge(consts_in, 16 * NCONST)
            stage_indices(L1)
            linear_bias(0)
            act.wait_ge(bn_ready, 1)

            def relu(t):
                for k in range(KH):
                    part = acc[:, k, bass.ds(t * CH, CH)]
                    last = act.activation(part, part, ACT.Relu, bias=bn_sc[:, 3, k:k + 1], scale=bn_sc[:, 2, k:k + 1])
                last.then_inc(relu_done, 1)

            def y_split(t, u):
                act.wait_ge(y_turned, t + 1)
                split_rows(1, t, u, ps[0:RB, 2 * u:2 * u + 2, :].rearrange("p a (b f) -> p (a b) f", b=2))

            relu(0)
            relu(1)
            y_split(0, 0)
            with act.Fori(1, PAIRS) as i:
                relu(i * 2)
                y_split(i * 2 - 1, 1)
                relu(i * 2 + 1)
                y_split(i * 2, 0)
            y_split(NCH - 1, 1)

            stage_indices(L2)
            linear_bias(1)
            act.wait_ge(bn_ready, 2)
            act.wait_ge(ffn_in, 16 * NFFN)

            def batch_norm2(t):
                wait(act, z_turned, t)
                hold(act)
                for k in range(KH):
                    last = act.activation(zb[:, k, :], acc[:, k, bass.ds(t * CH, CH)], ACT.Identity,
                                          bias=bn_sc[:, 3, k:k + 1], scale=bn_sc[:, 2, k:k + 1])
                last.then_inc(zb_done, 1)

            def root(t, u):
                act.wait_ge(var_done, t + 1)
                act.activation(sd4[u], var4[u], ACT.Sqrt).then_inc(sd_done, 1)

            def keep_xfT(t):
                wait(act, rh_done, t)
                act.wait_ge(x_turned, t + 1)
                hold(act)
                act.activation(xfT, ps[:, 2:2 + KH, 0:CH], ACT.Copy).then_inc(xfT_done, 1)

            def router_hidden(t):
                wait(act, lg_mm, t)
                act.wait_ge(rh_done, t + 1)
                hold(act)
                act.activation(rhT, ps[:, 4, 0:CH], ACT.Relu, bias=rb1_sb[:, 0:1]).then_inc(rhT_done, 1)

            def route(i, par, more):
                a = i * 2 + 2
                if more:
                    batch_norm2(a)
                    batch_norm2(a + 1)
                    root(a, 0)
                    root(a + 1, 1)
                if not isinstance(i, int) or i >= 0:
                    act.wait_ge(sh_done, i + 1)
                    hold(act)
                    act.activation(ex, lg, ACT.Exp).then_inc(ex_done, 1)
                if more:
                    keep_xfT(a)
                if not isinstance(i, int) or i >= 0:
                    act.wait_ge(gap_done, i + 1)
                    hold(act)
                    act.activation(e2, gap, ACT.Exp).then_inc(e2_done, 1)
                if more:
                    router_hidden(a)
                    keep_xfT(a + 1)
                    router_hidden(a + 1)

            routing(act, route)

            act.wait_ge(tiles_known, 1)

            def take_expert(s, u, part):
                done = (expert_a, expert_b)[part]
                if part == 0:
                    wait(act, l2_done, 2 * s - 2)
                    wait(act, h2_dve, s - 1)
                    wait(act, h2_act, s - 1)
                else:
                    wait(act, y_biased, s - 1)
                hold(act)
                e = act.value_load(tile_e_int[0:1, bass.ds(s, 1)], min_val=0, max_val=NX - 1)
                c0, c1 = ((0, EA), (EA, EA + EB))[part]
                hold(act)
                act.activation(we[u][:, c0:c1].unsqueeze(1), wx[:, bass.ds(e, 1), c0:c1], ACT.Copy).then_inc(done, 1)

            def keep_xT(s):
                wait(act, l1_done, 2 * s)
                act.wait_ge(tile_turned, s + 1)
                hold(act)
                act.activation(xT, ps[:, 0:KH, :], ACT.Copy).then_inc(xT_done, 1)

            def hidden(layer, s, u):
                done, used, hT, bank, out_sem = ((l1_done, (l2_done, 2 * s), h1T, 2, h1_act),
                                                 (l2_done, (l3_done, s), h2T, 4, h2_act))[layer]
                wait(act, *used)
                act.wait_ge(done, 2 * s + 1)
                hold(act)
                bias = we[u][:, 2 * KH * D + layer * KH:2 * KH * D + layer * KH + 1]
                act.activation(hT[:, 0, :], ps[:, bank, :], ACT.Relu, bias=bias).then_inc(out_sem, 1)

            def tile(s, u, next1, next2):
                hidden(1, s, u)
                if next2:
                    take_expert(s + 2, u, 0)
                if next1:
                    hidden(0, s + 1, 1 - u)
                    take_expert(s + 1, 1 - u, 1)
                if next2:
                    keep_xT(s + 2)

            take_expert(0, 0, 0)
            take_expert(1, 1, 0)
            take_expert(0, 0, 1)
            keep_xT(0)
            hidden(0, 0, 0)
            keep_xT(1)
            tiles(act, tile)

        @block.vector
        def _(dve):
            chain = Chain(dve, dve_chain)
            step = chain.step
            dve.wait_ge(iota_ready, 1)
            dve.tensor_copy(iota_bf[:, :], iota_i).then_inc(iota_bf_ready, 1)

            dve.wait_ge(edges_in, 32)
            dve.tensor_copy(src_f, src_i)
            step(dve.tensor_copy(dst_f, dst_i))
            dve.memset(marker[:, 0, 3:4], 0.0).then_inc(edges_ready, 1)
            step(dve.tensor_scalar(tmp_f, dst_f, 0.0, BIG, ALU.is_lt, ALU.mult))
            step(dve.tensor_tensor(tmp_f, tmp_f, dst_f, ALU.add))
            step(dve.tensor_reduce(wlo[:, :], tmp_f, AX.X, ALU.min))
            step(dve.tensor_reduce(whi[:, :], dst_f, AX.X, ALU.max))
            step(dve.tensor_scalar(wlo[:, :], wlo[:, :], float(WMAX), None, ALU.min))
            step(dve.tensor_tensor(whi[:, :], whi[:, :], wlo[:, :], ALU.subtract))
            dve.tensor_reduce(flags[:, 0:1], whi[:, :], AX.X, ALU.max).then_inc(span_ready, 1)
            dve.wait_ge(span_all, 1)
            step(dve.tensor_scalar(flags[:, 2:3], flags[:, 1:2], float(WIN), None, ALU.is_lt))
            step(dve.tensor_scalar(flags[:, 3:4], flags[:, 2:3], -1.0, 1.0, ALU.mult, ALU.add))
            dve.tensor_copy(bad_int[:, :], flags[:, 3:4]).then_inc(flag_ready, 1)
            step(dve.tensor_scalar(wlo[:, :], wlo[:, :], flags[:, 2:3], None, ALU.mult))
            dve.tensor_copy(w_int[:, :], wlo[:, :]).then_inc(w_ready, 1)
            def keep_table(table):
                for n in range(NT):
                    ng = min(P, TG - n * P)
                    turned = ps[:, n, :].rearrange("p (j g) -> p g j", j=CPG)
                    last = dve.tensor_copy(table[:, n * P:n * P + ng, :], turned[:, 0:ng, :])
                return last

            dve.wait_ge(dst_turned, 1)
            for n in range(NT):
                last = dve.tensor_scalar(dst_f[:, n, :], dst_f[:, n, :], wlo[:, n:n + 1], None, ALU.subtract)
            last.then_inc(rel_ready, 1)
            keep_table(dstT_i.rearrange("p (g j) -> p g j", j=CPG)).then_inc(dst_kept, 1)
            dve.wait_ge(dst_kept, 1)
            step(dve.tensor_scalar(digit_i, dstT_i, P - 1, None, ALU.bitwise_and))
            step(dve.tensor_copy(loT, digit_i))
            step(dve.tensor_scalar(digit_i, dstT_i, P.bit_length() - 1, None, ALU.arith_shift_right))
            dve.tensor_copy(hiT, digit_i)
            dve.wait_ge(iota_bf_ready, 1)
            step(dve.tensor_copy(iota_rep, iota_bf[:, 0:P].unsqueeze(2).to_broadcast([P, P, DCH])))
            dve.wait_ge(tables_turned, 1)
            keep_table(rel3).then_inc(tables_ready, 1)

            def row_stats(t, u):
                dve.wait_ge(stat_x_in[u], 16 * (half(t, u) + 1))
                hold(dve)
                for b in range(BPC):
                    last = dve.bn_stats(lnst[:, bass.ds(t * BPC + b, 1), :].rearrange("p o s -> p (o s)"), xbuf[0:RB, u, b, :])
                last.then_inc(stats_done, 1)

            def deg_step(d, u):
                wait(dve, deg_summed, d - 1)
                for table, oh, n in ((loT, oh_lo, P), (hiT, oh_hi, NHI)):
                    digit = table[:, bass.ds(d * DCH, DCH)].unsqueeze(1).to_broadcast([P, n, DCH])
                    last = dve.tensor_tensor(oh[u], iota_rep[:, 0:n, :], digit, ALU.is_equal)
                last.then_inc(deg_onehot, 1)

            def stats_and_degrees(t, u):
                row_stats(t, u)
                for k in range(DPER):
                    deg_step(t * DPER + k, (u * DPER + k) % 2)

            in_pairs(dve, stats_and_degrees)
            for d in range(NCH * DPER, DSTEPS):
                deg_step(d, d % 2)

            def mean_var(st, sm, df, m2, mean, var, step):
                step(dve.tensor_tensor(sm, st[:, :, 1], st[:, :, 4], ALU.add))
                step(dve.tensor_tensor(df, st[:, :, 1], st[:, :, 4], ALU.subtract))
                step(dve.tensor_tensor(m2, st[:, :, 2], st[:, :, 5], ALU.add))
                step(dve.tensor_scalar(mean, sm, 0.5, None, ALU.mult))
                step(dve.tensor_tensor(df, df, df, ALU.mult))
                step(dve.scalar_tensor_tensor(out=m2, in0=df, scalar=D / 4.0, in1=m2, op0=ALU.mult, op1=ALU.add))
                return dve.tensor_scalar(var, m2, 1.0 / D, EPS, ALU.mult, ALU.add)

            dve.wait_ge(stats_done, NCH)
            mean_var(lnst[:, :, :], ln_tmp[:, 0, :], ln_tmp[:, 1, :], ln_tmp[:, 2, :], ln_mean[:, :], ln_tmp[:, 0, :],
                     step).then_inc(ln_var, 1)
            dve.wait_ge(ln_sd, 1)
            step(dve.reciprocal(ln_rstd[:, :], ln_rstd[:, :]))

            dve.wait_ge(deg_summed, DSTEPS)
            dve.tensor_scalar(dg[:, :], ps[0:NHI, NT, 0:P], 1.0, None, ALU.add).then_inc(deg_done, 1)
            dve.wait_ge(sqrt_done, 1)
            dve.reciprocal(dg[:, :], dg[:, :]).then_inc(dinv_ready, 1)

            dve.wait_ge(flag_ready, 1)
            dve.wait_ge(w_row, 32)
            bad = dve.value_load(bad_int[0:1, 0:1], min_val=0, max_val=1)

            def aggregate(run):
                def sums(at, width):
                    return acc[:, :, bass.ds(at, width)]

                def partial(u, width):
                    return ps[:, 2 * u:2 * u + KH, 0:width]

                def product_done(n):
                    wait(dve, chunks_used, n * CPG + run * GATHERS if not isinstance(n, int) or n > 0 else 0)

                def make_onehot(g, u):
                    for j in range(CPG):
                        last = dve.tensor_scalar(onehot[:, u, j, 0:WIN], iota_bf[:, 0:WIN],
                                                 relT[:, bass.ds(g * CPG + j, 1)], None, ALU.is_equal)
                    last.then_inc(oh_fast[run], 1)

                def fast(g, u):
                    product_done(g)
                    hold(dve)
                    make_onehot(g + 1, 1 - u)
                    w = dve.value_load(wrow[0:1, bass.ds(g, 1)], min_val=0, max_val=WMAX)
                    product_done(g + 1)
                    wait(dve, ev_fast[run], g)
                    dve.tensor_tensor(sums(w, WIN), sums(w, WIN), partial(u, WIN), ALU.add).then_inc(ev_fast[run], 1)

                def general(g):
                    dve.wait_ge(rk_gen[run], g * (NW + 1) + 1)
                    hold(dve)
                    dve.tensor_copy(relk[:, :], relT[:, bass.ds(g * CPG, CPG)]).then_inc(rk_gen[run], 1)
                    with dve.Fori(0, NW) as k:
                        s = g * NW + k
                        dve.wait_ge(rk_gen[run], g * (NW + 1) + k + 2)
                        dve.wait_ge(mm_gen[run], s + 1)
                        hold(dve)
                        for j in range(CPG):
                            last = dve.tensor_scalar(onehot[:, 0, j, :], iota_bf[:, :], relk[:, j:j + 1], None, ALU.is_equal)
                        last.then_inc(oh_gen[run], 1)
                        dve.wait_ge(oh_gen[run], s + 1)
                        dve.tensor_scalar(relk[:, :], relk[:, :], float(GWIN), None, ALU.subtract).then_inc(rk_gen[run], 1)
                        dve.wait_ge(mm_gen[run], s + 2)
                        dve.wait_ge(ev_gen[run], s + 1)
                        hold(dve)
                        dve.tensor_tensor(sums(k * GWIN, GWIN), sums(k * GWIN, GWIN), partial(0, GWIN),
                                          ALU.add).then_inc(ev_gen[run], 1)
                    dve.memset(marker[:, run, 2:3], 0.0).then_inc(chunks_used, CPG)

                with dve.If(bad == 0):
                    make_onehot(0, 0)
                    for g in range(4):
                        fast(g, g % 2)
                    with dve.Fori(1, NG // 4) as i:
                        for q in range(4):
                            fast(i * 4 + q, q % 2)
                    dve.wait_ge(ev_fast[run], NG)
                with dve.Else():
                    dve.memset(marker[:, run, 0:1], 0.0).then_inc(mm_gen[run], 1)
                    dve.memset(marker[:, run, 1:2], 0.0).then_inc(ev_gen[run], 1)
                    dve.memset(marker[:, run, 4:5], 0.0).then_inc(rk_gen[run], 1)
                    with dve.Fori(0, NG) as g:
                        general(g)
                    dve.wait_ge(ev_gen[run], NG * NW + 1)

            dve.wait_ge(dn_turned, 1)
            step(dve.tensor_copy(dcol[:, :], ps[0:RB, 7, 0:NBLK]))
            step(dve.tensor_tensor(dcol[:, :], dcol[:, :], ln_rstd[:, :], ALU.mult))

            def split_rows(layer, t, u, rows):
                dve.wait_ge(hi_done[layer], t + 1)
                dve.tensor_tensor(rbuf[0:RB, u, :, :], rows, split[0:RB, u, :, 0:D], ALU.subtract).then_inc(r1_done[layer], 1)
                dve.wait_ge(mid_done[layer], t + 1)
                dve.tensor_tensor(split[0:RB, u, :, 2 * D:3 * D], rbuf[0:RB, u, :, :], split[0:RB, u, :, D:2 * D],
                                  ALU.subtract).then_inc(lo_done[layer], 1)

            def v_rows(t, u):
                dve.wait_ge(v_x_in[u], 16 * (half(t, u) + 1))
                hold(dve)
                for b in range(BPC):
                    at = t * BPC + b
                    last = dve.tensor_scalar(xbuf[0:RB, u, b, :], xbuf[0:RB, u, b, :], ln_mean[:, bass.ds(at, 1)],
                                             dcol[:, bass.ds(at, 1)], ALU.subtract, ALU.mult)
                last.then_inc(v_ready, 1)

            def v_split(t, u):
                split_rows(0, t, u, xbuf[0:RB, u, :, :])

            v_rows(0, 0)
            v_rows(1, 1)
            v_split(0, 0)
            with dve.Fori(1, PAIRS) as i:
                v_rows(i * 2, 0)
                v_split(i * 2 - 1, 1)
                v_rows(i * 2 + 1, 1)
                v_split(i * 2, 0)
            v_split(NCH - 1, 1)

            def linear(layer):
                dve.wait_ge(dinv_in, 16)

                def dinv_part(t):
                    return dinvT[:, bass.ds(t * CH, CH)].unsqueeze(1).to_broadcast([P, KH, CH])

                def scale(t, u):
                    dve.wait_ge(lin_done[layer], t + 1)
                    wait(dve, lin_biased[layer], t - 1)
                    hold(dve)
                    dve.tensor_tensor(lin_tmp[u], ps[:, 2 * u:2 * u + KH, 0:CH], dinv_part(t), ALU.mult).then_inc(lin_scaled[layer], 1)

                def stats(t, width=CH):
                    dve.wait_ge(lin_biased[layer], t + 1)
                    hold(dve)
                    for k in range(KH):
                        last = dve.bn_stats(bnst[:, k, bass.ds(t, 1), :].rearrange("p o s -> p (o s)"),
                                            acc[:, k, bass.ds(t * CH, width)])
                    return last

                scale(0, 0)
                scale(1, 1)
                stats(0)
                with dve.Fori(1, PAIRS) as i:
                    scale(i * 2, 0)
                    stats(i * 2 - 1)
                    scale(i * 2 + 1, 1)
                    stats(i * 2)
                step(stats(NCH - 1, TAIL))
                for k in range(KH):
                    last = dve.bn_aggr(bn_mv[:, k, :], bnst[:, k, :, :].rearrange("p t s -> p (t s)"))
                step(last)
                dve.tensor_scalar(bn_sc[:, 1, :], bn_mv[:, :, 1], EPS, None, ALU.add).then_inc(bn_var, 1)
                dve.wait_ge(bn_sd, layer + 1)
                step(dve.reciprocal(bn_sc[:, 1, :], bn_sc[:, 0, :]))
                step(dve.tensor_tensor(bn_sc[:, 2, :], vec[:, 3 * layer + 1, :], bn_sc[:, 1, :], ALU.mult))
                step(dve.tensor_tensor(bn_sc[:, 3, :], bn_mv[:, :, 0], bn_sc[:, 2, :], ALU.mult))
                dve.tensor_tensor(bn_sc[:, 3, :], vec[:, 3 * layer + 2, :], bn_sc[:, 3, :], ALU.subtract).then_inc(bn_ready, 1)

            dve.wait_ge(consts_in, 16 * NCONST)
            dve.wait_ge(v_kept, NCH)
            aggregate(L1)
            dve.memset(marker[:, L1, 3:4], 0.0).then_inc(agg_done, 1)
            linear(0)

            def y_cols(t, u):
                dve.wait_ge(relu_done, t + 1)
                wait(dve, y_turned, t - 1)
                wait(dve, y_kept, t - 1)
                dve.tensor_tensor(ybuf[u], acc[:, :, bass.ds(t * CH, CH)],
                                  dinvT[:, bass.ds(t * CH, CH)].unsqueeze(1).to_broadcast([P, KH, CH]), ALU.mult).then_inc(y_ready, 1)

            def y_split(t, u):
                dve.wait_ge(y_turned, t + 1)
                split_rows(1, t, u, ps[0:RB, 2 * u:2 * u + 2, :].rearrange("p a (b f) -> p (a b) f", b=2))

            y_cols(0, 0)
            y_cols(1, 1)
            y_split(0, 0)
            with dve.Fori(1, PAIRS) as i:
                y_cols(i * 2, 0)
                y_split(i * 2 - 1, 1)
                y_cols(i * 2 + 1, 1)
                y_split(i * 2, 0)
            y_split(NCH - 1, 1)

            dve.wait_ge(y_kept, NCH)
            aggregate(L2)
            dve.memset(marker[:, L2, 3:4], 0.0).then_inc(agg_done, 1)
            linear(1)

            for e in range(NX):
                dve.memset(wx[:, e, EA - 1:EA], float(e))
            step(dve.memset(run_bf, 0.0))
            dve.memset(ones_bf, 1.0).then_inc(ones_made, 1)
            dve.tensor_scalar(iota6, iota_bf[0:RB, 0:NX], float(NX), None, ALU.subtract)
            dve.tensor_scalar(region_start, iota_bf[0:RB, 0:NX], float(XR), None, ALU.mult)
            dve.wait_ge(masks_made, 3)
            dve.tensor_copy(tri_bf, tri_f)
            step(dve.tensor_copy(node_ids, iota_pb[0:RB, :]))
            dve.memset(marker[:, 0, 0:1], 0.0).then_inc(ones_made, 1)
            dve.wait_ge(ffn_in, 16 * NFFN)
            x1_steps, xf_steps, route_steps = Chain(dve, x1_chain), Chain(dve, xf_chain), Chain(dve, route_chain)
            X1_STEPS, XF_STEPS, ROUTE_STEPS = 9, 1, 23

            def x1_rows(t, u):
                xstep = x1_steps.step
                x1_steps.begin(t * X1_STEPS)
                xrows, x1 = xbuf[0:RB, u, :, :], rbuf[0:RB, u, :, :]
                dve.wait_ge(f_x_in[u], 16 * (half(t, u) + 1))
                hold(dve)
                for b in range(BPC):
                    at = t * BPC + b
                    last = dve.tensor_scalar(trow[:, b, :], xrows[:, b, :], ln_mean[:, bass.ds(at, 1)],
                                             ln_rstd[:, bass.ds(at, 1)], ALU.subtract, ALU.mult)
                xstep(last)
                dve.wait_ge(z_turned, t + 1)
                rows = ps[0:RB, 0:2, :].rearrange("p a (b f) -> p (a b) f", b=2)
                dve.tensor_tensor(trow, rows, trow, ALU.add).then_inc(z_added, 1)
                dve.wait_ge(z_added, t + 1)
                wait(dve, x1_out[u], 16 * half(t, u))
                hold(dve)
                dve.scalar_tensor_tensor(out=x1, in0=trow, scalar=0.0, in1=xrows, op0=ALU.max, op1=ALU.add).then_inc(x1_done, 1)
                dve.wait_ge(x1_done, t + 1)
                hold(dve)
                for b in range(BPC):
                    last = dve.bn_stats(st4[u][:, b, :], x1[:, b, :])
                xstep(last)
                mean_var(st4[u], sum4[u], dif4[u], m24[u], mean4[u], var4[u], xstep).then_inc(var_done, 1)
                xstep(dve.memset(marker[:, 0, 1:2], 0.0))
                assert x1_steps.n == X1_STEPS, x1_steps.n

            def xf_rows(t, u, par):
                xf_steps.begin(t * XF_STEPS)
                dve.wait_ge(sd_done, t + 1)
                xf_steps.step(dve.reciprocal(rstd4[u], sd4[u]))
                before = t // 4
                wait(dve, routed_out[par], 16 * 2 * B2 * before)
                hold(dve)
                for b in range(BPC):
                    last = dve.tensor_scalar(xrow[par][:, u * BPC + b, 0:D], rbuf[0:RB, u, b, :], mean4[u][:, b:b + 1],
                                             rstd4[u][:, b:b + 1], ALU.subtract, ALU.mult)
                last.then_inc(xf_done, 1)

            rstep = route_steps.step

            def over(a):
                return a.to_broadcast([RB, B2, NX])

            def across(a):
                return a.unsqueeze(1).to_broadcast([RB, B2, NX])

            def flat(a):
                return a.rearrange("p b o -> p (b o)")

            def route1(i):
                route_steps.begin(i * ROUTE_STEPS)
                dve.wait_ge(lg_mm, i * 2 + 2)
                logits = ps[0:RB, 5, 0:B2 * 8].rearrange("p (b n) -> p b n", b=B2)[:, :, 0:NX]
                dve.tensor_tensor(lg, logits, across(rb2_sb), ALU.add).then_inc(lg_read, 1)
                dve.wait_ge(lg_read, i + 1)
                rstep(dve.tensor_reduce(flat(lmax), lg, AX.X, ALU.max))
                dve.tensor_tensor(lg, lg, over(lmax), ALU.subtract).then_inc(sh_done, 1)

            def best(values, largest, where, mask):
                rstep(dve.tensor_reduce(flat(largest), values, AX.X, ALU.max))
                rstep(dve.tensor_tensor(eq, values, over(largest), ALU.is_equal))
                rstep(dve.tensor_tensor(cand, eq, across(iota6), ALU.mult))
                rstep(dve.tensor_reduce(flat(where), cand, AX.X, ALU.min))
                rstep(dve.tensor_tensor(mask, across(iota6), over(where), ALU.is_equal))

            def route2(i):
                dve.wait_ge(ex_done, i + 1)
                rstep(dve.tensor_reduce(flat(lsum), ex, AX.X, ALU.add))
                rstep(dve.reciprocal(lrec, lsum))
                rstep(dve.tensor_tensor(prob, ex, over(lrec), ALU.mult))
                best(prob, pmax, which1, m1st)
                rstep(dve.scalar_tensor_tensor(out=rest, in0=m1st, scalar=-2.0, in1=prob, op0=ALU.mult, op1=ALU.add))
                best(rest, pmax2, which2, m2nd)
                dve.tensor_tensor(gap, pmax2, pmax, ALU.subtract).then_inc(gap_done, 1)

            def route3(i, par):
                rstep(dve.tensor_tensor(mb_bf, m1st, m2nd, ALU.add))
                dve.memset(marker[:, 0, 2:3], 0.0).then_inc(mb_ready, 1)
                dve.wait_ge(e2_done, i + 1)
                rstep(dve.tensor_scalar(den, e2, 1.0, None, ALU.add))
                rstep(dve.reciprocal(xrow[par][:, :, D + 1:D + 2], den))
                dve.tensor_tensor(xrow[par][:, :, D + 2:D + 3], e2, xrow[par][:, :, D + 1:D + 2], ALU.mult)
                dve.tensor_scalar(xrow[par][:, :, D + 3:D + 4], which1, float(NX), None, ALU.add)
                rstep(dve.tensor_copy(xrow[par][:, :, D:D + 1], node_ids.unsqueeze(2)))
                rstep(dve.tensor_scalar(node_ids, node_ids, float(2 * CH), None, ALU.add))

            def route4(i, par):
                dve.wait_ge(ranked, i + 1)
                ranks = ps[0:RB, 6, 0:B2 * NX].rearrange("p (b e) -> p b e", e=NX)
                rstep(dve.tensor_tensor(pos, ranks, across(region_start), ALU.add))
                dve.tensor_reduce(run_add, mb_bf.rearrange("p b e -> p e b"), AX.X, ALU.add)
                dve.tensor_tensor(at1, m1st, pos, ALU.mult)
                rstep(dve.tensor_tensor(at2, m2nd, pos, ALU.mult))
                dve.tensor_tensor(run_bf, run_bf, run_add, ALU.add).then_inc(run_ready, 1)
                dve.tensor_reduce(addr1, at1, AX.X, ALU.add)
                rstep(dve.tensor_reduce(addr2, at2, AX.X, ALU.add))
                dve.tensor_copy(addr_int[:, par, 0, :], addr1)
                dve.tensor_copy(addr_int[:, par, 1, :], addr2).then_inc(rows_ready, 1)
                assert route_steps.n == ROUTE_STEPS, route_steps.n

            def route(i, par, more):
                a, small = i * 2 + 2, not isinstance(i, int) or i >= 0
                if more:
                    x1_rows(a, 0)
                    x1_rows(a + 1, 1)
                if small:
                    route1(i)
                if more:
                    xf_rows(a, 0, 1 - par)
                if small:
                    route2(i)
                if more:
                    xf_rows(a + 1, 1, 1 - par)
                if small:
                    route3(i, par)
                    route4(i, par)

            routing(dve, route)

            dve.wait_ge(zb_done, NCH)
            step(dve.memset(fill, 0.0))
            step(dve.tensor_scalar(fill[:, :, D:D + 1], iota_pb[:, 0:1].unsqueeze(1).to_broadcast([P, TB, 1]),
                                   float(NPAD), None, ALU.add))
            dve.memset(marker[:, 0, 4:5], 0.0).then_inc(fill_ready, 1)
            dve.wait_ge(counted, 1)
            dve.tensor_copy(count, ps[0:1, 7, 0:NX])
            dve.tensor_scalar(levels, iota_bf[0:1, 0:LEVELS], float(TOK), None, ALU.mult)
            step(dve.tensor_copy(tile_no, iota_bf[0:1, 0:TILES]))
            step(dve.tensor_tensor(reached, count.unsqueeze(2).to_broadcast([1, NX, LEVELS]),
                                   levels.unsqueeze(1).to_broadcast([1, NX, LEVELS]), ALU.is_gt))
            step(dve.tensor_reduce(n_tiles, reached, AX.X, ALU.add))
            step(dve.tensor_copy(last_tile, n_tiles))
            for e in range(1, NX):
                step(dve.tensor_tensor(last_tile[:, e:e + 1], last_tile[:, e - 1:e], last_tile[:, e:e + 1], ALU.add))
            dve.tensor_scalar(skip, n_tiles, -float(TOK), float(XR), ALU.mult, ALU.add)
            step(dve.tensor_tensor(behind, tile_no.unsqueeze(2).to_broadcast([1, TILES, NX]),
                                   last_tile.unsqueeze(1).to_broadcast([1, TILES, NX]), ALU.is_ge))
            step(dve.tensor_reduce(tile_e, behind, AX.X, ALU.add))
            step(dve.tensor_tensor(jump, behind, skip.unsqueeze(1).to_broadcast([1, TILES, NX]), ALU.mult))
            step(dve.tensor_reduce(tile_at, jump, AX.X, ALU.add))
            step(dve.scalar_tensor_tensor(out=tile_at, in0=tile_no, scalar=float(TOK), in1=tile_at, op0=ALU.mult, op1=ALU.add))
            step(dve.tensor_scalar(tile_at, tile_at, float(NX * XR), None, ALU.min))
            step(dve.tensor_scalar(tile_e, tile_e, float(NX - 1), None, ALU.min))
            step(dve.tensor_tensor(count, count, region_start[0:1, :], ALU.add))
            dve.tensor_copy(tail_int, count)
            dve.tensor_copy(tile_e_int, tile_e)
            dve.tensor_copy(tile_at_int, tile_at).then_inc(tiles_known, 1)

            def hidden(layer, s, u):
                done, used, hT, bank, out_sem = ((l1_done, (l2_done, 2 * s), h1T, 3, h1_dve),
                                                 (l2_done, (l3_done, s), h2T, 5, h2_dve))[layer]
                wait(dve, *used)
                dve.wait_ge(done, 2 * s + 2)
                bias = we[u][:, 2 * KH * D + layer * KH + 1:2 * KH * D + layer * KH + 2]
                dve.tensor_scalar(hT[:, 1, :], ps[:, bank, :], bias, 0.0, ALU.add, ALU.max).then_inc(out_sem, 1)

            def keep_ids(s, u):
                dve.wait_ge(rows_in[u], 16 * (half(s, u) + 1))
                dve.wait_ge(expert_a, s + 1)
                wait(dve, added[u], 16 * TB * half(s, u))
                hold(dve)
                columns = [tile_rows[u][:, :, D + n] for n in range(4)]
                number = we[u][:, EA - 1:EA]
                dve.scalar_tensor_tensor(out=wsel[:, u, :], in0=columns[3], scalar=number, in1=columns[1],
                                         op0=ALU.is_equal, op1=ALU.mult)
                dve.scalar_tensor_tensor(out=wsel2[:, u, :], in0=columns[3], scalar=number, in1=columns[2],
                                         op0=ALU.not_equal, op1=ALU.mult)
                dve.tensor_copy(out_idx[:, u, :], columns[0]).then_inc(ids_ready, 1)

            def y_rows(s, u):
                dve.wait_ge(ids_ready, s + 1)
                dve.tensor_tensor(wsel[:, u, :], wsel[:, u, :], wsel2[:, u, :], ALU.add)
                dve.wait_ge(l3_done, s + 1)
                wait(dve, added[u], 16 * TB * half(s, u))
                dve.wait_ge(expert_b, s + 1)
                rows = ps[:, 6:8, :].rearrange("p a (b f) -> p (a b) f", b=2)
                bias = we[u][:, EA + KH * D:EA + EB].unsqueeze(1).to_broadcast([P, TB, D])
                hold(dve)
                dve.tensor_tensor(yrow[u], rows, bias, ALU.add).then_inc(y_biased, 1)
                dve.wait_ge(y_biased, s + 1)
                hold(dve)
                for b in range(TB):
                    last = dve.tensor_scalar(yrow[u][:, b, :], yrow[u][:, b, :], wsel[:, u, b:b + 1], None, ALU.mult)
                last.then_inc(y_weighted, 1)

            def tile(s, u, next1, next2):
                hidden(1, s, u)
                if next1:
                    hidden(0, s + 1, 1 - u)
                y_rows(s, u)
                if next1:
                    keep_ids(s + 1, 1 - u)

            keep_ids(0, 0)
            hidden(0, 0, 0)
            tiles(dve, tile)

        @block.tensor
        def _(pe):
            def turn(out, in_, last_sem=None):
                n = in_.shape[0]
                return pe.transpose(out, in_, ident[0:n, 0:n])

            def turn_table(table, bank):
                for n in range(NT):
                    for j in range(CPG):
                        last = turn(ps[:, bank + n, j * P:(j + 1) * P], table[:, n, j * P:(j + 1) * P])
                return last

            pe.wait_ge(ident_ready, 2)
            pe.wait_ge(edges_ready, 1)
            turn_table(dst_f, 0)
            turn_table(src_f, NT).then_inc(dst_turned, 1)
            pe.wait_ge(rel_ready, 1)
            pe.wait_ge(dst_kept, 1)
            turn_table(dst_f, 0).then_inc(tables_turned, 1)

            pe.wait_ge(src_kept, 1)

            def deg_product(d, u, first=False, final=False):
                pe.wait_ge(deg_onehot, d + 1)
                for j in range(DCH):
                    last = pe.matmul(ps[0:NHI, NT, 0:P], oh_hi[u][:, :, j], oh_lo[u][:, :, j],
                                     start=first and j == 0, stop=final and j == DCH - 1)
                last.then_inc(deg_summed, 1)

            for u in range(2):
                deg_product(u, u, first=u == 0)
            if DSTEPS > 4:
                with pe.Fori(1, DSTEPS // 2 - 1) as i:
                    for u in range(2):
                        deg_product(i * 2 + u, u)
            for u in range(2):
                deg_product(DSTEPS - 2 + u, u, final=u == 1)

            pe.wait_ge(flag_ready, 1)
            pe.wait_ge(tables_ready, 1)
            bad = pe.value_load(bad_int[0:1, 0:1], min_val=0, max_val=1)

            def aggregate(run):
                done = run * GATHERS

                def product(u, ohu, j, s, width):
                    for k in range(KH):
                        for n in range(PARTS):
                            last = pe.matmul(ps[:, 2 * u + k, 0:width], slots[:, s, n * D + k * P:n * D + (k + 1) * P],
                                             onehot[:, ohu, j, 0:width], start=j == 0 and n == 0,
                                             stop=j == CPG - 1 and n == PARTS - 1)
                    return last

                def landed(s, use):
                    pe.wait_ge(got[s], 16 * (use + done // SLOTS + 1))

                def fast(i, q):
                    g, u = i * 4 + q, q % 2
                    pe.wait_ge(oh_fast[run], g + 1)
                    wait(pe, ev_fast[run], g - 1)
                    for j in range(CPG):
                        s = (q * CPG + j) % SLOTS
                        landed(s, i * 2 + (q * CPG + j) // SLOTS)
                        product(u, u, j, s, WIN).then_inc(chunks_used, 1)

                def general(i, u):
                    g = i * 2 + u

                    for j in range(CPG):
                        landed(u * CPG + j, i)
                    hold(pe)
                    with pe.Fori(0, NW) as k:
                        s = g * NW + k
                        pe.wait_ge(oh_gen[run], s + 1)
                        pe.wait_ge(ev_gen[run], s + 1)
                        for j in range(CPG):
                            last = product(0, 0, j, u * CPG + j, GWIN)
                        last.then_inc(mm_gen[run], 1)

                with pe.If(bad == 0):
                    for q in range(4):
                        fast(0, q)
                    with pe.Fori(1, NG // 4) as i:
                        for q in range(4):
                            fast(i, q)
                with pe.Else():
                    with pe.Fori(0, NG // 2) as i:
                        for u in range(2):
                            general(i, u)

            pe.wait_ge(dn_in, 32)
            turn(ps[0:RB, 7, 0:NBLK], dn[:, :]).then_inc(dn_turned, 1)

            def v_turn(t, u):
                pe.wait_ge(v_ready, t + 1)
                wait(pe, v_kept, t - 1)
                for b in range(BPC):
                    for k in range(KH):
                        last = turn(ps[:, 2 * u + k, b * RB:(b + 1) * RB], xbuf[0:RB, u, b, k * P:(k + 1) * P])
                last.then_inc(v_turned, 1)

            in_pairs(pe, v_turn)

            def linear(layer):
                pe.wait_ge(agg_done, layer + 1)

                def lin(t, u):
                    wait(pe, lin_scaled[layer], t - 1)
                    for m in range(KH):
                        for k in range(KH):
                            last = pe.matmul(ps[:, 2 * u + m, 0:CH], wconv[:, layer, k, m * P:(m + 1) * P],
                                             acc[:, k, bass.ds(t * CH, CH)], start=k == 0, stop=k == KH - 1)
                    last.then_inc(lin_done[layer], 1)

                in_pairs(pe, lin)

            pe.wait_ge(consts_in, 16 * NCONST)
            pe.wait_ge(v_kept, NCH)
            aggregate(L1)
            linear(0)

            def y_turn(t, u):
                pe.wait_ge(y_ready, t + 1)
                wait(pe, r1_done[1], t - 1)
                for b in range(BPC):
                    for k in range(KH):
                        at = (b % 2) * D + k * P
                        last = turn(ps[0:RB, 2 * u + b // 2, at:at + P], ybuf[u][:, k, b * RB:(b + 1) * RB])
                last.then_inc(y_turned, 1)

            in_pairs(pe, y_turn)
            pe.wait_ge(r1_done[1], NCH)
            aggregate(L2)
            linear(1)
            pe.wait_ge(ffn_in, 16 * NFFN)
            pe.wait_ge(ones_made, 2)

            def turn_z(t):
                pe.wait_ge(zb_done, t + 1)
                wait(pe, z_added, t)
                hold(pe)
                for b in range(BPC):
                    for k in range(KH):
                        at = (b % 2) * D + k * P
                        last = turn(ps[0:RB, b // 2, at:at + P], zb[:, k, b * RB:(b + 1) * RB])
                last.then_inc(z_turned, 1)

            def router(t, u, par):
                pe.wait_ge(xf_done, t + 1)
                wait(pe, xfT_done, t)
                hold(pe)
                for b in range(BPC):
                    for k in range(KH):
                        last = turn(ps[:, 2 + k, b * RB:(b + 1) * RB], xrow[par][:, u * BPC + b, k * P:(k + 1) * P])
                last.then_inc(x_turned, 1)

            def router_mm(t, u):
                pe.wait_ge(xfT_done, t + 1)
                wait(pe, rhT_done, t)
                hold(pe)
                for k in range(KH):
                    last = pe.matmul(ps[:, 4, 0:CH], rw1_sb[:, k, :], xfT[:, k, :], start=k == 0, stop=k == KH - 1)
                last.then_inc(rh_done, 1)
                pe.wait_ge(rhT_done, t + 1)
                wait(pe, lg_read, (t - u) // 2 if isinstance(t, int) else t // 2)
                hold(pe)
                for b in range(BPC):
                    at = (u * BPC + b) * 8
                    last = pe.matmul(ps[0:RB, 5, at:at + NX], rhT[:, b * RB:(b + 1) * RB], rw2_sb, start=True, stop=True)
                last.then_inc(lg_mm, 1)

            def rank(i):
                pe.wait_ge(mb_ready, i + 1)
                wait(pe, run_ready, i)
                hold(pe)
                every = mb_bf.rearrange("p b e -> p (b e)")
                pe.matmul(ps[0:RB, 6, 0:B2 * NX], tri_bf, every, start=True, stop=False)
                pe.matmul(ps[0:RB, 6, 0:B2 * NX], ones_bf[:, 0:RB], run_bf.unsqueeze(1).to_broadcast([RB, B2, NX]),
                          start=False, stop=False)
                for b in range(B2 - 1):
                    n = B2 - 1 - b
                    last = pe.matmul(ps[0:RB, 6, (b + 1) * NX:B2 * NX], ones_bf[:, 0:RB],
                                     mb_bf[:, b:b + 1, :].to_broadcast([RB, n, NX]), start=False, stop=n == 1)
                last.then_inc(ranked, 1)

            def route(i, par, more):
                a, small = i * 2 + 2, not isinstance(i, int) or i >= 0
                if more:
                    turn_z(a)
                    turn_z(a + 1)
                    router(a, 0, 1 - par)
                    router_mm(a, 0)
                    router(a + 1, 1, 1 - par)
                if small:
                    rank(i)
                if more:
                    router_mm(a + 1, 1)

            routing(pe, route)
            pe.wait_ge(run_ready, PAIRS)
            pe.matmul(ps[:, 7, 0:NX], ones_bf, run_bf, start=True, stop=True).then_inc(counted, 1)

            pe.wait_ge(tiles_known, 1)

            def turn_tile(s, u):
                pe.wait_ge(rows_in[u], 16 * (half(s, u) + 1))
                wait(pe, xT_done, s)
                hold(pe)
                for b in range(TB):
                    for k in range(KH):
                        last = turn(ps[:, k, b * P:(b + 1) * P], tile_rows[u][:, b, k * P:(k + 1) * P])
                last.then_inc(tile_turned, 1)

            def hidden(layer, s, u):
                if layer == 0:
                    pe.wait_ge(xT_done, s + 1)
                    pe.wait_ge(expert_a, s + 1)
                    rhs, done, free, bank = xT, l1_done, (h1_act, h1_dve), 2
                else:
                    pe.wait_ge(h1_act, s + 1)
                    pe.wait_ge(h1_dve, s + 1)
                    rhs, done, free, bank = h1T, l2_done, (h2_act, h2_dve), 4
                for f in free:
                    wait(pe, f, s)
                hold(pe)
                for m in range(KH):
                    for k in range(KH):
                        last = pe.matmul(ps[:, bank + m, :], w_of(u, layer, k, m * P, (m + 1) * P), rhs[:, k, :],
                                         start=k == 0, stop=k == KH - 1)
                    last.then_inc(done, 1)

            def rows_out(s, u):
                pe.wait_ge(h2_act, s + 1)
                pe.wait_ge(h2_dve, s + 1)
                pe.wait_ge(expert_b, s + 1)
                wait(pe, y_biased, s)
                hold(pe)
                for b in range(TB):
                    for k in range(KH):
                        last = pe.matmul(ps[:, 6 + b // 2, (b % 2) * D:(b % 2 + 1) * D], h2T[:, k, b * P:(b + 1) * P],
                                         w_of(u, 2, k, 0, D), start=k == 0, stop=k == KH - 1)
                last.then_inc(l3_done, 1)

            def tile(s, u, next1, next2):
                hidden(1, s, u)
                if next1:
                    hidden(0, s + 1, 1 - u)
                rows_out(s, u)
                if next2:
                    turn_tile(s + 2, u)

            turn_tile(0, 0)
            hidden(0, 0, 0)
            turn_tile(1, 1)
            tiles(pe, tile)


_INS = ["x", "src", "dst", "L0_gnn_W1", "L0_gnn_b1", "L0_gnn_W2", "L0_gnn_b2", "L0_gnn_gamma1", "L0_gnn_beta1",
        "L0_gnn_gamma2", "L0_gnn_beta2", "L0_ffn_router_w1", "L0_ffn_router_b1", "L0_ffn_router_w2", "L0_ffn_router_b2",
        "L0_ffn_expert_w1", "L0_ffn_expert_b1", "L0_ffn_expert_w2", "L0_ffn_expert_b2", "L0_ffn_expert_w3", "L0_ffn_expert_b3"]


def kernel(**inputs):
    import numpy as _np
    import concourse.bacc as _bacc
    from concourse import mybir as _mybir
    from concourse.bass_utils import run_bass_kernel_spmd as _run

    nc = _bacc.Bacc("TRN2", target_bir_lowering=False, num_devices=1)
    n_nodes, n_edges = inputs["x"].shape[0], inputs["src"].shape[0]
    n_chunks, _, n_tables = sizes(n_nodes, n_edges)
    pads = {"x": (n_chunks * CH, 0), "src": (n_tables * P * GE, 0), "dst": (n_tables * P * GE, -1)}
    arrays, args = {}, []
    for name in _INS:
        a = _np.ascontiguousarray(inputs[name])
        if name in pads:
            rows, fill = pads[name]
            padded = _np.full((rows,) + a.shape[1:], fill, a.dtype)
            padded[:a.shape[0]] = a
            a = padded
        arrays[f"in_{name}_dram"] = a
        args.append(nc.dram_tensor(f"in_{name}_dram", a.shape, _mybir.dt.from_np(a.dtype), kind="ExternalInput").ap())
    shape = (n_chunks * CH + P, inputs["x"].shape[1])
    args.append(nc.dram_tensor("out_0_dram", shape, _mybir.dt.float32, kind="ExternalOutput").ap())
    gnn_moe(nc, n_nodes, n_edges, *args)
    r = _run(nc, [arrays], core_ids=[0])
    return r.results[0]["out_0_dram"][:n_nodes]
```

```python
from contextlib import ExitStack

import numpy as np

import concourse.bass as bass
from concourse import mybir

F32 = mybir.dt.float32
BF16 = mybir.dt.bfloat16
I32 = mybir.dt.int32
U32 = mybir.dt.uint32
ALU = mybir.AluOpType
ACT = mybir.ActivationFunctionType
AX = mybir.AxisListType
RMAX = bass.bass_isa.ReduceOp.max
RADD = bass.bass_isa.ReduceOp.add

P = 128
RB = 112
BPC = 4
CH = RB * BPC
EC = P
CPG = 4
GE = EC * CPG
WIN = 64
GWIN = 256
DCH = 16
TB = 4
TOK = P * TB
SLOTS = 8
BIG = float(1 << 20)
EPS = 1e-5


def sizes(n_nodes, n_edges):
    n_chunks = -(-n_nodes // CH)
    n_chunks += -n_chunks % 4
    n_groups = -(-n_edges // GE)
    stride = -(-n_groups // (4 * n_chunks)) * 4
    n_groups += -n_groups % (2 * stride)
    n_tables = -(-(n_groups + 4) // P)
    return n_chunks, n_groups, n_tables, stride



def wait(eng, sem, value):
    if not isinstance(value, int) or value > 0:
        eng.wait_ge(sem, value)


def hold(eng):
    eng.nop(nofuse=True)


class Chain:

    def __init__(self, eng, sem):
        self.eng, self.sem, self.base, self.n = eng, sem, 0, 0

    def begin(self, base):
        self.base, self.n = base, 0

    def step(self, instruction):
        self.n += 1
        instruction.then_inc(self.sem, 1)
        self.eng.wait_ge(self.sem, self.base + self.n)


def gnn_moe(nc, N, E, x, src, dst, W1, b1, W2, b2, gamma1, beta1, gamma2, beta2,
            rw1, rb1, rw2, rb2, ew1, eb1, ew2, eb2, ew3, eb3, out):
    D = x.shape[1]
    KH = D // P
    NX = ew1.shape[0]
    NCH, NG, NT, STRIDE = sizes(N, E)
    STRIDES = NG // STRIDE
    NPAD = NCH * CH
    NBLK = NCH * BPC
    NW = -(-NPAD // GWIN)
    WIDTH = max(NPAD, NW * GWIN)
    WMAX = NPAD - WIN
    TG = min(NT * P, NG + 32)
    TAIL = N - (NCH - 1) * CH
    PAIRS = NCH // 2
    PARTS = 3
    LOW = P // 2
    NHI = NPAD // LOW
    DSTEPS = NG * CPG // DCH
    DBASE = 4 if DSTEPS % 4 == 0 else 2
    HWIN = 12
    NBASE = DSTEPS // DBASE
    BASE_GROUPS = NG // NBASE
    LATE = 2 * min(4, NCH // 6, WIDTH // (2 * BPC * (D + 9)))
    EARLY = NCH - LATE
    ROW = D + 4
    XR = NPAD + TOK
    TILES = (2 * NPAD + NX * (TOK - 1)) // TOK
    TILES += TILES % 2
    LEVELS = -(-NPAD // TOK)
    assert D == 256 and 3 <= STRIDES <= NCH + 1 and PAIRS >= 4 and NPAD % P == 0 and NHI <= GWIN and LATE < EARLY // 2 and NHI >= 2 * HWIN and NHI % 2 == 0 and NHI // 2 <= P and 2 * (NHI + HWIN) <= 512 and DSTEPS >= 4 and NBLK <= P and NT <= 4 and 0 < TAIL <= CH and rw1.shape[1] == P and TILES <= GWIN

    t_dram = [nc.dram_tensor(f"messages_{n}", (NPAD, PARTS * D), BF16, kind="Internal").ap() for n in (1, 2)]
    routed = nc.dram_tensor("routed_rows", (NX * XR + TOK, ROW), F32, kind="Internal").ap()
    w_dram = nc.dram_tensor("window_starts", (NT * P,), I32, kind="Internal").ap()
    dinv_dram = nc.dram_tensor("dinv_row", (NPAD,), F32, kind="Internal").ap()

    with ExitStack() as ctx:
        def sb(name, shape, dt=F32):
            return ctx.enter_context(nc.sbuf_tensor(name, shape, dt))

        def sem(name):
            return ctx.enter_context(nc.semaphore(name))

        def sems(name, n):
            return [sem(f"{name}{i}") for i in range(n)]

        acc = sb("acc", [P, KH, WIDTH])
        dinvT = sb("dinvT", [P, WIDTH])
        tables = sb("tables", [P, 2 * max(TG * CPG, KH * 2 * CH)])
        relT = tables[:, 0:TG * CPG]
        srcT = tables[:, TG * CPG:2 * TG * CPG]
        ring = sb("ring", [P, SLOTS * PARTS * D // 2])
        onehot_mem = sb("onehot_mem", [P, 2 * CPG * GWIN // 2])
        rows_mem = sb("rows_mem", [P, 4 * BPC * D])
        xbuf = rows_mem[:, 0:2 * BPC * D].rearrange("p (u b f) -> p u b f", u=2, b=BPC)
        rbuf = rows_mem[:, 2 * BPC * D:4 * BPC * D].rearrange("p (u b f) -> p u b f", u=2, b=BPC)
        wconv = sb("wconv", [P, 2, KH, D])
        vec = sb("vec", [P, 6, KH])
        ident = sb("ident", [P, P])
        iota_bf = sb("iota_bf", [P, GWIN], BF16)
        idx_stage = sb("idx_stage", [P, 2, SLOTS], I32)
        relk = sb("relk", [P, CPG])
        wrow = sb("wrow", [1, NT * P], I32)
        bnst = sb("bnst", [P, KH, NCH, 6])
        ln_part = sb("ln_part", [RB, 3, BPC])
        ln_mean = sb("ln_mean", [RB, NBLK])
        ln_rstd = sb("ln_rstd", [RB, NBLK])
        ln_tmp = sb("ln_tmp", [RB, 3, NBLK])
        dcol = sb("dcol", [RB, NBLK])
        dn = sb("dn", [NBLK, RB])
        wlo = sb("wlo", [P, NT])
        whi = sb("whi", [P, NT])
        w_int = sb("w_int", [P, NT], I32)
        flags = sb("flags", [P, 4])
        bad_int = sb("bad_int", [P, 1], I32)
        bn_mv = sb("bn_mv", [P, KH, 2])
        bn_sc = sb("bn_sc", [P, 4, KH])
        marker = sb("marker", [P, 2, 5])
        ps = ctx.enter_context(nc.psum_tensor("ps", [P, 8, 512], F32))

        accflat = acc[:, :, :].rearrange("p k n -> p (k n)")
        TE = NT * GE
        dst_i = accflat[:, 0:TE].bitcast(I32).rearrange("p (t e) -> p t e", t=NT)
        src_i = accflat[:, TE:2 * TE].bitcast(I32).rearrange("p (t e) -> p t e", t=NT)
        dst_f = accflat[:, 2 * TE:3 * TE].rearrange("p (t e) -> p t e", t=NT)
        src_f = accflat[:, 3 * TE:4 * TE].rearrange("p (t e) -> p t e", t=NT)
        tmp_f = accflat[:, 4 * TE:5 * TE].rearrange("p (t e) -> p t e", t=NT)
        iota_i = accflat[:, 5 * TE:5 * TE + GWIN].bitcast(I32)
        lent = [5 * TE + GWIN]

        def lend(n_bytes):
            a = accflat[:, lent[0]:lent[0] + n_bytes // 4]
            lent[0] += n_bytes // 4
            assert lent[0] <= KH * WIDTH
            return a

        group_i, group_f, group_lo = lend(4 * NT).bitcast(I32), lend(4 * NT), lend(4 * NT)
        dstT_i, digit_i = lend(4 * TG * CPG).bitcast(I32), lend(4 * TG * CPG).bitcast(I32)
        loT, hiT = lend(2 * TG * CPG).bitcast(BF16), lend(2 * TG * CPG).bitcast(BF16)
        hrT = lend(2 * TG * CPG).bitcast(BF16)
        w_all, base_i, base_f = lend(4 * NT * P).bitcast(I32), lend(4 * NBASE).bitcast(I32), lend(4 * NBASE)
        zeros_bf = lend(2 * P).bitcast(BF16)
        deg_check, deg_bad = lend(16), lend(4).bitcast(I32)
        pair_total, parity = lend(8), lend(8)
        iota_rep = lend(2 * max(NHI, LOW) * DCH).bitcast(BF16).rearrange("p (w j) -> p w j", j=DCH)
        oh_lo = [lend(2 * LOW * DCH).bitcast(BF16).rearrange("p (a w j) -> p a w j", j=2, w=LOW) for _ in range(DBASE)]
        oh_hi = [lend(2 * NHI * DCH).bitcast(BF16).rearrange("p (w j) -> p w j", j=DCH) for _ in range(2)]
        oh_win = [oh_hi[u % 2][:, u // 2 * HWIN:(u // 2 + 1) * HWIN, :] for u in range(DBASE)]
        rel3 = relT.rearrange("p (g j) -> p g j", j=CPG)
        src3 = srcT.bitcast(I32).rearrange("p (g j) -> p g j", j=CPG)
        srcidx = srcT.bitcast(I32)
        dg = ring[0:NHI // 2, 0:P]
        counted_in = ring[:, P:P + 2 * NHI].rearrange("p (j h) -> p j h", j=2)
        ring_bf = ring[:, :].bitcast(BF16)
        slots = ring_bf.rearrange("p (s f) -> p s f", s=SLOTS)
        onehot = onehot_mem[:, :].bitcast(BF16).rearrange("p (u j w) -> p u j w", u=2, j=CPG)
        lin_tmp = rbuf[:, 0, :, :].rearrange("p b f -> p (b f)")[:, 0:KH * CH].rearrange("p (k n) -> p k n", k=KH)
        PART = BPC * PARTS * D // 2
        y_parts = [mem[0:RB, n * PART:(n + 1) * PART].bitcast(BF16).rearrange("p (b f) -> p b f", b=BPC)
                   for mem in (ring, rows_mem) for n in range(2)]
        ybuf = [mem[:, at:at + KH * CH].rearrange("p (k n) -> p k n", k=KH) for mem, at in ((onehot_mem, 0), (rows_mem, 2 * PART))]
        v_row = [buf[0:RB, u, :, :] for buf in (xbuf, rbuf) for u in range(2)]
        LATE_BLOCKS = LATE * BPC
        x_late = dinvT[0:RB, 0:LATE_BLOCKS * D].rearrange("p (b f) -> p b f", f=D)
        st_late = dinvT[0:RB, LATE_BLOCKS * D:LATE_BLOCKS * (D + 6)].rearrange("p (b s) -> p b s", s=6)
        sum_late, dif_late, m2_late = [dinvT[0:RB, LATE_BLOCKS * (D + n):LATE_BLOCKS * (D + n + 1)] for n in (6, 7, 8)]
        v_left = [dinvT[0:RB, q * BPC * D:(q + 1) * BPC * D].rearrange("p (b f) -> p b f", b=BPC) for q in range(4)]
        v_parts = [dinvT[0:RB, 4 * BPC * D + q * BPC * PARTS * D // 2:4 * BPC * D + (q + 1) * BPC * PARTS * D // 2].bitcast(BF16)
                   .rearrange("p (b f) -> p b f", b=BPC) for q in range(4)]

        class Region:

            def __init__(self, mem, start=0):
                self.mem, self.at = mem, start

            def take(self, parts, *shape):
                n = int(np.prod(shape))
                a = self.mem[0:parts, self.at:self.at + n]
                self.at += n
                assert self.at <= self.mem.shape[1]
                if len(shape) == 1:
                    return a
                names = "abcd"[:len(shape)]
                return a.rearrange(f"p ({' '.join(names)}) -> p {' '.join(names)}", **dict(zip(names, shape)))

        ln_bias = ln_tmp[:, 1, :]
        B2 = 2 * BPC
        EA, EB = 2 * KH * D + 2 * KH + 1, KH * D + D
        old_dinv = Region(dinvT)
        x_in = [[xbuf[0:RB, 0, :, :], xbuf[0:RB, 1, :, :]], [old_dinv.take(RB, BPC, D) for _ in range(2)]]
        xhat = [old_dinv.take(RB, BPC, D) for _ in range(2)]
        rhT = old_dinv.take(P, CH)
        rw1_sb = old_dinv.take(P, KH, P)
        rw2_sb, rb1_sb, rb2_sb = old_dinv.take(P, NX), old_dinv.take(P, 1), old_dinv.take(RB, NX)
        iota6, region_start = old_dinv.take(RB, NX), old_dinv.take(RB, NX)
        tri_bf = old_dinv.take(RB, RB // 2).bitcast(BF16)
        ones_bf = old_dinv.take(RB, P // 2).bitcast(BF16)
        st8 = old_dinv.take(RB, B2, 6)
        sum8, dif8, m28, mean8, var8, sd8, rstd8, shift8 = [old_dinv.take(RB, B2) for _ in range(8)]
        lg, ex, prob, eq, cand, m1st, m2nd, rest, pos, at1, at2 = [old_dinv.take(RB, B2, NX) for _ in range(11)]
        lmax, lsum, lrec, pmax, which1, pmax2, which2, gap, e2, den = [old_dinv.take(RB, B2, 1) for _ in range(10)]
        node_ids, addr1, addr2 = old_dinv.take(RB, B2), old_dinv.take(RB, B2), old_dinv.take(RB, B2)
        mb_bf = old_dinv.take(RB, B2 * NX // 2).bitcast(BF16).rearrange("p (b e) -> p b e", e=NX)
        run_bf = old_dinv.take(RB, NX // 2).bitcast(BF16)
        run_add = old_dinv.take(RB, NX)
        old_ring, old_tables = Region(ring), Region(tables)
        xrow = [mem.take(RB, B2, ROW) for mem in (old_ring, old_tables, old_dinv, old_dinv)]
        XBUFS = len(xrow)
        zb = [old_ring.take(P, KH, CH), Region(onehot_mem).take(P, KH, CH)]
        xfT = old_tables.take(P, KH, CH)
        tri_f = old_tables.take(RB, RB)
        iota_pb = old_tables.take(P, B2).bitcast(I32)
        addr_int = old_tables.take(RB, XBUFS, 2, B2).bitcast(I32)
        old_acc = Region(accflat)
        wx = old_acc.take(P, NX, EA + EB)
        WX_CHUNKS = min(NCH, -(-NX * (EA + EB) // CH))
        we = [old_acc.take(P, EA + EB) for _ in range(2)]
        tile_rows = [old_acc.take(P, TB, ROW) for _ in range(2)]
        xT, h1T, h2T = [old_acc.take(P, KH, TOK) for _ in range(3)]
        yrow = [old_acc.take(P, TB, D) for _ in range(2)]
        fill = old_acc.take(P, TB, ROW)
        out_idx, wsel, wsel2 = old_acc.take(P, 2, TB).bitcast(I32), old_acc.take(P, 2, TB), old_acc.take(P, 2, TB)
        count, n_tiles, last_tile, skip = [old_acc.take(1, NX) for _ in range(4)]
        levels = old_acc.take(1, LEVELS)
        reached = old_acc.take(1, NX, LEVELS)
        behind, jump = old_acc.take(1, TILES, NX), old_acc.take(1, TILES, NX)
        tile_no, tile_e, tile_at = [old_acc.take(1, TILES) for _ in range(3)]
        tail_int, tile_e_int, tile_at_int = old_acc.take(1, NX).bitcast(I32), old_acc.take(1, TILES).bitcast(I32), old_acc.take(1, TILES).bitcast(I32)

        RANKS = 128

        def w_of(u, m, k, n0, n1):
            at = (0, KH * D, EA)[m] + k * D
            return we[u][:, at + n0:at + n1]

        experts_in = sem("experts_in")
        edges_in, consts_in, w_row, dn_in, router_in = sem("edges_in"), sem("consts_in"), sem("w_row"), sem("dn_in"), sem("router_in")
        group_ready = sem("group_ready")
        ident_ready, iota_ready, iota_bf_ready = sem("ident_ready"), sem("iota_ready"), sem("iota_bf_ready")
        span_ready, span_all, flag_ready, w_ready = sem("span_ready"), sem("span_all"), sem("flag_ready"), sem("w_ready")
        edges_ready, dst_turned, dst_kept = sem("edges_ready"), sem("dst_turned"), sem("dst_kept")
        rel_ready, tables_turned, tables_ready, src_kept = sem("rel_ready"), sem("tables_turned"), sem("tables_ready"), sem("src_kept")
        dinv_in = sem("dinv_in")
        deg_onehot, deg_summed, dinv_ready = sem("deg_onehot"), sem("deg_summed"), sem("dinv_ready")
        base_ready, deg_total, deg_checked, deg_flag, deg_kept, dg_turned = [
            sem(n) for n in ("base_ready", "deg_total", "deg_checked", "deg_flag", "deg_kept", "dg_turned")]
        dn_turned, root_wanted, root_done = sem("dn_turned"), sem("root_wanted"), sem("root_done")
        stat_x_in, stats_done = sems("stat_x_in", 2), sem("stats_done")
        late_in = sem("late_in")
        row_chain = sem("row_chain")
        dve_chain = sem("dve_chain")
        got = sems("got", SLOTS)
        stage_ready, chunks_used = sem("stage_ready"), sem("chunks_used")
        oh_fast, ev_fast = sems("oh_fast", 2), sems("ev_fast", 2)
        oh_gen, mm_gen, ev_gen, rk_gen = sems("oh_gen", 2), sems("mm_gen", 2), sems("ev_gen", 2), sems("rk_gen", 2)
        agg_done = sem("agg_done")
        x_in_sem = sems("x_in", 4)
        v_ready, v_turned, v_kept = sem("v_ready"), sem("v_turned"), sem("v_kept")
        hi_done, r1_done, mid_done, lo_done = sems("hi_done", 2), sems("r1_done", 2), sems("mid_done", 2), sems("lo_done", 2)
        stored = sems("stored", 4)
        lin_done, lin_scaled, lin_biased = sems("lin_done", 2), sems("lin_scaled", 2), sems("lin_biased", 2)
        bn_var, bn_sd, bn_ready = sem("bn_var"), sem("bn_sd"), sem("bn_ready")
        relu_done, y_ready, y_kept, y_turned = sem("relu_done"), sem("y_ready"), sem("y_kept"), sem("y_turned")
        x1_out = sems("x1_out", 2)
        xhat_done, zb_done, z_turned, x1_done = sem("xhat_done"), sem("zb_done"), sem("z_turned"), sem("x1_done")
        var_done, sd_done, rstd_ready, x_turned, xfT_done = sem("var_done"), sem("sd_done"), sem("rstd_ready"), sem("x_turned"), sem("xfT_done")
        rh_done, rhT_done, lg_mm, lg_read = sem("rh_done"), sem("rhT_done"), sem("lg_mm"), sem("lg_read")
        sh_done, ex_done, gap_done, e2_done = sem("sh_done"), sem("ex_done"), sem("gap_done"), sem("e2_done")
        xf_done, z_added = sems("xf_done", 2), sem("z_added")
        st_done, var_chain, xf_chain, route_chain = sem("st_done"), sem("var_chain"), sem("xf_chain"), sem("route_chain")
        pos_done = sem("pos_done")
        mb_ready, ranked, run_ready, rows_ready = sem("mb_ready"), sem("ranked"), sem("run_ready"), sem("rows_ready")
        routed_out = sems("routed_out", XBUFS)
        ln_bias_ready = sem("ln_bias_ready")
        masks_made, ones_made, counted, fill_ready, filled = sem("masks_made"), sem("ones_made"), sem("counted"), sem("fill_ready"), sem("filled")
        tiles_known, rows_in = sem("tiles_known"), sems("rows_in", 2)
        tile_turned, xT_done, expert_a, expert_b = sem("tile_turned"), sem("xT_done"), sem("expert_a"), sem("expert_b")
        l1_done, l2_done, l3_done = sem("l1_done"), sem("l2_done"), sem("l3_done")
        h1_act, h1_dve, h2_act, h2_dve = sem("h1_act"), sem("h1_dve"), sem("h2_act"), sem("h2_dve")
        y_biased, y_weighted, ids_ready, added = sem("y_biased"), sem("y_weighted"), sem("ids_ready"), sems("added", 2)

        NCONST = 2 + 6
        NROUTER, NEXPERT = 4, 4 * NX + 2 * KH
        GATHERS = NG * CPG
        L1, L2 = 0, 1

        def nodes(ap, t):
            return ap[bass.ds(t * CH, CH), :].rearrange("(b p) f -> p b f", p=RB)

        def in_pairs(eng, body, last=PAIRS):
            for u in range(2):
                body(u, u)
            if last > 1:
                with eng.Fori(1, last) as i:
                    for u in range(2):
                        body(i * 2 + u, u)

        def turned_rows(q):
            return ps[0:RB, 2 * q:2 * q + 2, :].rearrange("p a (b f) -> p (a b) f", b=2)

        def in_fours(eng, body, first=0, last=NCH):
            for t in range(first, 4):
                body(t, t % 4)
            if NCH > 8:
                with eng.Fori(1, NCH // 4 - 1) as i:
                    for q in range(4):
                        body(i * 4 + q, q)
            for t in range(max(NCH - 4, 4), last):
                body(t, t % 4)

        def strides(eng, fours, end, middle=None):
            per = STRIDE // 4

            def stride(g):
                at = 0
                if isinstance(g, int) and g == 0:
                    fours(0)
                    at = 1
                for upto, then in ((per // 2, middle), (per, end)):
                    if upto > at:
                        hold(eng)
                        with eng.Fori(at, upto) as i:
                            fours(g * per + i)
                        at = upto
                    if then:
                        then(g)

            for g in range(3):
                stride(g)
            if STRIDES > 3:
                with eng.Fori(3, STRIDES) as g:
                    stride(g)

        deg_sums = ps[:, NT, 0:2 * (NHI + HWIN)].rearrange("p (j h) -> p j h", j=2)

        def last_banks(t):
            return 4 if t < STRIDES - 1 or (t - STRIDES) % 2 == 0 else 6

        def half(t, u):
            return (t - u) // 2 if isinstance(t, int) else t // 2

        def routing(eng, body):
            loops = max((PAIRS - 1) // XBUFS - 1, 0)
            for i in range(-1, XBUFS - 1):
                body(i, i % XBUFS, i + 1 < PAIRS, i + 2 < PAIRS)
            if loops:
                with eng.Fori(1, loops + 1) as j:
                    for k in range(XBUFS):
                        body(j * XBUFS + k - 1, (k - 1) % XBUFS, True, True)
            for i in range(XBUFS - 1 + loops * XBUFS, PAIRS):
                body(i, i % XBUFS, i + 1 < PAIRS, i + 2 < PAIRS)

        def tiles(eng, body):
            for u in range(2):
                body(u, u, TILES > u + 1, TILES > u + 2)
            if TILES > 4:
                with eng.Fori(1, TILES // 2 - 1) as i:
                    for u in range(2):
                        body(i * 2 + u, u, True, True)
            body(TILES - 2, 0, True, False)
            body(TILES - 1, 1, False, False)

        block = ctx.enter_context(nc.Block())

        @block.sync
        def _(sp):
            sp.dma_start(dst_i, dst.rearrange("(t q e) -> q t e", q=P, e=GE)).then_inc(edges_in, 16)
            sp.dma_start(src_i, src.rearrange("(t q e) -> q t e", q=P, e=GE)).then_inc(edges_in, 16)
            for n, w in enumerate((W1, W2)):
                sp.dma_start(wconv[:, n, :, :], w.rearrange("(k p) n -> p k n", p=P)).then_inc(consts_in, 16)
            with nc.allow_non_contiguous_dma(reason="small vectors, one feature a partition"):
                for n, v in enumerate((b1, gamma1, beta1, b2, gamma2, beta2)):
                    sp.dma_start(vec[:, n, :], v.rearrange("(k p) -> p k", p=P)).then_inc(consts_in, 16)

            sp.wait_ge(w_ready, 1)
            with nc.allow_non_contiguous_dma(reason="one window start a partition"):
                sp.dma_start(w_dram.rearrange("(t q) -> q t", q=P), w_int[:, :]).then_inc(w_row, 16)
            sp.wait_ge(w_row, 16)
            sp.dma_start(wrow[:, :], w_dram.rearrange("(o n) -> o n", o=1)).then_inc(w_row, 16)
            sp.dma_start(w_all, w_dram.rearrange("(o n) -> o n", o=1).to_broadcast([P, NT * P])).then_inc(w_row, 16)

            def stat_load(t, u):
                wait(sp, stats_done, t - 1)
                sp.dma_start(xbuf[0:RB, u, :, :], nodes(x, t)).then_inc(stat_x_in[u], 16)

            def late_load(n):
                sp.dma_start(x_late[:, bass.ds(n * BPC, BPC), :], nodes(x, EARLY + n)).then_inc(late_in, 16)

            for u in range(2):
                stat_load(u, u)
            with sp.Fori(1, LATE + 1) as i:
                for u in range(2):
                    stat_load(i * 2 + u, u)
                late_load(i - 1)
            if LATE + 1 < EARLY // 2:
                with sp.Fori(LATE + 1, EARLY // 2) as i:
                    for u in range(2):
                        stat_load(i * 2 + u, u)

            sp.wait_ge(dinv_ready, 1)
            sp.dma_start(dinv_dram.rearrange("(h l) -> h l", l=P), dg[:, :]).then_inc(dn_in, 16)
            sp.wait_ge(dn_in, 16)
            sp.dma_start(dn[:, :], dinv_dram.rearrange("(n p) -> n p", p=RB)).then_inc(dn_in, 16)

            sp.wait_ge(stats_done, EARLY)

            def v_load(t, q):
                wait(sp, v_turned, t - 3)
                wait(sp, r1_done[0], t - 3)
                sp.dma_start(v_row[q], nodes(x, t)).then_inc(x_in_sem[q], 16)

            def v_store(t, q):
                sp.wait_ge(lo_done[0], t + 1)
                sp.dma_start(nodes(t_dram[0], t), v_parts[q]).then_inc(stored[q], 16)

            for q in range(4):
                v_load(q, q)
            with sp.Fori(1, NCH // 4) as i:
                for q in range(4):
                    v_load(i * 4 + q, q)
                    v_store(i * 4 + q - 4, q)
            for q in range(4):
                v_store(NCH - 4 + q, q)

            for q in range(4):
                sp.wait_ge(stored[q], 16 * (NCH // 4))
            dinv_row = dinv_dram.rearrange("(o n) -> o n", o=1)

            DINV_STEP = 2 * STRIDE * CPG // NCH

            def dinv_load(t):
                wait(sp, chunks_used, t * DINV_STEP)
                sp.dma_start(dinvT[:, bass.ds(t * CH, CH)], dinv_row[:, bass.ds(t * CH, CH)].to_broadcast([P, CH])).then_inc(dinv_in, 16)

            dinv_load(0)
            with sp.Fori(1, NCH) as t:
                dinv_load(t)

            def y_store(t, q):
                sp.wait_ge(lo_done[1], t + 1)
                sp.dma_start(nodes(t_dram[1], t), y_parts[q]).then_inc(stored[q], 16)

            in_fours(sp, y_store)

            sp.wait_ge(lin_scaled[1], NCH)
            with nc.allow_non_contiguous_dma(reason="small vectors, one feature a partition"):
                sp.dma_start(rw1_sb, rw1.rearrange("(k p) n -> p k n", p=P)).then_inc(router_in, 16)
                sp.dma_start(rb1_sb, rb1.rearrange("(p o) -> p o", o=1)).then_inc(router_in, 16)
                sp.dma_start(rw2_sb, rw2).then_inc(router_in, 16)
                sp.dma_start(rb2_sb, rb2.rearrange("(o n) -> o n", o=1).to_broadcast([RB, NX])).then_inc(router_in, 16)

            def x_load(t, q):
                wait(sp, x1_done, t - 3)
                sp.dma_start(x_in[q // 2][q % 2], nodes(x, t)).then_inc(x_in_sem[q], 16)

            def x1_store(t, u):
                sp.wait_ge(x1_done, t + 1)
                sp.dma_start(nodes(out, t), rbuf[0:RB, u, :, :]).then_inc(x1_out[u], 16)

            for q in range(4):
                x_load(q, q)
            with sp.Fori(1, NCH // 4) as i:
                for q in range(4):
                    x_load(i * 4 + q, q)
                    x1_store(i * 4 + q - 4, q % 2)
            sp.wait_ge(zb_done, WX_CHUNKS)
            for e in range(NX):
                for w, at in ((ew1, 0), (ew2, KH * D), (ew3, EA)):
                    sp.dma_start(wx[:, e, at:at + KH * D].rearrange("p (k n) -> p k n", k=KH),
                                 w[e, :, :].rearrange("(k p) n -> p k n", p=P)).then_inc(experts_in, 16)
                sp.dma_start(wx[:, e, EA + KH * D:EA + EB], eb3[e:e + 1, :].to_broadcast([P, D])).then_inc(experts_in, 16)
            with nc.allow_non_contiguous_dma(reason="small vectors, one feature a partition"):
                for b_d, at in ((eb1, 2 * KH * D), (eb2, 2 * KH * D + KH)):
                    for k in range(KH):
                        sp.dma_start(wx[:, :, at + k], b_d[:, k * P:(k + 1) * P].rearrange("e p -> p e")).then_inc(experts_in, 16)
            for q in range(4):
                x1_store(NCH - 4 + q, q % 2)

            sp.wait_ge(tiles_known, 1)
            tails = [sp.value_load(tail_int[0:1, e:e + 1], min_val=e * XR, max_val=e * XR + NPAD) for e in range(NX)]
            sp.wait_ge(fill_ready, 1)
            whole = "(p b) f -> p (b f)"
            fill_flat = fill.rearrange("p b f -> p (b f)")
            sp.dma_start(out[NPAD:NPAD + P, :], fill[:, 0, 0:D]).then_inc(filled, 16)
            sp.dma_start(routed[NX * XR:NX * XR + TOK, :].rearrange(whole, b=TB), fill_flat).then_inc(filled, 16)
            for tail in tails:
                sp.dma_start(routed[bass.ds(tail, TOK), :].rearrange(whole, b=TB), fill_flat).then_inc(filled, 16)
            sp.wait_ge(filled, 16 * (NX + 2))
            for q in range(XBUFS):
                sp.wait_ge(routed_out[q], 16 * 2 * B2 * len(range(q, PAIRS, XBUFS)))

            def tile_load(s, u):
                wait(sp, tile_turned, s - 1)
                wait(sp, ids_ready, s - 1)
                hold(sp)
                at = sp.value_load(tile_at_int[0:1, bass.ds(s, 1)], min_val=0, max_val=NX * XR)
                sp.dma_start(tile_rows[u].rearrange("p b f -> p (b f)"),
                             routed[bass.ds(at, TOK), :].rearrange(whole, b=TB)).then_inc(rows_in[u], 16)

            in_pairs(sp, tile_load, TILES // 2)
            for u in range(2):
                sp.wait_ge(added[u], 16 * TB * TILES // 2)

        @block.gpsimd
        def _(pool):
            pool.memset(ident[:, :], 0.0).then_inc(ident_ready, 1)
            pool.iota(iota_i, pattern=[[1, GWIN]], base=0, channel_multiplier=0).then_inc(iota_ready, 1)
            pool.iota(group_i, pattern=[[P, NT]], base=0, channel_multiplier=1).then_inc(group_ready, 1)
            pool.wait_ge(ident_ready, 1)
            pool.affine_select(out=ident[:, :], in_=ident[:, :], compare_op=ALU.not_equal, fill=1.0, base=0,
                               pattern=[[-1, P]], channel_multiplier=1).then_inc(ident_ready, 1)
            pool.memset(zeros_bf, 0.0).then_inc(ident_ready, 1)
            pool.wait_ge(span_ready, 1)
            pool.partition_all_reduce(flags[:, 1:2], flags[:, 0:1], P, RMAX).then_inc(span_all, 1)
            pool.wait_ge(deg_total, 1)
            pool.partition_all_reduce(deg_check[:, 1:2], deg_check[:, 0:1], P, RADD).then_inc(deg_checked, 1)

            def gathers(layer):
                done = layer * GATHERS
                for q in range(4):
                    pool.wait_ge(stored[q], 16 * (NCH // 4) * (layer + 1))

                def gather(i, u, first):
                    c0 = i * (2 * SLOTS) + u * SLOTS
                    pool.wait_ge(stage_ready, i * 2 + u + 1 + done // SLOTS)
                    for s in range(SLOTS):
                        wait(pool, chunks_used, c0 + s - SLOTS + 1 + done)
                        hold(pool)
                        pool.indirect_dma_start(
                            out=slots[:, s, :], out_offset=None, in_=t_dram[layer],
                            in_offset=bass.IndirectOffsetOnAxis(ap=idx_stage[:, u, s:s + 1], axis=0),
                        ).then_inc(got[s], 16)

                for u in range(2):
                    gather(0, u, True)
                if GATHERS > 2 * SLOTS:
                    with pool.Fori(1, GATHERS // (2 * SLOTS)) as i:
                        for u in range(2):
                            gather(i, u, False)

            gathers(L1)

            def keep_y(t, u):
                pool.wait_ge(y_ready, t + 1)
                hold(pool)
                pool.tensor_copy(acc[:, :, bass.ds(t * CH, CH)], ybuf[u]).then_inc(y_kept, 1)

            in_pairs(pool, keep_y)
            gathers(L2)

            pool.wait_ge(agg_done, 2)
            pool.iota(iota_pb, pattern=[[RB, B2]], base=0, channel_multiplier=1).then_inc(masks_made, 1)
            pool.memset(tri_f, 1.0).then_inc(masks_made, 1)
            pool.wait_ge(masks_made, 2)
            pool.affine_select(out=tri_f, in_=tri_f, compare_op=ALU.is_gt, fill=0.0, base=0, pattern=[[1, RB]],
                               channel_multiplier=-1).then_inc(masks_made, 1)

            def route(i, q):
                pool.wait_ge(rows_ready, i + 1)
                hold(pool)
                for c in range(2):
                    for b in range(B2):
                        pool.indirect_dma_start(
                            out=routed, out_offset=bass.IndirectOffsetOnAxis(ap=addr_int[:, q, c, b:b + 1], axis=0),
                            in_=xrow[q][:, b, :], in_offset=None).then_inc(routed_out[q], 16)

            with pool.Fori(0, PAIRS // XBUFS) as j:
                for q in range(XBUFS):
                    route(j * XBUFS + q, q)
            for i in range(PAIRS - PAIRS % XBUFS, PAIRS):
                route(i, i % XBUFS)

            for u in range(2):
                pool.wait_ge(x1_out[u], 16 * PAIRS)

            def add_rows(s, u):
                pool.wait_ge(y_weighted, s + 1)
                wait(pool, added[1 - u], 16 * TB * (half(s - 1, 1 - u) + 1) if not isinstance(s, int) or s > 0 else 0)
                hold(pool)
                for b in range(TB):
                    pool.indirect_dma_start(
                        out=out, out_offset=bass.IndirectOffsetOnAxis(ap=out_idx[:, u, b:b + 1], axis=0),
                        in_=yrow[u][:, b, :], in_offset=None, compute_op=ALU.add).then_inc(added[u], 16)
                    pool.wait_ge(added[u], 16 * TB * half(s, u) + 16 * b + 16)
                    hold(pool)

            in_pairs(pool, add_rows, TILES // 2)

        @block.scalar
        def _(act):
            act.wait_ge(dst_turned, 1)
            for n in range(NT):
                ng = min(P, TG - n * P)
                turned = ps[:, NT + n, :].rearrange("p (j g) -> p g j", j=CPG)
                last = act.activation(src3[:, n * P:n * P + ng, :], turned[:, 0:ng, :], ACT.Copy)
            last.then_inc(src_kept, 1)
            unused = rbuf[0:RB, 0, :, :]

            row_steps = Chain(act, row_chain)

            def row_stats(t, u):
                row_steps.begin(t * 3)
                act.wait_ge(stat_x_in[u], 16 * (half(t, u) + 1))
                wait(act, stats_done, t)
                hold(act)
                for b in range(BPC):
                    last = act.activation(unused[:, b, :], xbuf[0:RB, u, b, :], ACT.Identity, accum_out=ln_part[:, 0, b:b + 1])
                row_steps.step(last)
                hold(act)
                act.activation(ln_mean[:, bass.ds(t * BPC, BPC)], ln_part[:, 0, :], ACT.Copy, scale=1.0 / D)
                row_steps.step(act.activation(ln_part[:, 1, :], ln_part[:, 0, :], ACT.Copy, scale=-1.0 / D))
                hold(act)
                for b in range(BPC):
                    last = act.activation(unused[:, b, :], xbuf[0:RB, u, b, :], ACT.Square, bias=ln_part[:, 1, b:b + 1],
                                          accum_out=ln_part[:, 2, b:b + 1])
                row_steps.step(last)
                hold(act)
                act.activation(ln_tmp[:, 0, bass.ds(t * BPC, BPC)], ln_part[:, 2, :], ACT.Copy, scale=1.0 / D).then_inc(stats_done, 1)

            in_pairs(act, row_stats, EARLY // 2)
            act.wait_ge(root_wanted, 1)
            act.activation(dg, dg, ACT.Sqrt).then_inc(root_done, 1)
            act.wait_ge(root_wanted, 2)
            act.activation(ln_rstd[:, :], ln_tmp[:, 0, :], ACT.Sqrt).then_inc(root_done, 1)

            def v_high(t, q):
                act.wait_ge(v_ready, t + 1)
                wait(act, stored[q], 16 * (t // 4))
                hold(act)
                act.activation(v_parts[q][:, :, 0:D], v_row[q], ACT.Copy).then_inc(hi_done[0], 1)

            def v_middle(t, q):
                act.wait_ge(r1_done[0], t + 1)
                hold(act)
                act.activation(v_parts[q][:, :, D:2 * D], v_left[q], ACT.Copy).then_inc(mid_done[0], 1)

            def v_keep(t, q):
                act.wait_ge(v_turned, t + 1)
                hold(act)
                act.activation(acc[:, :, bass.ds(t * CH, CH)], ps[:, 2 * q:2 * q + KH, 0:CH], ACT.Copy).then_inc(v_kept, 1)

            def v_step(t, q):
                ends = isinstance(t, int)
                if not ends or t > 0:
                    v_middle(t - 1, (q - 1) % 4)
                if not ends or t + 1 < NCH:
                    v_high(t + 1, (q + 1) % 4)
                v_keep(t, q)

            v_high(0, 0)
            in_fours(act, v_step)
            v_middle(NCH - 1, 3)

            def aggregate(layer):
                done = layer * GATHERS

                def stage(i, u):
                    wait(act, chunks_used, (i - 1) * (2 * SLOTS) + u * SLOTS + SLOTS + done)
                    hold(act)
                    act.activation(idx_stage[:, u, :], srcidx[:, bass.ds(i * (2 * SLOTS) + u * SLOTS, SLOTS)],
                                   ACT.Copy).then_inc(stage_ready, 1)

                def stages(i):
                    for u in range(2):
                        stage(i, u)

                def add_bias(t):
                    act.wait_ge(lin_scaled[layer], t + 1)
                    hold(act)
                    for k in range(KH):
                        last = act.activation(acc[:, k, bass.ds(t * CH, CH)], lin_tmp[:, k, :], ACT.Identity,
                                              bias=vec[:, 3 * layer, k:k + 1])
                    last.then_inc(lin_biased[layer], 1)

                def stride_end(g):
                    if not isinstance(g, int) or g >= 3:
                        add_bias(g - 3)

                with act.If(bad == 0):
                    strides(act, stages, stride_end)
                    for t in range(max(STRIDES - 3, 0), NCH):
                        add_bias(t)
                with act.Else():
                    stages(0)
                    with act.Fori(1, NG // 4) as i:
                        stages(i)
                    with act.Fori(0, NCH) as t:
                        add_bias(t)

                act.wait_ge(bn_var, layer + 1)
                act.activation(bn_sc[:, 0, :], bn_sc[:, 1, :], ACT.Sqrt).then_inc(bn_sd, 1)

            act.wait_ge(src_kept, 1)
            act.wait_ge(consts_in, 16 * NCONST)
            act.wait_ge(flag_ready, 1)
            bad = act.value_load(bad_int[0:1, 0:1], min_val=0, max_val=1)
            aggregate(L1)
            act.wait_ge(bn_ready, 1)

            def relu(t):
                for k in range(KH):
                    part = acc[:, k, bass.ds(t * CH, CH)]
                    last = act.activation(part, part, ACT.Relu, bias=bn_sc[:, 3, k:k + 1], scale=bn_sc[:, 2, k:k + 1])
                last.then_inc(relu_done, 1)

            def y_step(t, q):
                ends = isinstance(t, int)
                if not ends or t > 0:
                    act.wait_ge(r1_done[1], t)
                    hold(act)
                    act.activation(y_parts[(q - 1) % 4][:, :, D:2 * D], turned_rows((q - 1) % 4), ACT.Copy).then_inc(mid_done[1], 1)
                act.wait_ge(y_turned, t + 1)
                wait(act, stored[q], 16 * (NCH // 4 + t // 4))
                hold(act)
                act.activation(y_parts[q][:, :, 0:D], turned_rows(q), ACT.Copy).then_inc(hi_done[1], 1)
                if not ends or t + 2 < NCH:
                    relu(t + 2)

            relu(0)
            relu(1)
            in_fours(act, y_step)
            act.wait_ge(r1_done[1], NCH)
            act.activation(y_parts[3][:, :, D:2 * D], turned_rows(3), ACT.Copy).then_inc(mid_done[1], 1)

            aggregate(L2)
            act.wait_ge(bn_ready, 2)
            act.wait_ge(router_in, 16 * NROUTER)

            act.wait_ge(ln_bias_ready, 1)

            def norm_x(t, u, par):
                act.wait_ge(x_in_sem[par * 2 + u], 16 * (NCH // 4 + t // 4 + 1))
                wait(act, x1_done, t - 1)
                hold(act)
                for b in range(BPC):
                    at = t * BPC + b
                    last = act.activation(xhat[u][:, b, :], x_in[par][u][:, b, :], ACT.Identity,
                                          bias=ln_bias[:, bass.ds(at, 1)], scale=ln_rstd[:, bass.ds(at, 1)])
                last.then_inc(xhat_done, 1)

            def norm_x1(p, q):
                act.wait_ge(rstd_ready, p + 1)
                wait(act, routed_out[q], 16 * 2 * B2 * (p // XBUFS))
                hold(act)
                for b in range(BPC):
                    at = BPC + b
                    last = act.activation(xrow[q][:, at, 0:D], rbuf[0:RB, 1, b, :], ACT.Identity,
                                          bias=shift8[:, at:at + 1], scale=rstd8[:, at:at + 1])
                last.then_inc(xf_done[1], 1)

            def batch_norm2(t, u):
                wait(act, z_turned, t - 1)
                hold(act)
                for k in range(KH):
                    last = act.activation(zb[u][:, k, :], acc[:, k, bass.ds(t * CH, CH)], ACT.Identity,
                                          bias=bn_sc[:, 3, k:k + 1], scale=bn_sc[:, 2, k:k + 1])
                last.then_inc(zb_done, 1)

            def keep_xfT(t):
                wait(act, rh_done, t)
                act.wait_ge(x_turned, t + 1)
                hold(act)
                act.activation(xfT, ps[:, 4:4 + KH, 0:CH], ACT.Copy).then_inc(xfT_done, 1)

            def router_hidden(t):
                wait(act, lg_mm, t)
                act.wait_ge(rh_done, t + 1)
                hold(act)
                act.activation(rhT, ps[:, 6, 0:CH], ACT.Relu, bias=rb1_sb[:, 0:1]).then_inc(rhT_done, 1)

            def route(i, q, next1, next2):
                a, small = i * 2 + 2, not isinstance(i, int) or i >= 0
                if next2:
                    norm_x(a + 2, 0, q % 2)
                    batch_norm2(a + 2, 0)
                if next1:
                    act.wait_ge(var_done, i + 2)
                    hold(act)
                    act.activation(sd8, var8, ACT.Sqrt).then_inc(sd_done, 1)
                if small:
                    act.wait_ge(sh_done, i + 1)
                    hold(act)
                    act.activation(ex, lg, ACT.Exp).then_inc(ex_done, 1)
                if next1:
                    norm_x1(i + 1, (q + 1) % XBUFS)
                if next1:
                    keep_xfT(a)
                if small:
                    act.wait_ge(gap_done, i + 1)
                    hold(act)
                    act.activation(e2, gap, ACT.Exp).then_inc(e2_done, 1)
                if next2:
                    norm_x(a + 3, 1, q % 2)
                    batch_norm2(a + 3, 1)
                if next1:
                    router_hidden(a)
                    keep_xfT(a + 1)
                    router_hidden(a + 1)

            for u in range(2):
                norm_x(u, u, 0)
                batch_norm2(u, u)
            routing(act, route)

            act.wait_ge(experts_in, 16 * NEXPERT)
            act.wait_ge(tiles_known, 1)

            def take_expert(s, u, part):
                done = (expert_a, expert_b)[part]
                if part == 0:
                    wait(act, l2_done, 2 * s - 2)
                    wait(act, h2_dve, s - 1)
                    wait(act, h2_act, s - 1)
                else:
                    wait(act, y_biased, s - 1)
                hold(act)
                e = act.value_load(tile_e_int[0:1, bass.ds(s, 1)], min_val=0, max_val=NX - 1)
                c0, c1 = ((0, EA), (EA, EA + EB))[part]
                hold(act)
                act.activation(we[u][:, c0:c1].unsqueeze(1), wx[:, bass.ds(e, 1), c0:c1], ACT.Copy).then_inc(done, 1)

            def keep_xT(s):
                wait(act, l1_done, 2 * s)
                act.wait_ge(tile_turned, s + 1)
                hold(act)
                act.activation(xT, ps[:, 0:KH, :], ACT.Copy).then_inc(xT_done, 1)

            def hidden(layer, s, u):
                done, used, hT, bank, out_sem = ((l1_done, (l2_done, 2 * s), h1T, 2, h1_act),
                                                 (l2_done, (l3_done, s), h2T, 4, h2_act))[layer]
                wait(act, *used)
                act.wait_ge(done, 2 * s + 1)
                hold(act)
                bias = we[u][:, 2 * KH * D + layer * KH:2 * KH * D + layer * KH + 1]
                act.activation(hT[:, 0, :], ps[:, bank, :], ACT.Relu, bias=bias).then_inc(out_sem, 1)

            def tile(s, u, next1, next2):
                hidden(1, s, u)
                if next2:
                    take_expert(s + 2, u, 0)
                if next1:
                    hidden(0, s + 1, 1 - u)
                    take_expert(s + 1, 1 - u, 1)
                if next2:
                    keep_xT(s + 2)

            take_expert(0, 0, 0)
            take_expert(1, 1, 0)
            take_expert(0, 0, 1)
            keep_xT(0)
            hidden(0, 0, 0)
            keep_xT(1)
            tiles(act, tile)

        @block.vector
        def _(dve):
            chain = Chain(dve, dve_chain)
            step = chain.step
            dve.wait_ge(iota_ready, 1)
            dve.tensor_copy(iota_bf[:, :], iota_i).then_inc(iota_bf_ready, 1)

            dve.wait_ge(edges_in, 32)
            dve.tensor_copy(src_f, src_i)
            step(dve.tensor_copy(dst_f, dst_i))
            dve.memset(marker[:, 0, 3:4], 0.0).then_inc(edges_ready, 1)
            step(dve.tensor_scalar(tmp_f, dst_f, 0.0, BIG, ALU.is_lt, ALU.mult))
            step(dve.tensor_tensor(tmp_f, tmp_f, dst_f, ALU.add))
            step(dve.tensor_reduce(wlo[:, :], tmp_f, AX.X, ALU.min))
            step(dve.tensor_reduce(whi[:, :], dst_f, AX.X, ALU.max))
            step(dve.tensor_scalar(wlo[:, :], wlo[:, :], float(WMAX), None, ALU.min))
            step(dve.tensor_tensor(whi[:, :], whi[:, :], wlo[:, :], ALU.subtract))
            dve.wait_ge(group_ready, 1)
            step(dve.tensor_copy(group_f, group_i))
            step(dve.tensor_scalar(group_lo, group_f, CH / STRIDE, -float(CH), ALU.mult, ALU.add))
            step(dve.tensor_scalar(group_lo, group_lo, float(WMAX), None, ALU.min))
            step(dve.tensor_tensor(group_lo, wlo[:, :], group_lo, ALU.is_lt))
            step(dve.scalar_tensor_tensor(out=whi[:, :], in0=group_lo, scalar=BIG, in1=whi[:, :], op0=ALU.mult, op1=ALU.add))
            dve.tensor_reduce(flags[:, 0:1], whi[:, :], AX.X, ALU.max).then_inc(span_ready, 1)
            dve.wait_ge(span_all, 1)
            step(dve.tensor_scalar(flags[:, 2:3], flags[:, 1:2], float(WIN), None, ALU.is_lt))
            step(dve.tensor_scalar(flags[:, 3:4], flags[:, 2:3], -1.0, 1.0, ALU.mult, ALU.add))
            dve.tensor_copy(bad_int[:, :], flags[:, 3:4]).then_inc(flag_ready, 1)
            step(dve.tensor_scalar(wlo[:, :], wlo[:, :], flags[:, 2:3], None, ALU.mult))
            dve.tensor_copy(w_int[:, :], wlo[:, :]).then_inc(w_ready, 1)
            def keep_table(table):
                for n in range(NT):
                    ng = min(P, TG - n * P)
                    turned = ps[:, n, :].rearrange("p (j g) -> p g j", j=CPG)
                    last = dve.tensor_copy(table[:, n * P:n * P + ng, :], turned[:, 0:ng, :])
                return last

            dve.wait_ge(dst_turned, 1)
            for n in range(NT):
                last = dve.tensor_scalar(dst_f[:, n, :], dst_f[:, n, :], wlo[:, n:n + 1], None, ALU.subtract)
            last.then_inc(rel_ready, 1)
            keep_table(dstT_i.rearrange("p (g j) -> p g j", j=CPG)).then_inc(dst_kept, 1)
            dve.wait_ge(dst_kept, 1)
            step(dve.tensor_scalar(digit_i, dstT_i, LOW - 1, None, ALU.bitwise_and))
            step(dve.tensor_copy(loT, digit_i))
            step(dve.tensor_scalar(digit_i, dstT_i, LOW.bit_length() - 1, None, ALU.arith_shift_right))
            dve.tensor_copy(hiT, digit_i)
            dve.wait_ge(iota_bf_ready, 1)
            dve.wait_ge(ident_ready, 2)
            dve.tensor_reduce(parity, ident[:, :].rearrange("p (l j) -> p j l", j=2), AX.X, ALU.add)
            step(dve.tensor_copy(iota_rep, iota_bf[:, 0:max(NHI, LOW)].unsqueeze(2).to_broadcast([P, max(NHI, LOW), DCH])))
            dve.wait_ge(tables_turned, 1)
            keep_table(rel3).then_inc(tables_ready, 1)
            dve.wait_ge(w_row, 48)
            first_w = w_all[:, 0:NG].rearrange("p (b g) -> p b g", g=BASE_GROUPS)[:, :, 0]
            step(dve.tensor_scalar(base_i, first_w, LOW.bit_length() - 1, None, ALU.arith_shift_right))
            step(dve.tensor_copy(base_f, base_i))
            by_base = "p (b c) -> p b c"
            dve.tensor_tensor(hrT[:, 0:NG * CPG].rearrange(by_base, b=NBASE), hiT[:, 0:NG * CPG].rearrange(by_base, b=NBASE),
                              base_f.unsqueeze(2).to_broadcast([P, NBASE, DBASE * DCH]), ALU.subtract).then_inc(base_ready, 1)
            dve.wait_ge(base_ready, 1)

            def deg_step(d, u, high, oh, before):
                wait(dve, deg_summed, before)
                width = oh.shape[1]
                here = bass.ds(d * DCH, DCH)
                pairs = [P, DCH // 2, LOW, 2]
                dve.tensor_tensor(oh_lo[u], iota_rep[:, 0:LOW, 0:2].unsqueeze(1).to_broadcast(pairs),
                                  loT[:, here].rearrange("p (a j) -> p a j", j=2).unsqueeze(2).to_broadcast(pairs), ALU.is_equal)
                dve.tensor_tensor(oh, iota_rep[:, 0:width, :],
                                  high[:, here].unsqueeze(1).to_broadcast([P, width, DCH]), ALU.is_equal).then_inc(deg_onehot, 1)

            def fast_steps(b):
                for u in range(DBASE):
                    d = b * DBASE + u
                    deg_step(d, u, hrT, oh_win[u], d - DBASE + 1)

            fast_steps(0)
            if NBASE > 1:
                with dve.Fori(1, NBASE) as b:
                    fast_steps(b)
            dve.wait_ge(deg_summed, DSTEPS + 1)
            step(dve.tensor_reduce(pair_total, deg_sums, AX.X, ALU.add))
            step(dve.tensor_tensor(pair_total, pair_total, parity, ALU.mult))
            dve.tensor_reduce(deg_check[:, 0:1], pair_total, AX.X, ALU.add).then_inc(deg_total, 1)
            dve.wait_ge(deg_checked, 1)
            step(dve.tensor_scalar(deg_check[:, 2:3], deg_check[:, 1:2], float(E), None, ALU.not_equal))
            dve.tensor_copy(deg_bad, deg_check[:, 2:3]).then_inc(deg_flag, 1)
            dve.wait_ge(deg_flag, 1)
            uncounted = dve.value_load(deg_bad[0:1, 0:1], min_val=0, max_val=1)
            with dve.If(uncounted == 1):
                in_pairs(dve, lambda d, u: deg_step(d, u, hiT, oh_hi[u], d + DSTEPS), DSTEPS // 2)
                dve.wait_ge(deg_summed, 2 * DSTEPS + 1)

            def mean_var(st, sm, df, m2, mean, var, step):
                step(dve.tensor_tensor(sm, st[:, :, 1], st[:, :, 4], ALU.add))
                step(dve.tensor_tensor(df, st[:, :, 1], st[:, :, 4], ALU.subtract))
                step(dve.tensor_tensor(m2, st[:, :, 2], st[:, :, 5], ALU.add))
                step(dve.tensor_scalar(mean, sm, 0.5, None, ALU.mult))
                step(dve.tensor_tensor(df, df, df, ALU.mult))
                step(dve.scalar_tensor_tensor(out=m2, in0=df, scalar=D / 4.0, in1=m2, op0=ALU.mult, op1=ALU.add))
                return dve.tensor_scalar(var, m2, 1.0 / D, EPS, ALU.mult, ALU.add)

            dve.tensor_copy(counted_in, deg_sums[:, :, 0:NHI]).then_inc(deg_kept, 1)
            dve.wait_ge(late_in, 16 * LATE)
            for b in range(LATE_BLOCKS // 2):
                dve.bn_stats(st_late[:, b, :], x_late[:, b, :])
            dve.wait_ge(dg_turned, 1)
            dve.tensor_scalar(dg, ps[0:NHI // 2, NT + 1, 0:P], 1.0, None, ALU.add).then_inc(root_wanted, 1)
            dve.wait_ge(root_done, 1)
            dve.reciprocal(dg, dg).then_inc(dinv_ready, 1)
            for b in range(LATE_BLOCKS // 2, LATE_BLOCKS):
                last = dve.bn_stats(st_late[:, b, :], x_late[:, b, :])
            step(last)
            step(mean_var(st_late, sum_late, dif_late, m2_late, ln_mean[:, NBLK - LATE_BLOCKS:NBLK],
                          ln_tmp[:, 0, NBLK - LATE_BLOCKS:NBLK], step))
            dve.wait_ge(stats_done, EARLY)
            early = ln_tmp[:, 0, 0:NBLK - LATE_BLOCKS]
            dve.tensor_scalar(early, early, EPS, None, ALU.add).then_inc(root_wanted, 1)
            dve.wait_ge(root_done, 2)
            step(dve.reciprocal(ln_rstd[:, :], ln_rstd[:, :]))

            dve.wait_ge(flag_ready, 1)
            dve.wait_ge(w_row, 48)
            bad = dve.value_load(bad_int[0:1, 0:1], min_val=0, max_val=1)

            def aggregate(run):
                def sums(at, width):
                    return acc[:, :, bass.ds(at, width)]

                def partial(u, width):
                    return ps[:, 2 * u:2 * u + KH, 0:width]

                def product_done(n):
                    wait(dve, chunks_used, n * CPG + run * GATHERS if not isinstance(n, int) or n > 0 else 0)

                def make_onehot(g, u):
                    for j in range(CPG):
                        last = dve.tensor_scalar(onehot[:, u, j, 0:WIN], iota_bf[:, 0:WIN],
                                                 relT[:, bass.ds(g * CPG + j, 1)], None, ALU.is_equal)
                    last.then_inc(oh_fast[run], 1)

                def fast(g, u):
                    product_done(g)
                    hold(dve)
                    make_onehot(g + 1, 1 - u)
                    w = dve.value_load(wrow[0:1, bass.ds(g, 1)], min_val=0, max_val=WMAX)
                    product_done(g + 1)
                    wait(dve, ev_fast[run], g)
                    dve.tensor_tensor(sums(w, WIN), sums(w, WIN), partial(u, WIN), ALU.add).then_inc(ev_fast[run], 1)

                def general(g):
                    dve.wait_ge(rk_gen[run], g * (NW + 1) + 1)
                    hold(dve)
                    dve.tensor_copy(relk[:, :], relT[:, bass.ds(g * CPG, CPG)]).then_inc(rk_gen[run], 1)
                    with dve.Fori(0, NW) as k:
                        s = g * NW + k
                        dve.wait_ge(rk_gen[run], g * (NW + 1) + k + 2)
                        dve.wait_ge(mm_gen[run], s + 1)
                        hold(dve)
                        for j in range(CPG):
                            last = dve.tensor_scalar(onehot[:, 0, j, :], iota_bf[:, :], relk[:, j:j + 1], None, ALU.is_equal)
                        last.then_inc(oh_gen[run], 1)
                        dve.wait_ge(oh_gen[run], s + 1)
                        dve.tensor_scalar(relk[:, :], relk[:, :], float(GWIN), None, ALU.subtract).then_inc(rk_gen[run], 1)
                        dve.wait_ge(mm_gen[run], s + 2)
                        dve.wait_ge(ev_gen[run], s + 1)
                        hold(dve)
                        dve.tensor_tensor(sums(k * GWIN, GWIN), sums(k * GWIN, GWIN), partial(0, GWIN),
                                          ALU.add).then_inc(ev_gen[run], 1)
                    dve.memset(marker[:, run, 2:3], 0.0).then_inc(chunks_used, CPG)

                def scale(t, bank=4):
                    dve.wait_ge(dinv_in, 16 * NCH)
                    dve.wait_ge(lin_done[run], t + 1)
                    wait(dve, lin_biased[run], t)
                    hold(dve)
                    part = dinvT[:, bass.ds(t * CH, CH)].unsqueeze(1).to_broadcast([P, KH, CH])
                    dve.tensor_tensor(lin_tmp, ps[:, bank:bank + KH, 0:CH], part, ALU.mult).then_inc(lin_scaled[run], 1)

                def stats(t, width=CH):
                    dve.wait_ge(lin_biased[run], t + 1)
                    hold(dve)
                    for k in range(KH):
                        last = dve.bn_stats(bnst[:, k, bass.ds(t, 1), :].rearrange("p o s -> p (o s)"),
                                            acc[:, k, bass.ds(t * CH, width)])
                    return last

                def fours(i):
                    for q in range(4):
                        fast(i * 4 + q, q % 2)

                def stride_end(g):
                    if not isinstance(g, int) or g >= 2:
                        scale(g - 2)
                    if not isinstance(g, int) or g >= 3:
                        stats(g - 3)

                with dve.If(bad == 0):
                    make_onehot(0, 0)
                    strides(dve, fours, stride_end)
                    dve.wait_ge(ev_fast[run], NG)
                    dve.memset(marker[:, run, 3:4], 0.0).then_inc(agg_done, 1)
                    for t in range(max(STRIDES - 2, 0), NCH):
                        if t > 0:
                            stats(t - 1)
                        scale(t, last_banks(t))
                with dve.Else():
                    dve.memset(marker[:, run, 0:1], 0.0).then_inc(mm_gen[run], 1)
                    dve.memset(marker[:, run, 1:2], 0.0).then_inc(ev_gen[run], 1)
                    dve.memset(marker[:, run, 4:5], 0.0).then_inc(rk_gen[run], 1)
                    with dve.Fori(0, NG) as g:
                        general(g)
                    dve.wait_ge(ev_gen[run], NG * NW + 1)
                    dve.memset(marker[:, run, 3:4], 0.0).then_inc(agg_done, 1)
                    scale(0)
                    with dve.Fori(1, NCH) as t:
                        stats(t - 1)
                        scale(t)

                step(stats(NCH - 1, TAIL))
                for k in range(KH):
                    last = dve.bn_aggr(bn_mv[:, k, :], bnst[:, k, :, :].rearrange("p t s -> p (t s)"))
                step(last)
                dve.tensor_scalar(bn_sc[:, 1, :], bn_mv[:, :, 1], EPS, None, ALU.add).then_inc(bn_var, 1)
                dve.wait_ge(bn_sd, run + 1)
                step(dve.reciprocal(bn_sc[:, 1, :], bn_sc[:, 0, :]))
                step(dve.tensor_tensor(bn_sc[:, 2, :], vec[:, 3 * run + 1, :], bn_sc[:, 1, :], ALU.mult))
                step(dve.tensor_tensor(bn_sc[:, 3, :], bn_mv[:, :, 0], bn_sc[:, 2, :], ALU.mult))
                dve.tensor_tensor(bn_sc[:, 3, :], vec[:, 3 * run + 2, :], bn_sc[:, 3, :], ALU.subtract).then_inc(bn_ready, 1)

            dve.wait_ge(dn_turned, 1)
            step(dve.tensor_copy(dcol[:, :], ps[0:RB, 7, 0:NBLK]))
            step(dve.tensor_tensor(dcol[:, :], dcol[:, :], ln_rstd[:, :], ALU.mult))

            def v_rows(t, q):
                dve.wait_ge(x_in_sem[q], 16 * (t // 4 + 1))
                hold(dve)
                for b in range(BPC):
                    at = t * BPC + b
                    last = dve.tensor_scalar(v_row[q][:, b, :], v_row[q][:, b, :], ln_mean[:, bass.ds(at, 1)],
                                             dcol[:, bass.ds(at, 1)], ALU.subtract, ALU.mult)
                last.then_inc(v_ready, 1)

            def v_rest(t, q):
                dve.wait_ge(hi_done[0], t + 1)
                wait(dve, lo_done[0], t - 3)
                dve.tensor_tensor(v_left[q], v_row[q], v_parts[q][:, :, 0:D], ALU.subtract).then_inc(r1_done[0], 1)

            def v_low(t, q):
                dve.wait_ge(mid_done[0], t + 1)
                dve.tensor_tensor(v_parts[q][:, :, 2 * D:3 * D], v_left[q], v_parts[q][:, :, D:2 * D],
                                  ALU.subtract).then_inc(lo_done[0], 1)

            def v_step(t, q):
                ends = isinstance(t, int)
                if not ends or t + 1 < NCH:
                    v_rows(t + 1, (q + 1) % 4)
                v_rest(t, q)
                if not ends or t > 0:
                    v_low(t - 1, (q - 1) % 4)

            v_rows(0, 0)
            in_fours(dve, v_step)
            v_low(NCH - 1, 3)

            dve.wait_ge(consts_in, 16 * NCONST)
            dve.wait_ge(v_kept, NCH)
            aggregate(L1)

            def y_cols(t, u):
                dve.wait_ge(relu_done, t + 1)
                wait(dve, y_turned, t - 1)
                wait(dve, y_kept, t - 1)
                dve.tensor_tensor(ybuf[u], acc[:, :, bass.ds(t * CH, CH)],
                                  dinvT[:, bass.ds(t * CH, CH)].unsqueeze(1).to_broadcast([P, KH, CH]), ALU.mult).then_inc(y_ready, 1)

            def y_low(t, q):
                dve.wait_ge(mid_done[1], t + 1)
                hold(dve)
                dve.tensor_tensor(y_parts[q][:, :, 2 * D:3 * D], turned_rows(q), y_parts[q][:, :, D:2 * D], ALU.subtract).then_inc(lo_done[1], 1)

            def y_step(t, q):
                ends = isinstance(t, int)
                if not ends or t + 1 < NCH:
                    y_cols(t + 1, (q + 1) % 2)
                if not ends or t > 0:
                    y_low(t - 1, (q - 1) % 4)
                dve.wait_ge(hi_done[1], t + 1)
                hold(dve)
                dve.tensor_tensor(turned_rows(q), turned_rows(q), y_parts[q][:, :, 0:D], ALU.subtract).then_inc(r1_done[1], 1)

            y_cols(0, 0)
            in_fours(dve, y_step)
            y_low(NCH - 1, 3)

            dve.wait_ge(y_kept, NCH)
            aggregate(L2)

            step(dve.memset(run_bf, 0.0))
            dve.memset(ones_bf, 1.0).then_inc(ones_made, 1)
            dve.tensor_scalar(iota6, iota_bf[0:RB, 0:NX], float(NX), None, ALU.subtract)
            dve.tensor_scalar(region_start, iota_bf[0:RB, 0:NX], float(XR), None, ALU.mult)
            dve.wait_ge(masks_made, 3)
            dve.tensor_copy(tri_bf, tri_f)
            step(dve.tensor_copy(node_ids, iota_pb[0:RB, :]))
            dve.memset(marker[:, 0, 0:1], 0.0).then_inc(ones_made, 1)
            step(dve.tensor_tensor(ln_bias, ln_mean[:, :], ln_rstd[:, :], ALU.mult))
            dve.tensor_scalar(ln_bias, ln_bias, -1.0, None, ALU.mult).then_inc(ln_bias_ready, 1)
            dve.wait_ge(router_in, 16 * NROUTER)
            var_steps, xf_steps, route_steps = Chain(dve, var_chain), Chain(dve, xf_chain), Chain(dve, route_chain)
            VAR_STEPS, ROUTE_STEPS, PLACE_STEPS = 6, 21, 2

            def x1_rows(t, u, par):
                x1 = rbuf[0:RB, u, :, :]
                dve.wait_ge(xhat_done, t + 1)
                dve.wait_ge(z_turned, t + 1)
                rows = ps[0:RB, 2 * u:2 * u + 2, :].rearrange("p a (b f) -> p (a b) f", b=2)
                hold(dve)
                dve.tensor_tensor(xhat[u], rows, xhat[u], ALU.add).then_inc(z_added, 1)
                dve.wait_ge(z_added, t + 1)
                wait(dve, x1_out[u], 16 * half(t, u))
                wait(dve, xf_done[u], t // 2)
                hold(dve)
                dve.scalar_tensor_tensor(out=x1, in0=xhat[u], scalar=0.0, in1=x_in[par][u],
                                         op0=ALU.max, op1=ALU.add).then_inc(x1_done, 1)
                dve.wait_ge(x1_done, t + 1)
                hold(dve)
                for b in range(BPC):
                    last = dve.bn_stats(st8[:, u * BPC + b, :], x1[:, b, :])
                last.then_inc(st_done, 1)

            def row_vars(p):
                var_steps.begin(p * VAR_STEPS)
                dve.wait_ge(st_done, p * 2 + 2)
                mean_var(st8, sum8, dif8, m28, mean8, var8, var_steps.step).then_inc(var_done, 1)
                assert var_steps.n == VAR_STEPS, var_steps.n

            def xf_rows(p, q):
                xf_steps.begin(p)
                dve.wait_ge(sd_done, p + 1)
                wait(dve, xf_done[1], p)
                hold(dve)
                xf_steps.step(dve.reciprocal(rstd8, sd8))
                dve.scalar_tensor_tensor(out=shift8, in0=mean8, scalar=-1.0, in1=rstd8, op0=ALU.mult, op1=ALU.mult).then_inc(rstd_ready, 1)
                wait(dve, routed_out[q], 16 * 2 * B2 * (p // XBUFS))
                hold(dve)
                for b in range(BPC):
                    last = dve.tensor_scalar(xrow[q][:, b, 0:D], rbuf[0:RB, 0, b, :], mean8[:, b:b + 1],
                                             rstd8[:, b:b + 1], ALU.subtract, ALU.mult)
                last.then_inc(xf_done[0], 1)

            rstep = route_steps.step

            def over(a):
                return a.to_broadcast([RB, B2, NX])

            def across(a):
                return a.unsqueeze(1).to_broadcast([RB, B2, NX])

            def flat(a):
                return a.rearrange("p b o -> p (b o)")

            def late(i):
                return not isinstance(i, int) or i < PAIRS - 3

            def route1(i):
                route_steps.begin(i * ROUTE_STEPS - (PLACE_STEPS if not isinstance(i, int) or i > 0 and late(i - 1) else 0))
                dve.wait_ge(lg_mm, i * 2 + 2)
                logits = ps[0:RB, 7, 0:B2 * 8].rearrange("p (b n) -> p b n", b=B2)[:, :, 0:NX]
                dve.tensor_tensor(lg, logits, across(rb2_sb), ALU.add).then_inc(lg_read, 1)
                dve.wait_ge(lg_read, i + 1)
                rstep(dve.tensor_reduce(flat(lmax), lg, AX.X, ALU.max))
                dve.tensor_tensor(lg, lg, over(lmax), ALU.subtract).then_inc(sh_done, 1)

            def best(values, largest, where, mask):
                rstep(dve.tensor_reduce(flat(largest), values, AX.X, ALU.max))
                rstep(dve.tensor_tensor(eq, values, over(largest), ALU.is_equal))
                rstep(dve.tensor_tensor(cand, eq, across(iota6), ALU.mult))
                rstep(dve.tensor_reduce(flat(where), cand, AX.X, ALU.min))
                rstep(dve.tensor_tensor(mask, across(iota6), over(where), ALU.is_equal))

            def route2(i):
                dve.wait_ge(ex_done, i + 1)
                rstep(dve.tensor_reduce(flat(lsum), ex, AX.X, ALU.add))
                rstep(dve.reciprocal(lrec, lsum))
                rstep(dve.tensor_tensor(prob, ex, over(lrec), ALU.mult))
                best(prob, pmax, which1, m1st)
                rstep(dve.scalar_tensor_tensor(out=rest, in0=m1st, scalar=-2.0, in1=prob, op0=ALU.mult, op1=ALU.add))
                best(rest, pmax2, which2, m2nd)
                dve.tensor_tensor(gap, pmax2, pmax, ALU.subtract).then_inc(gap_done, 1)
                dve.tensor_tensor(mb_bf, m1st, m2nd, ALU.add).then_inc(mb_ready, 1)

            def route3(i, q):
                dve.wait_ge(e2_done, i + 1)
                rstep(dve.tensor_scalar(den, e2, 1.0, None, ALU.add))
                rstep(dve.reciprocal(xrow[q][:, :, D + 1:D + 2], den))
                dve.tensor_tensor(xrow[q][:, :, D + 2:D + 3], e2, xrow[q][:, :, D + 1:D + 2], ALU.mult)
                dve.tensor_scalar(xrow[q][:, :, D + 3:D + 4], which1, float(NX), None, ALU.add)
                rstep(dve.tensor_copy(xrow[q][:, :, D:D + 1], node_ids.unsqueeze(2)))
                rstep(dve.tensor_scalar(node_ids, node_ids, float(2 * CH), None, ALU.add))

            def places(i):
                dve.wait_ge(ranked, i + 1)
                ranks = ps[0:RB, 7, RANKS:RANKS + B2 * NX].rearrange("p (b e) -> p b e", e=NX)
                dve.tensor_tensor(pos, ranks, across(region_start), ALU.add).then_inc(pos_done, 1)

            def route4(i, q):
                dve.wait_ge(pos_done, i + 1)
                dve.tensor_reduce(run_add, mb_bf.rearrange("p b e -> p e b"), AX.X, ALU.add)
                dve.tensor_tensor(at1, m1st, pos, ALU.mult)
                rstep(dve.tensor_tensor(at2, m2nd, pos, ALU.mult))
                dve.tensor_tensor(run_bf, run_bf, run_add, ALU.add).then_inc(run_ready, 1)
                dve.tensor_reduce(addr1, at1, AX.X, ALU.add)
                rstep(dve.tensor_reduce(addr2, at2, AX.X, ALU.add))
                dve.tensor_copy(addr_int[:, q, 0, :], addr1)
                dve.tensor_copy(addr_int[:, q, 1, :], addr2).then_inc(rows_ready, 1)

            def route(i, q, next1, next2):
                a, small = i * 2 + 2, not isinstance(i, int) or i >= 0
                if next1:
                    x1_rows(a, 0, 1 - q % 2)
                    x1_rows(a + 1, 1, 1 - q % 2)
                    row_vars(i + 1)
                if small:
                    route1(i)
                if not isinstance(i, int) or i > 0 and late(i - 1):
                    route4(i - 1, (q - 1) % XBUFS)
                if next1:
                    xf_rows(i + 1, (q + 1) % XBUFS)
                if small:
                    route2(i)
                    route3(i, q)
                    places(i)
                    if not late(i):
                        route4(i, q)
                    before = not isinstance(i, int) or i > 0 and late(i - 1)
                    assert route_steps.n == ROUTE_STEPS + PLACE_STEPS * (before - late(i))

            routing(dve, route)

            dve.wait_ge(zb_done, NCH)
            for e in range(NX):
                dve.memset(wx[:, e, EA - 1:EA], float(e))
            step(dve.memset(fill, 0.0))
            step(dve.tensor_scalar(fill[:, :, D:D + 1], iota_pb[:, 0:1].unsqueeze(1).to_broadcast([P, TB, 1]),
                                   float(NPAD), None, ALU.add))
            dve.memset(marker[:, 0, 4:5], 0.0).then_inc(fill_ready, 1)
            dve.wait_ge(counted, 1)
            dve.tensor_copy(count, ps[0:1, 7, 0:NX])
            dve.tensor_scalar(levels, iota_bf[0:1, 0:LEVELS], float(TOK), None, ALU.mult)
            step(dve.tensor_copy(tile_no, iota_bf[0:1, 0:TILES]))
            step(dve.tensor_tensor(reached, count.unsqueeze(2).to_broadcast([1, NX, LEVELS]),
                                   levels.unsqueeze(1).to_broadcast([1, NX, LEVELS]), ALU.is_gt))
            step(dve.tensor_reduce(n_tiles, reached, AX.X, ALU.add))
            step(dve.tensor_copy(last_tile, n_tiles))
            for e in range(1, NX):
                step(dve.tensor_tensor(last_tile[:, e:e + 1], last_tile[:, e - 1:e], last_tile[:, e:e + 1], ALU.add))
            dve.tensor_scalar(skip, n_tiles, -float(TOK), float(XR), ALU.mult, ALU.add)
            step(dve.tensor_tensor(behind, tile_no.unsqueeze(2).to_broadcast([1, TILES, NX]),
                                   last_tile.unsqueeze(1).to_broadcast([1, TILES, NX]), ALU.is_ge))
            step(dve.tensor_reduce(tile_e, behind, AX.X, ALU.add))
            step(dve.tensor_tensor(jump, behind, skip.unsqueeze(1).to_broadcast([1, TILES, NX]), ALU.mult))
            step(dve.tensor_reduce(tile_at, jump, AX.X, ALU.add))
            step(dve.scalar_tensor_tensor(out=tile_at, in0=tile_no, scalar=float(TOK), in1=tile_at, op0=ALU.mult, op1=ALU.add))
            step(dve.tensor_scalar(tile_at, tile_at, float(NX * XR), None, ALU.min))
            step(dve.tensor_scalar(tile_e, tile_e, float(NX - 1), None, ALU.min))
            step(dve.tensor_tensor(count, count, region_start[0:1, :], ALU.add))
            dve.tensor_copy(tail_int, count)
            dve.tensor_copy(tile_e_int, tile_e)
            dve.tensor_copy(tile_at_int, tile_at).then_inc(tiles_known, 1)

            def hidden(layer, s, u):
                done, used, hT, bank, out_sem = ((l1_done, (l2_done, 2 * s), h1T, 3, h1_dve),
                                                 (l2_done, (l3_done, s), h2T, 5, h2_dve))[layer]
                wait(dve, *used)
                dve.wait_ge(done, 2 * s + 2)
                bias = we[u][:, 2 * KH * D + layer * KH + 1:2 * KH * D + layer * KH + 2]
                dve.tensor_scalar(hT[:, 1, :], ps[:, bank, :], bias, 0.0, ALU.add, ALU.max).then_inc(out_sem, 1)

            def keep_ids(s, u):
                dve.wait_ge(rows_in[u], 16 * (half(s, u) + 1))
                dve.wait_ge(expert_a, s + 1)
                wait(dve, added[u], 16 * TB * half(s, u))
                hold(dve)
                columns = [tile_rows[u][:, :, D + n] for n in range(4)]
                number = we[u][:, EA - 1:EA]
                dve.scalar_tensor_tensor(out=wsel[:, u, :], in0=columns[3], scalar=number, in1=columns[1],
                                         op0=ALU.is_equal, op1=ALU.mult)
                dve.scalar_tensor_tensor(out=wsel2[:, u, :], in0=columns[3], scalar=number, in1=columns[2],
                                         op0=ALU.not_equal, op1=ALU.mult)
                dve.tensor_copy(out_idx[:, u, :], columns[0]).then_inc(ids_ready, 1)

            def y_rows(s, u):
                dve.wait_ge(ids_ready, s + 1)
                dve.tensor_tensor(wsel[:, u, :], wsel[:, u, :], wsel2[:, u, :], ALU.add)
                dve.wait_ge(l3_done, s + 1)
                wait(dve, added[u], 16 * TB * half(s, u))
                dve.wait_ge(expert_b, s + 1)
                rows = ps[:, 6:8, :].rearrange("p a (b f) -> p (a b) f", b=2)
                bias = we[u][:, EA + KH * D:EA + EB].unsqueeze(1).to_broadcast([P, TB, D])
                hold(dve)
                dve.tensor_tensor(yrow[u], rows, bias, ALU.add).then_inc(y_biased, 1)
                dve.wait_ge(y_biased, s + 1)
                hold(dve)
                for b in range(TB):
                    last = dve.tensor_scalar(yrow[u][:, b, :], yrow[u][:, b, :], wsel[:, u, b:b + 1], None, ALU.mult)
                last.then_inc(y_weighted, 1)

            def tile(s, u, next1, next2):
                hidden(1, s, u)
                if next1:
                    hidden(0, s + 1, 1 - u)
                y_rows(s, u)
                if next1:
                    keep_ids(s + 1, 1 - u)

            keep_ids(0, 0)
            hidden(0, 0, 0)
            tiles(dve, tile)

        @block.tensor
        def _(pe):
            def turn(out, in_, last_sem=None):
                n = in_.shape[0]
                return pe.transpose(out, in_, ident[0:n, 0:n])

            def turn_table(table, bank):
                for n in range(NT):
                    for j in range(CPG):
                        last = turn(ps[:, bank + n, j * P:(j + 1) * P], table[:, n, j * P:(j + 1) * P])
                return last

            pe.wait_ge(ident_ready, 2)
            pe.wait_ge(edges_ready, 1)
            turn_table(dst_f, 0)
            turn_table(src_f, NT).then_inc(dst_turned, 1)
            pe.wait_ge(rel_ready, 1)
            pe.wait_ge(dst_kept, 1)
            turn_table(dst_f, 0).then_inc(tables_turned, 1)

            pe.wait_ge(src_kept, 1)
            pe.wait_ge(ident_ready, 3)
            pe.wait_ge(base_ready, 1)

            def deg_zeros(start):
                return pe.matmul(ps[:, NT, 0:2 * (NHI + HWIN)], zeros_bf, zeros_bf[:, 0:1].to_broadcast([P, 2 * (NHI + HWIN)]),
                                 start=start, stop=not start)

            def pair_product(u, j, oh, at, start, stop):
                return pe.matmul(deg_sums[:, :, at], oh_lo[u][:, j, :, :].rearrange("p w j -> p (w j)"),
                                 oh[:, :, 2 * j:2 * j + 2].rearrange("p w j -> p j w"), start=start, stop=stop)

            deg_zeros(True)
            with pe.Fori(0, NBASE) as b:
                base = pe.value_load(base_i[0:1, bass.ds(b, 1)], min_val=0, max_val=NHI - 1)
                for k in range(DBASE):
                    pe.wait_ge(deg_onehot, b * DBASE + k + 1)
                    hold(pe)
                    for j in range(DCH // 2):
                        last = pair_product(k, j, oh_win[k], bass.ds(base, HWIN), False, False)
                    last.then_inc(deg_summed, 1)
                hold(pe)
            deg_zeros(False).then_inc(deg_summed, 1)

            pe.wait_ge(deg_flag, 1)
            uncounted = pe.value_load(deg_bad[0:1, 0:1], min_val=0, max_val=1)

            def deg_product(d, u, first=False, final=False):
                pe.wait_ge(deg_onehot, DSTEPS + d + 1)
                hold(pe)
                for j in range(DCH // 2):
                    last = pair_product(u, j, oh_hi[u], slice(0, NHI), first and j == 0, final and j == DCH // 2 - 1)
                last.then_inc(deg_summed, 1)

            with pe.If(uncounted == 1):
                for u in range(2):
                    deg_product(u, u, first=u == 0, final=False)
                if DSTEPS > 4:
                    with pe.Fori(1, DSTEPS // 2 - 1) as i:
                        for u in range(2):
                            deg_product(i * 2 + u, u)
                for u in range(2):
                    deg_product(DSTEPS - 2 + u, u, final=u == 1)
            pe.wait_ge(deg_kept, 1)
            for c in range(2):
                for j in range(2):
                    last = pe.matmul(ps[0:NHI // 2, NT + 1, c * LOW:(c + 1) * LOW],
                                     counted_in[:, j, :].rearrange("p (h c) -> p c h", c=2)[:, c, :],
                                     ident[:, :].rearrange("p (l j) -> p j l", j=2)[:, j, :], start=j == 0, stop=j == 1)
            last.then_inc(dg_turned, 1)

            pe.wait_ge(flag_ready, 1)
            pe.wait_ge(tables_ready, 1)
            bad = pe.value_load(bad_int[0:1, 0:1], min_val=0, max_val=1)

            def aggregate(run):
                done = run * GATHERS

                def product(u, ohu, j, s, width):
                    for k in range(KH):
                        for n in range(PARTS):
                            last = pe.matmul(ps[:, 2 * u + k, 0:width], slots[:, s, n * D + k * P:n * D + (k + 1) * P],
                                             onehot[:, ohu, j, 0:width], start=j == 0 and n == 0,
                                             stop=j == CPG - 1 and n == PARTS - 1)
                    return last

                def landed(s, use):
                    pe.wait_ge(got[s], 16 * (use + done // SLOTS + 1))

                def fast(i, q):
                    g, u = i * 4 + q, q % 2
                    pe.wait_ge(oh_fast[run], g + 1)
                    wait(pe, ev_fast[run], g - 1)
                    for j in range(CPG):
                        s = (q * CPG + j) % SLOTS
                        landed(s, i * 2 + (q * CPG + j) // SLOTS)
                        product(u, u, j, s, WIN).then_inc(chunks_used, 1)

                def general(i, u):
                    g = i * 2 + u

                    for j in range(CPG):
                        landed(u * CPG + j, i)
                    hold(pe)
                    with pe.Fori(0, NW) as k:
                        s = g * NW + k
                        pe.wait_ge(oh_gen[run], s + 1)
                        pe.wait_ge(ev_gen[run], s + 1)
                        for j in range(CPG):
                            last = product(0, 0, j, u * CPG + j, GWIN)
                        last.then_inc(mm_gen[run], 1)

                def lin_part(t, m, bank=4):
                    for k in range(KH):
                        last = pe.matmul(ps[:, bank + m, 0:CH], wconv[:, run, k, m * P:(m + 1) * P],
                                         acc[:, k, bass.ds(t * CH, CH)], start=k == 0, stop=k == KH - 1)
                    return last

                def lin_begin(t):
                    wait(pe, lin_scaled[run], t)
                    for m in range(KH - 1):
                        lin_part(t, m)

                def lin_finish(t):
                    lin_part(t, KH - 1).then_inc(lin_done[run], 1)

                def lin(t):
                    lin_begin(t)
                    lin_finish(t)

                def fours(i):
                    for q in range(4):
                        fast(i, q)

                def stride_end(g):
                    if not isinstance(g, int) or g >= 1:
                        pe.wait_ge(ev_fast[run], (g + 1) * STRIDE)
                        lin_begin(g - 1)

                def stride_middle(g):
                    if not isinstance(g, int) or g >= 2:
                        lin_finish(g - 2)

                with pe.If(bad == 0):
                    strides(pe, fours, stride_end, stride_middle)
                    lin_finish(STRIDES - 2)
                    for t in range(STRIDES - 1, NCH):
                        wait(pe, lin_scaled[run], t - 1)
                        for m in range(KH):
                            last = lin_part(t, m, last_banks(t))
                        last.then_inc(lin_done[run], 1)
                with pe.Else():
                    with pe.Fori(0, NG // 2) as i:
                        for u in range(2):
                            general(i, u)
                    pe.wait_ge(agg_done, run + 1)
                    lin(0)
                    with pe.Fori(1, NCH) as t:
                        lin(t)

            pe.wait_ge(dn_in, 32)
            turn(ps[0:RB, 7, 0:NBLK], dn[:, :]).then_inc(dn_turned, 1)

            def v_turn(t, q):
                pe.wait_ge(v_ready, t + 1)
                wait(pe, v_kept, t - 3)
                for b in range(BPC):
                    for k in range(KH):
                        last = turn(ps[:, 2 * q + k, b * RB:(b + 1) * RB], v_row[q][:, b, k * P:(k + 1) * P])
                last.then_inc(v_turned, 1)

            in_fours(pe, v_turn)

            pe.wait_ge(consts_in, 16 * NCONST)
            pe.wait_ge(v_kept, NCH)
            aggregate(L1)

            def y_turn(t, q):
                pe.wait_ge(y_ready, t + 1)
                wait(pe, lo_done[1], t - 3)
                for b in range(BPC):
                    for k in range(KH):
                        at = (b % 2) * D + k * P
                        last = turn(ps[0:RB, 2 * q + b // 2, at:at + P], ybuf[q % 2][:, k, b * RB:(b + 1) * RB])
                last.then_inc(y_turned, 1)

            in_fours(pe, y_turn)
            pe.wait_ge(lo_done[1], NCH)
            aggregate(L2)
            pe.wait_ge(router_in, 16 * NROUTER)
            pe.wait_ge(ones_made, 2)

            def turn_z(t, u):
                pe.wait_ge(zb_done, t + 1)
                wait(pe, z_added, t - 1)
                hold(pe)
                for b in range(BPC):
                    for k in range(KH):
                        at = (b % 2) * D + k * P
                        last = turn(ps[0:RB, 2 * u + b // 2, at:at + P], zb[u][:, k, b * RB:(b + 1) * RB])
                last.then_inc(z_turned, 1)

            def router(t, u, q):
                pe.wait_ge(xf_done[u], t // 2 + 1)
                wait(pe, xfT_done, t)
                hold(pe)
                for b in range(BPC):
                    for k in range(KH):
                        last = turn(ps[:, 4 + k, b * RB:(b + 1) * RB], xrow[q][:, u * BPC + b, k * P:(k + 1) * P])
                last.then_inc(x_turned, 1)

            def router_mm(t):
                pe.wait_ge(xfT_done, t + 1)
                wait(pe, rhT_done, t)
                hold(pe)
                for k in range(KH):
                    last = pe.matmul(ps[:, 6, 0:CH], rw1_sb[:, k, :], xfT[:, k, :], start=k == 0, stop=k == KH - 1)
                last.then_inc(rh_done, 1)

            def router_logits(t, u):
                pe.wait_ge(rhT_done, t + 1)
                wait(pe, pos_done, t // 2)
                hold(pe)
                for b in range(BPC):
                    at = (u * BPC + b) * 8
                    last = pe.matmul(ps[0:RB, 7, at:at + NX], rhT[:, b * RB:(b + 1) * RB], rw2_sb, start=True, stop=True)
                last.then_inc(lg_mm, 1)

            def rank(i):
                pe.wait_ge(mb_ready, i + 1)
                pe.wait_ge(lg_read, i + 1)
                wait(pe, run_ready, i)
                hold(pe)
                every = mb_bf.rearrange("p b e -> p (b e)")
                pe.matmul(ps[0:RB, 7, RANKS:RANKS + B2 * NX], tri_bf, every, start=True, stop=False)
                pe.matmul(ps[0:RB, 7, RANKS:RANKS + B2 * NX], ones_bf[:, 0:RB], run_bf.unsqueeze(1).to_broadcast([RB, B2, NX]),
                          start=False, stop=False)
                for b in range(B2 - 1):
                    n = B2 - 1 - b
                    last = pe.matmul(ps[0:RB, 7, RANKS + (b + 1) * NX:RANKS + B2 * NX], ones_bf[:, 0:RB],
                                     mb_bf[:, b:b + 1, :].to_broadcast([RB, n, NX]), start=False, stop=n == 1)
                last.then_inc(ranked, 1)

            def route(i, q, next1, next2):
                a, small = i * 2 + 2, not isinstance(i, int) or i >= 0
                if next1:
                    router(a, 0, (q + 1) % XBUFS)
                if next2:
                    turn_z(a + 2, 0)
                if small:
                    rank(i)
                if next1:
                    router_mm(a)
                    router(a + 1, 1, (q + 1) % XBUFS)
                if next2:
                    turn_z(a + 3, 1)
                if next1:
                    router_logits(a, 0)
                    router_mm(a + 1)
                    router_logits(a + 1, 1)

            turn_z(0, 0)
            turn_z(1, 1)
            routing(pe, route)
            pe.wait_ge(run_ready, PAIRS)
            pe.matmul(ps[:, 7, 0:NX], ones_bf, run_bf, start=True, stop=True).then_inc(counted, 1)

            pe.wait_ge(tiles_known, 1)

            def turn_tile(s, u):
                pe.wait_ge(rows_in[u], 16 * (half(s, u) + 1))
                wait(pe, xT_done, s)
                hold(pe)
                for b in range(TB):
                    for k in range(KH):
                        last = turn(ps[:, k, b * P:(b + 1) * P], tile_rows[u][:, b, k * P:(k + 1) * P])
                last.then_inc(tile_turned, 1)

            def hidden(layer, s, u):
                if layer == 0:
                    pe.wait_ge(xT_done, s + 1)
                    pe.wait_ge(expert_a, s + 1)
                    rhs, done, free, bank = xT, l1_done, (h1_act, h1_dve), 2
                else:
                    pe.wait_ge(h1_act, s + 1)
                    pe.wait_ge(h1_dve, s + 1)
                    rhs, done, free, bank = h1T, l2_done, (h2_act, h2_dve), 4
                for f in free:
                    wait(pe, f, s)
                hold(pe)
                for m in range(KH):
                    for k in range(KH):
                        last = pe.matmul(ps[:, bank + m, :], w_of(u, layer, k, m * P, (m + 1) * P), rhs[:, k, :],
                                         start=k == 0, stop=k == KH - 1)
                    last.then_inc(done, 1)

            def rows_out(s, u):
                pe.wait_ge(h2_act, s + 1)
                pe.wait_ge(h2_dve, s + 1)
                pe.wait_ge(expert_b, s + 1)
                wait(pe, y_biased, s)
                hold(pe)
                for b in range(TB):
                    for k in range(KH):
                        last = pe.matmul(ps[:, 6 + b // 2, (b % 2) * D:(b % 2 + 1) * D], h2T[:, k, b * P:(b + 1) * P],
                                         w_of(u, 2, k, 0, D), start=k == 0, stop=k == KH - 1)
                last.then_inc(l3_done, 1)

            def tile(s, u, next1, next2):
                hidden(1, s, u)
                if next1:
                    hidden(0, s + 1, 1 - u)
                rows_out(s, u)
                if next2:
                    turn_tile(s + 2, u)

            turn_tile(0, 0)
            hidden(0, 0, 0)
            turn_tile(1, 1)
            tiles(pe, tile)


_INS = ["x", "src", "dst", "L0_gnn_W1", "L0_gnn_b1", "L0_gnn_W2", "L0_gnn_b2", "L0_gnn_gamma1", "L0_gnn_beta1",
        "L0_gnn_gamma2", "L0_gnn_beta2", "L0_ffn_router_w1", "L0_ffn_router_b1", "L0_ffn_router_w2", "L0_ffn_router_b2",
        "L0_ffn_expert_w1", "L0_ffn_expert_b1", "L0_ffn_expert_w2", "L0_ffn_expert_b2", "L0_ffn_expert_w3", "L0_ffn_expert_b3"]


def kernel(**inputs):
    import numpy as _np
    import concourse.bacc as _bacc
    from concourse import mybir as _mybir
    from concourse.bass_utils import run_bass_kernel_spmd as _run

    nc = _bacc.Bacc("TRN2", target_bir_lowering=False, num_devices=1)
    n_nodes, n_edges = inputs["x"].shape[0], inputs["src"].shape[0]
    n_chunks, _, n_tables, _ = sizes(n_nodes, n_edges)
    pads = {"x": (n_chunks * CH, 0), "src": (n_tables * P * GE, 0), "dst": (n_tables * P * GE, -1)}
    arrays, args = {}, []
    for name in _INS:
        a = _np.ascontiguousarray(inputs[name])
        if name in pads:
            rows, fill = pads[name]
            padded = _np.full((rows,) + a.shape[1:], fill, a.dtype)
            padded[:a.shape[0]] = a
            a = padded
        arrays[f"in_{name}_dram"] = a
        args.append(nc.dram_tensor(f"in_{name}_dram", a.shape, _mybir.dt.from_np(a.dtype), kind="ExternalInput").ap())
    shape = (n_chunks * CH + P, inputs["x"].shape[1])
    args.append(nc.dram_tensor("out_0_dram", shape, _mybir.dt.float32, kind="ExternalOutput").ap())
    gnn_moe(nc, n_nodes, n_edges, *args)
    r = _run(nc, [arrays], core_ids=[0])
    return r.results[0]["out_0_dram"][:n_nodes]
```
